# Optimizing a Trainium2 kernel written in Bass

```python
import numpy as np
import jax
import jax.numpy as jnp

def _softmax(x, axis=-1):
    return jax.nn.softmax(x, axis=axis)

def _gelu(x):
    return jax.nn.gelu(x, approximate=True)

def _silu(x):
    return jax.nn.silu(x)

def _sigmoid(x):
    return jax.nn.sigmoid(x)

def _layernorm(x, axis=-1, eps=1e-05):
    m = jnp.mean(x, axis=axis, keepdims=True)
    v = jnp.var(x, axis=axis, keepdims=True)
    return (x - m) / jnp.sqrt(v + eps)

def _scatter_add(tgt, idx, src, axis=0):
    return tgt.at[idx].add(src)

def _segment_sum(src, seg, n):
    return jax.ops.segment_sum(src, seg, n)
kernel_name = 'mk_gps_d1_gnn_r8_82fce6'

def setup_inputs(seed: int=0):
    np.random.seed(seed)
    _w = jnp.asarray

    def _rec_inputs():
        import jax
        import jax.numpy as jnp
        _gk = jax.random.key(seed)
        x = -0.0003713 + 1 * jax.random.normal(jax.random.fold_in(_gk, 1), (6250, 256), jnp.float32)
        _s = jax.random.randint(jax.random.fold_in(_gk, 2), (50000,), 0, 6250, jnp.int32)
        _d = jax.random.randint(jax.random.fold_in(_gk, 3), (50000,), 0, 6250, jnp.int32)
        _loop = jnp.arange(6250, dtype=jnp.int32)
        src = jnp.concatenate([_s, _d, _loop])
        dst = jnp.concatenate([_d, _s, _loop])
        _o = jnp.argsort(dst, stable=True)
        src = src[_o]
        dst = dst[_o]
        edge_attr_16 = 0.000254156 + 0.999948 * jax.random.normal(jax.random.fold_in(_gk, 11), (106250, 16), jnp.float32)
        return (x, src, dst, edge_attr_16)
    x, src, dst, edge_attr_16 = _rec_inputs()

    def _L0_gnn_setup():
        import jax, jax.numpy as jnp
        import numpy as np
        N = 6250
        E = 100000
        F = 256
        H = 8
        C1 = 32
        C2 = 32
        ED = 16
        NEG_SLOPE = 0.2

        def gat_conv(x, src, dst, edge_attr, W, att_src, att_dst, W_e, att_e, bias, n_nodes):
            Hh, C = att_src.shape
            xp = (x @ W).reshape(-1, Hh, C)
            a_src = jnp.einsum('nhc,hc->nh', xp, att_src)
            a_dst = jnp.einsum('nhc,hc->nh', xp, att_dst)
            w_e = jnp.einsum('dhc,hc->dh', W_e.reshape(-1, Hh, C), att_e)
            a_edge = edge_attr @ w_e
            alpha = a_src[src] + a_dst[dst] + a_edge
            alpha = jax.nn.leaky_relu(alpha, NEG_SLOPE)
            m = jax.lax.stop_gradient(jax.ops.segment_max(alpha, dst, num_segments=n_nodes))
            ex = jnp.exp(alpha - m[dst])
            denom = jax.ops.segment_sum(ex, dst, num_segments=n_nodes)
            alpha = ex / (denom[dst] + 1e-16)
            msg = xp[src] * alpha[:, :, None]
            out = jax.ops.segment_sum(msg, dst, num_segments=n_nodes)
            return out.reshape(n_nodes, Hh * C) + bias
        key = jax.random.key(seed)
        ks = jax.random.split(key, 16)
        s = 0.05
        f32 = jnp.float32
        return {'x': jax.random.normal(ks[0], (N, F), f32), 'edge_index': jax.random.randint(ks[1], (2, E), 0, N, dtype=jnp.int32), 'edge_attr': jax.random.normal(ks[2], (E, ED), f32), 'W1': jax.random.normal(ks[3], (F, H * C1), f32) * s, 'att_src1': jax.random.normal(ks[4], (H, C1), f32) * s, 'att_dst1': jax.random.normal(ks[5], (H, C1), f32) * s, 'W_e1': jax.random.normal(ks[6], (ED, H * C1), f32) * s, 'att_e1': jax.random.normal(ks[7], (H, C1), f32) * s, 'b1': jnp.zeros((H * C1,), f32), 'W2': jax.random.normal(ks[8], (H * C1, H * C2), f32) * s, 'att_src2': jax.random.normal(ks[9], (H, C2), f32) * s, 'att_dst2': jax.random.normal(ks[10], (H, C2), f32) * s, 'W_e2': jax.random.normal(ks[11], (ED, H * C2), f32) * s, 'att_e2': jax.random.normal(ks[12], (H, C2), f32) * s, 'b2': jnp.zeros((H * C2,), f32)}
    _L0_gnn_all = _L0_gnn_setup()
    _L0_gnn_in = {k: v for k, v in _L0_gnn_all.items() if k in ('W1', 'att_src1', 'att_dst1', 'W_e1', 'att_e1', 'b1', 'W2', 'att_src2', 'att_dst2', 'W_e2', 'att_e2', 'b2')}
    del _L0_gnn_all

    def _L0_mix_setup():
        import math
        import jax, jax.numpy as jnp
        import numpy as np
        EPS_DIV = 1e-07
        EPS_NORM = 1e-12

        def _l2_normalize(x, axis):
            n = jnp.sqrt(jnp.sum(x * x, axis=axis, keepdims=True))
            return x / jnp.maximum(n, EPS_NORM)
        key = jax.random.key(seed)
        ks = jax.random.split(key, 5)
        b, N, C = (8, 512, 256)
        x = jax.random.normal(ks[0], (b, N, C), dtype=jnp.float32)
        W_qkv = jax.random.normal(ks[1], (C, 3 * C), dtype=jnp.float32) * (1.0 / math.sqrt(C))
        b_qkv = jax.random.normal(ks[2], (3 * C,), dtype=jnp.float32) * 0.02
        W_out = jax.random.normal(ks[3], (C, C), dtype=jnp.float32) * (1.0 / math.sqrt(C))
        b_out = jax.random.normal(ks[4], (C,), dtype=jnp.float32) * 0.02
        return {'x': x, 'W_qkv': W_qkv, 'b_qkv': b_qkv, 'W_out': W_out, 'b_out': b_out}
    _L0_mix_all = _L0_mix_setup()
    _L0_mix_in = {k: v for k, v in _L0_mix_all.items() if k in ('W_qkv', 'b_qkv', 'W_out', 'b_out')}
    del _L0_mix_all

    def _L0_ffn_setup():
        import jax, jax.numpy as jnp
        import numpy as np
        E, D, H, TOP_K = (6, 256, 256, 2)
        ROUTER_H = D // 2
        key = jax.random.key(seed)
        ks = jax.random.split(key, 12)
        s = 1.0 / np.sqrt(D)
        sh = 1.0 / np.sqrt(H)
        sr = 1.0 / np.sqrt(ROUTER_H)
        return {'features': jax.random.normal(ks[0], (8, 512, D), dtype=jnp.float32), 'router_w1': jax.random.uniform(ks[1], (D, ROUTER_H), jnp.float32, -s, s), 'router_b1': jnp.zeros((ROUTER_H,), jnp.float32), 'router_w2': jax.random.uniform(ks[2], (ROUTER_H, E), jnp.float32, -sr, sr), 'router_b2': jnp.zeros((E,), jnp.float32), 'expert_w1': jax.random.uniform(ks[3], (E, D, H), jnp.float32, -s, s), 'expert_b1': jnp.zeros((E, H), jnp.float32), 'expert_w2': jax.random.uniform(ks[4], (E, H, H), jnp.float32, -sh, sh), 'expert_b2': jnp.zeros((E, H), jnp.float32), 'expert_w3': jax.random.uniform(ks[5], (E, H, D), jnp.float32, -sh, sh), 'expert_b3': jnp.zeros((E, D), jnp.float32)}
    _L0_ffn_all = _L0_ffn_setup()
    _L0_ffn_in = {k: v for k, v in _L0_ffn_all.items() if k in ('router_w1', 'router_b1', 'router_w2', 'router_b2', 'expert_w1', 'expert_b1', 'expert_w2', 'expert_b2', 'expert_w3', 'expert_b3')}
    del _L0_ffn_all
    return {'x': x, 'src': src, 'dst': dst, 'edge_attr_16': edge_attr_16, 'L0_gnn_W1': _L0_gnn_in['W1'], 'L0_gnn_att_src1': _L0_gnn_in['att_src1'], 'L0_gnn_att_dst1': _L0_gnn_in['att_dst1'], 'L0_gnn_W_e1': _L0_gnn_in['W_e1'], 'L0_gnn_att_e1': _L0_gnn_in['att_e1'], 'L0_gnn_b1': _L0_gnn_in['b1'], 'L0_gnn_W2': _L0_gnn_in['W2'], 'L0_gnn_att_src2': _L0_gnn_in['att_src2'], 'L0_gnn_att_dst2': _L0_gnn_in['att_dst2'], 'L0_gnn_W_e2': _L0_gnn_in['W_e2'], 'L0_gnn_att_e2': _L0_gnn_in['att_e2'], 'L0_gnn_b2': _L0_gnn_in['b2'], 'L0_mix_W_qkv': _L0_mix_in['W_qkv'], 'L0_mix_b_qkv': _L0_mix_in['b_qkv'], 'L0_mix_W_out': _L0_mix_in['W_out'], 'L0_mix_b_out': _L0_mix_in['b_out'], 'L0_ffn_router_w1': _L0_ffn_in['router_w1'], 'L0_ffn_router_b1': _L0_ffn_in['router_b1'], 'L0_ffn_router_w2': _L0_ffn_in['router_w2'], 'L0_ffn_router_b2': _L0_ffn_in['router_b2'], 'L0_ffn_expert_w1': _L0_ffn_in['expert_w1'], 'L0_ffn_expert_b1': _L0_ffn_in['expert_b1'], 'L0_ffn_expert_w2': _L0_ffn_in['expert_w2'], 'L0_ffn_expert_b2': _L0_ffn_in['expert_b2'], 'L0_ffn_expert_w3': _L0_ffn_in['expert_w3'], 'L0_ffn_expert_b3': _L0_ffn_in['expert_b3']}

def reference(x, src, dst, edge_attr_16, L0_gnn_W1, L0_gnn_att_src1, L0_gnn_att_dst1, L0_gnn_W_e1, L0_gnn_att_e1, L0_gnn_b1, L0_gnn_W2, L0_gnn_att_src2, L0_gnn_att_dst2, L0_gnn_W_e2, L0_gnn_att_e2, L0_gnn_b2, L0_mix_W_qkv, L0_mix_b_qkv, L0_mix_W_out, L0_mix_b_out, L0_ffn_router_w1, L0_ffn_router_b1, L0_ffn_router_w2, L0_ffn_router_b2, L0_ffn_expert_w1, L0_ffn_expert_b1, L0_ffn_expert_w2, L0_ffn_expert_b2, L0_ffn_expert_w3, L0_ffn_expert_b3):
    import jax
    import jax.numpy as jnp

    def _L0_gnn_ref(x, edge_index, edge_attr, W1, att_src1, att_dst1, W_e1, att_e1, b1, W2, att_src2, att_dst2, W_e2, att_e2, b2):
        import jax, jax.numpy as jnp
        import numpy as np
        N = 6250
        E = 100000
        F = 256
        H = 8
        C1 = 32
        C2 = 32
        ED = 16
        NEG_SLOPE = 0.2

        def gat_conv(x, src, dst, edge_attr, W, att_src, att_dst, W_e, att_e, bias, n_nodes):
            Hh, C = att_src.shape
            xp = (x @ W).reshape(-1, Hh, C)
            a_src = jnp.einsum('nhc,hc->nh', xp, att_src)
            a_dst = jnp.einsum('nhc,hc->nh', xp, att_dst)
            w_e = jnp.einsum('dhc,hc->dh', W_e.reshape(-1, Hh, C), att_e)
            a_edge = edge_attr @ w_e
            alpha = a_src[src] + a_dst[dst] + a_edge
            alpha = jax.nn.leaky_relu(alpha, NEG_SLOPE)
            m = jax.lax.stop_gradient(jax.ops.segment_max(alpha, dst, num_segments=n_nodes))
            ex = jnp.exp(alpha - m[dst])
            denom = jax.ops.segment_sum(ex, dst, num_segments=n_nodes)
            alpha = ex / (denom[dst] + 1e-16)
            msg = xp[src] * alpha[:, :, None]
            out = jax.ops.segment_sum(msg, dst, num_segments=n_nodes)
            return out.reshape(n_nodes, Hh * C) + bias
        src, dst = (edge_index[0], edge_index[1])
        h = jax.nn.relu(x)
        h = gat_conv(h, src, dst, edge_attr, W1, att_src1, att_dst1, W_e1, att_e1, b1, N)
        h = jax.nn.relu(h)
        h = gat_conv(h, src, dst, edge_attr, W2, att_src2, att_dst2, W_e2, att_e2, b2, N)
        return h + x

    def _L0_mix_ref(x, W_qkv, b_qkv, W_out, b_out):
        import math
        import jax, jax.numpy as jnp
        import numpy as np
        EPS_DIV = 1e-07
        EPS_NORM = 1e-12

        def _l2_normalize(x, axis):
            n = jnp.sqrt(jnp.sum(x * x, axis=axis, keepdims=True))
            return x / jnp.maximum(n, EPS_NORM)
        b, N, C = x.shape
        qkv = x @ W_qkv + b_qkv
        q, k, v = jnp.split(qkv, 3, axis=2)
        q = q - jnp.mean(q, axis=2, keepdims=True)
        k = k - jnp.mean(k, axis=2, keepdims=True)
        q2 = q * q
        k2 = k * k
        q2s = jnp.sum(q2, axis=2, keepdims=True)
        k2s = jnp.sum(k2, axis=2, keepdims=True)
        k2 = _l2_normalize(k2 / (k2s + EPS_DIV), axis=-2)
        q2 = _l2_normalize(q2 / (q2s + EPS_DIV), axis=-1)
        kv = jnp.einsum('bnc,bnd->bcd', k2, v)
        t2 = jnp.einsum('bnc,bcd->bnd', q2, kv) / math.sqrt(N)
        attn = v + t2
        return attn @ W_out + b_out

    def _L0_ffn_ref(features, router_w1, router_b1, router_w2, router_b2, expert_w1, expert_b1, expert_w2, expert_b2, expert_w3, expert_b3):
        import jax, jax.numpy as jnp
        import numpy as np
        E, D, H, TOP_K = (6, 256, 256, 2)
        ROUTER_H = D // 2
        rh = jax.nn.relu(features @ router_w1 + router_b1)
        expert_logits = jax.nn.softmax(rh @ router_w2 + router_b2, axis=-1)
        top_w, top_i = jax.lax.top_k(expert_logits, TOP_K)
        routing_weights = jax.nn.softmax(top_w, axis=-1)
        h1 = jax.nn.relu(jnp.einsum('bsd,edh->bseh', features, expert_w1) + expert_b1)
        h2 = jax.nn.relu(jnp.einsum('bseh,ehf->bsef', h1, expert_w2) + expert_b2)
        expert_out = jnp.einsum('bsef,efo->bseo', h2, expert_w3) + expert_b3
        sel = jnp.take_along_axis(expert_out, top_i[:, :, :, None], axis=2)
        combined = jnp.sum(sel * routing_weights[..., None], axis=2)
        return combined
    edge_index = jnp.stack([src, dst])
    xn = _layernorm(x, axis=-1)
    x = x + _L0_gnn_ref(xn, edge_index, edge_attr_16, L0_gnn_W1, L0_gnn_att_src1, L0_gnn_att_dst1, L0_gnn_W_e1, L0_gnn_att_e1, L0_gnn_b1, L0_gnn_W2, L0_gnn_att_src2, L0_gnn_att_dst2, L0_gnn_W_e2, L0_gnn_att_e2, L0_gnn_b2) + _L0_mix_ref(xn[None], L0_mix_W_qkv, L0_mix_b_qkv, L0_mix_W_out, L0_mix_b_out)[0]
    x = x + _L0_ffn_ref(_layernorm(x, axis=-1)[None], L0_ffn_router_w1, L0_ffn_router_b1, L0_ffn_router_w2, L0_ffn_router_b2, L0_ffn_expert_w1, L0_ffn_expert_b1, L0_ffn_expert_w2, L0_ffn_expert_b2, L0_ffn_expert_w3, L0_ffn_expert_b3)[0]
    return x

_drawn_inputs = setup_inputs


def setup_inputs(seed=0):
    import zlib

    import numpy as np

    out = dict(_drawn_inputs(seed))
    spreads = {'L0_gnn_b1': (0.0, 0.353),
     'L0_gnn_b2': (0.0, 0.1),
     'L0_ffn_router_b1': (0.0, 0.475),
     'L0_ffn_router_b2': (0.0, 0.308),
     'L0_ffn_expert_b1': (0.0, 0.8),
     'L0_ffn_expert_b2': (0.0, 0.643),
     'L0_ffn_expert_b3': (0.0, 0.1)}
    factors = {'edge_attr_16': 8.0,
     'L0_gnn_att_src1': 29.278,
     'L0_gnn_att_dst1': 64.0,
     'L0_gnn_W_e1': 8.0,
     'L0_gnn_att_e1': 8.0,
     'L0_gnn_att_src2': 51.233,
     'L0_gnn_att_dst2': 64.0,
     'L0_gnn_W_e2': 8.0,
     'L0_gnn_att_e2': 8.0,
     'L0_mix_b_out': 6.002}
    for name, (base, spread) in spreads.items():
        noise = np.random.default_rng([zlib.crc32(name.encode()), seed]).standard_normal(out[name].shape)
        drawn = base * np.exp(spread * noise) if base else spread * noise
        out[name] = jnp.asarray(drawn.astype(out[name].dtype))
    for name, factor in factors.items():
        out[name] = (out[name] * factor).astype(out[name].dtype)
    return out
```

```python
from contextlib import ExitStack

import numpy as np

import concourse.bass as bass
from concourse import mybir

F32 = mybir.dt.float32
BF16 = mybir.dt.bfloat16
I32 = mybir.dt.int32
U32 = mybir.dt.uint32
ALU = mybir.AluOpType
ACT = mybir.ActivationFunctionType
AX = mybir.AxisListType

P = 128
N = 6250
E = 106250
F = 256
H = 8
C = F // H
D_EDGE = 16
NEXP = 6
NB = 50
NP = NB * P
GT = P // H
NG = -(-E // (P * GT))
T = NG * GT
EP = T * P
ROW = F + H
WIN = P + 1
BIG = 1e38
LN_EPS = 1e-5
EPS_DIV = 1e-7
EPS_NORM = 1e-12
NCH = NB // 2


def ln_stats(nc, vec, x, stats, mv):
    nc.vector.bn_stats(stats, x)
    vec.drain()
    nc.vector.bn_aggr(mv, stats)


def build(nc, x, src_t, dst_t, dst_g, first_row, last_row, edge_b, W1, as1, ad1, We1, ae1, b1, W2, as2, ad2, We2,
          ae2, b2, Wqkv, bqkv, Wout, bout, rw1, rb1, rw2, rb2, ew1, eb1, ew2, eb2, ew3, eb3, out):
    with ExitStack() as top:
        def sb(name, shape, dt=F32, ctx=top):
            return ctx.enter_context(nc.sbuf_tensor(name, shape, dt))

        def pb(name, shape, ctx):
            return ctx.enter_context(nc.psum_tensor(name, shape, F32))

        def sem(name, ctx):
            return ctx.enter_context(nc.semaphore(name))

        table = [nc.dram_tensor(f"table{l}", (NP, ROW), F32).ap() for l in range(2)]
        score_dst = [nc.dram_tensor(f"score_dst{l}", (H, NP), F32).ap() for l in range(2)]

        ident = sb("ident", [P, P])
        acc = sb("acc", [P, 2, NP])
        sep = sb("sep", [P, NG, P + 1], BF16)
        same = sb("same", [P, NG, P + 1], BF16)
        ends = sb("ends", [P, NG, 2, 3])
        parts = sb("parts", [P, T, 2, 2])
        src_sb = sb("src_sb", [P, T], I32)
        rel = sb("rel", [P, T])
        islast = sb("islast", [P, T])
        first_sb = sb("first_sb", [1, T], I32)
        row_iota = sb("row_iota", [P, P])
        kmask = sb("kmask", [P, GT])
        hsel = sb("hsel", [P, 2, P])
        wext = sb("wext", [P, 2, 2, ROW])
        wdst = sb("wdst", [P, 2, 2, H])
        wedge = sb("wedge", [P, 2, H, H])
        gbias = sb("gbias", [P, 2, 2])
        wq = sb("wq", [P, 2, F])
        bq = sb("bq", [P, F])
        vw = sb("vw", [P, 2, F])
        bvw = sb("bvw", [P, F])
        kvw = sb("kvw", [P, 2, F])
        cst = sb("cst", [P, 4])

        prepare(nc, sb, pb, sem, locals())
        blocks(nc, sb, pb, sem, locals())
        for layer in range(2):
            edges(nc, sb, pb, sem, locals())
            join(nc, sb, pb, sem, locals())
            if layer == 0:
                second_table(nc, sb, pb, sem, locals())
        last(nc, sb, pb, sem, locals())


def prepare(nc, sb, pb, sem, v):
    ident, sep, same, ends = v["ident"], v["sep"], v["same"], v["ends"]
    src_sb, rel, islast, first_sb = v["src_sb"], v["rel"], v["islast"], v["first_sb"]
    row_iota, kmask, hsel = v["row_iota"], v["kmask"], v["hsel"]
    wext, wdst, wedge, gbias = v["wext"], v["wdst"], v["wedge"], v["gbias"]
    wq, bq, vw, bvw, cst = v["wq"], v["bq"], v["vw"], v["bvw"], v["cst"]
    with ExitStack() as ctx:
        def tmp(name, shape, dt=F32):
            return sb(name, shape, dt, ctx)

        dst_sb = tmp("dst_sb", [P, T], I32)
        first_b = tmp("first_b", [P, T], I32)
        last_b = tmp("last_b", [P, T], I32)
        dg = tmp("dg", [P, NG, P], I32)
        pcol = tmp("pcol", [P, 1], I32)
        bits = tmp("bits", [P, 3], I32)
        bitsf = tmp("bitsf", [P, 4])
        irow = tmp("irow", [P, P], I32)
        ihead = tmp("ihead", [P, 2, P], I32)
        headf = tmp("headf", [P, 2, P])
        att = tmp("att", [P, 6, F])
        we = tmp("we", [P, 2, F])
        prod = tmp("prod", [P, 2, F])
        we_h = tmp("we_h", [P, 2, H])
        bmask = tmp("bmask", [P, H])
        means = tmp("means", [P, 4])
        wv = tmp("wv", [P, 2, F])
        wvT = tmp("wvT", [P, 2, F])
        wo = tmp("wo", [P, 2, F])
        bv = tmp("bv", [P, 2])
        bvb = tmp("bvb", [P, 2, P])
        ones = tmp("ones", [P, P])
        bo = tmp("bo", [P, F])
        tp = pb("prep_t", [P, 512], ctx)
        mm0 = pb("prep_m0", [P, 512], ctx)
        mm1 = pb("prep_m1", [P, 512], ctx)
        s_in = sem("prep_in", ctx)
        s_iota = sem("prep_iota", ctx)
        s_bits = sem("prep_bits", ctx)
        s_ready = sem("prep_ready", ctx)
        s_t = sem("prep_transposed", ctx)
        s_tc = sem("prep_copied", ctx)
        s_mm = sem("prep_product", ctx)
        block = ctx.enter_context(nc.Block())
        loads = []

        def load(to, of):
            loads.append((to, of))

        load(dst_sb[:], v["dst_t"])
        load(src_sb[:], v["src_t"])
        load(first_b[:], v["first_row"].broadcast_to((P, T)))
        load(last_b[:], v["last_row"].broadcast_to((P, T)))
        load(first_sb[:], v["first_row"])
        for k in range(GT):
            load(dg[H * k:H * k + H], v["dst_g"][:, k, :].unsqueeze(0).broadcast_to((H, NG, P)))
        for l in range(2):
            W, a_s, a_d, W_e, a_e = ((v[f"{n}{l + 1}"]) for n in ("W", "as", "ad", "We", "ae"))
            load(wext[:, :, l, 0:F], W.rearrange("(a p) f -> p a f", p=P))
            for j, a in enumerate((a_s, a_d, a_e)):
                load(att[:, 3 * l + j, :], a.rearrange("(a h) c -> a (h c)", a=1).broadcast_to((P, F)))
            for b in range(H):
                load(we[D_EDGE * b:D_EDGE * b + D_EDGE, l, :], W_e)
            for a in range(2):
                load(gbias[:, l, a:a + 1], v[f"b{l + 1}"].rearrange("(a p b) -> a p b", p=P, b=1)[a])
        Wqkv, bqkv = v["Wqkv"], v["bqkv"].rearrange("(a f) -> a f", a=1)
        load(wq[:], Wqkv[:, 0:F].rearrange("(a p) f -> p a f", p=P))
        load(bq[:], bqkv[:, 0:F].broadcast_to((P, F)))
        load(wv[:], Wqkv[:, 2 * F:3 * F].rearrange("(a p) f -> p a f", p=P))
        load(wo[:], v["Wout"].rearrange("(a p) f -> p a f", p=P))
        load(bo[:], v["bout"].rearrange("(a f) -> a f", a=1).broadcast_to((P, F)))
        for a in range(2):
            load(bv[:, a:a + 1], v["bqkv"].rearrange("(a p b) -> a p b", p=P, b=1)[4 + a])

        @block.sync
        def _(sp):
            for to, of in loads:
                sp.dma_start(to, of).then_inc(s_in, 16)

        @block.gpsimd
        def _(pool):
            nc.gpsimd.iota(pcol[:], pattern=[[0, 1]], base=0, channel_multiplier=1).then_inc(s_iota, 1)
            nc.gpsimd.iota(irow[:], pattern=[[1, P]], base=0, channel_multiplier=0).then_inc(s_iota, 1)
            nc.gpsimd.iota(ihead[:].rearrange("p a (h c) -> p a h c", c=C), pattern=[[4, 2], [1, 4], [0, C]],
                           base=0, channel_multiplier=0).then_inc(s_iota, 1)
            nc.gpsimd.memset(cst[:, 0:1], -0.5)
            nc.gpsimd.memset(cst[:, 1:2], 0.5)
            nc.gpsimd.memset(cst[:, 2:4], 0.0)
            nc.gpsimd.memset(ones[:], 1.0).then_inc(s_iota, 1)

        @block.vector
        def _(vec):
            vec.wait_ge(s_iota, 4)
            nc.vector.tensor_single_scalar(bits[:, 0:1], pcol[:], 3, ALU.logical_shift_right)
            nc.vector.tensor_single_scalar(bits[:, 1:2], pcol[:], 7, ALU.bitwise_and)
            nc.vector.tensor_single_scalar(bits[:, 2:3], pcol[:], 4, ALU.logical_shift_right)
            nc.vector.tensor_copy(bitsf[:, 3:4], pcol[:])
            nc.vector.tensor_copy(row_iota[:], irow[:])
            nc.vector.tensor_copy(headf[:], ihead[:])
            vec.drain()
            nc.vector.tensor_copy(bitsf[:, 0:3], bits[:])
            vec.drain()
            nc.vector.tensor_scalar(ident[:], row_iota[:], bitsf[:, 3:4], None, ALU.is_equal)
            nc.vector.tensor_scalar(kmask[:], row_iota[:, 0:GT], bitsf[:, 0:1], None, ALU.is_equal)
            nc.vector.tensor_scalar(bmask[:], row_iota[:, 0:H], bitsf[:, 2:3], None, ALU.is_equal)
            nc.vector.tensor_scalar(hsel[:], headf[:], bitsf[:, 1:2], None, ALU.is_equal)
            vec.wait_ge(s_in, 16 * len(loads))
            nc.vector.tensor_tensor(rel[:], dst_sb[:], first_b[:], ALU.subtract)
            nc.vector.tensor_tensor(islast[:], dst_sb[:], last_b[:], ALU.is_equal)
            nc.vector.memset(same[:], 0.0)
            nc.vector.memset(v["acc"][:, :, N:NP], 0.0)
            nc.vector.tensor_copy(ends[:, :, 0, 2:3], dg[:, :, 0:1])
            nc.vector.tensor_copy(ends[:, :, 1, 2:3], dg[:, :, P - 1:P])
            vec.drain()
            nc.vector.tensor_tensor(same[:, :, 1:P], dg[:, :, 1:P], dg[:, :, 0:P - 1], ALU.is_equal)
            vec.drain()
            nc.vector.tensor_scalar(sep[:], same[:], BIG, -BIG, ALU.mult, ALU.add)
            for l in range(2):
                for j, to in ((0, wext[:, :, l, F:ROW]), (1, wdst[:, :, l, :])):
                    nc.vector.tensor_tensor(prod[:], wext[:, :, l, 0:F],
                                            att[:, 3 * l + j, :].unsqueeze(1).broadcast_to((P, 2, F)), ALU.mult)
                    vec.drain()
                    nc.vector.tensor_reduce(to, prod[:].rearrange("p a (h c) -> p a h c", c=C), AX.X, ALU.add)
                    vec.drain()
                nc.vector.tensor_tensor(prod[:, 0, :], we[:, l, :], att[:, 3 * l + 2, :], ALU.mult)
                vec.drain()
                nc.vector.tensor_reduce(we_h[:, l, :], prod[:, 0, :].rearrange("p (h c) -> p h c", c=C), AX.X, ALU.add)
                vec.drain()
                nc.vector.tensor_tensor(wedge[:, l], we_h[:, l, :].unsqueeze(1).broadcast_to((P, H, H)),
                                        bmask[:].unsqueeze(2).broadcast_to((P, H, H)), ALU.mult)
            nc.vector.tensor_reduce(means[:, 0:2], wq[:], AX.X, ALU.add)
            nc.vector.tensor_reduce(means[:, 2:3], bq[:], AX.X, ALU.add)
            vec.drain()
            nc.vector.tensor_single_scalar(means[:, 0:3], means[:, 0:3], 1.0 / F, ALU.mult)
            vec.drain()
            for a in range(2):
                nc.vector.tensor_scalar(wq[:, a, :], wq[:, a, :], means[:, a:a + 1], None, ALU.subtract)
            nc.vector.tensor_scalar(bq[:], bq[:], means[:, 2:3], None, ALU.subtract)
            for a in range(2):
                nc.vector.tensor_scalar(bvb[:, a, :], ones[:], bv[:, a:a + 1], None, ALU.mult)
            nc.vector.memset(means[:, 3:4], 0.0).then_inc(s_ready, 1)
            vec.wait_ge(s_t, 1)
            nc.vector.tensor_copy(wvT[:], tp[:].rearrange("p (b f) -> p b f", b=2)).then_inc(s_tc, 1)
            vec.wait_ge(s_mm, 1)
            nc.vector.tensor_copy(vw[:], mm0[:].rearrange("p (b f) -> p b f", b=2))
            nc.vector.tensor_tensor(bvw[:], mm1[:, 0:F], bo[:], ALU.add)

        @block.tensor
        def _(pe):
            pe.wait_ge(s_ready, 1)
            for b in range(2):
                for a in range(2):
                    last = nc.tensor.transpose(tp[:, b * F + a * P:b * F + a * P + P], wv[:, a, b * P:b * P + P], ident[:])
            last.then_inc(s_t, 1)
            pe.wait_ge(s_tc, 1)
            for a in range(2):
                for b in range(2):
                    nc.tensor.matmul(mm0[:, a * F:a * F + F], wvT[:, b, a * P:a * P + P], wo[:, b, :],
                                     start=(b == 0), stop=(b == 1))
            for b in range(2):
                last = nc.tensor.matmul(mm1[:, 0:F], bvb[:, b, :], wo[:, b, :], start=(b == 0), stop=(b == 1))
            last.then_inc(s_mm, 1)


def blocks(nc, sb, pb, sem, v):
    ident, acc, wext, wdst, cst = v["ident"], v["acc"], v["wext"], v["wdst"], v["cst"]
    vw, kvw, x = v["vw"], v["kvw"], v["x"]
    table, score_dst = v["table"][0], v["score_dst"][0]
    with ExitStack() as ctx:
        def tmp(name, shape, dt=F32):
            return sb(name, shape, dt, ctx)

        wk = tmp("wk", [P, 2, F])
        bk = tmp("bk", [P, F])
        kmean = tmp("kmean", [P, 3])
        wvo = tmp("wvo", [P, 2, F])
        bvwk = tmp("bvwk", [1, F])
        bv2 = tmp("bv2", [P, 2])
        xb = tmp("xb", [P, 2, F])
        xn = tmp("xn", [P, 2, F + 1])
        stats = tmp("stats", [P, 2, 6])
        mv = tmp("mv", [P, 2, 2])
        rstd = tmp("rstd", [P, 2])
        epsb = tmp("epsb", [P, 2])
        xnT = tmp("xnT", [P, 2, 2, P])
        hT = tmp("hT", [P, 2, 2, P])
        row = tmp("row", [P, 2, ROW])
        sd = tmp("sd", [H, NP])
        kc = tmp("kc", [P, 2, F])
        k2 = tmp("k2", [P, 2, F])
        k2r = tmp("k2r", [P, 2, F])
        k4 = tmp("k4", [P, 2, F])
        k2s = tmp("k2s", [P, 2])
        inv = tmp("inv", [P, 2])
        nmask = tmp("nmask", [P, NB])
        inode = tmp("inode", [P, NB], I32)
        ones = tmp("ones_b", [P, 1])
        norm = tmp("norm", [P, 2])
        kxs = tmp("kxs", [P, 2, F + 1])
        kxT = tmp("kxT", [P, 2, F])
        ksT = tmp("ksT", [1, F])
        turn = [pb(f"turn{s}", [P, 512], ctx) for s in range(2)]
        ps_row = pb("ps_row", [P, 512], ctx)
        ps_sd = pb("ps_sd", [P, 512], ctx)
        ps_k = pb("ps_k", [P, 512], ctx)
        ps_kx = [pb(f"ps_kx{a}", [P, 512], ctx) for a in range(2)]
        ps_end = pb("ps_end", [P, 512], ctx)
        names = ("w_in", "x0", "x1", "xfree", "mv", "rstd", "xn", "turned", "copied", "row", "rowc", "sd", "sdc", "k", "kc",
                 "k2", "k2r", "kx", "out0", "out1", "setup", "fin", "fins", "finp", "sdout", "mask")
        s = {n: sem("blk_" + n, ctx) for n in names}
        block = ctx.enter_context(nc.Block())

        @block.sync
        def _(sp):
            sp.dma_start(wk[:], v["Wqkv"][:, F:2 * F].rearrange("(a p) f -> p a f", p=P)).then_inc(s["w_in"], 16)
            sp.dma_start(bk[:], v["bqkv"].rearrange("(a f) -> a f", a=1)[:, F:2 * F].broadcast_to((P, F))).then_inc(s["w_in"], 16)
            for a in range(2):
                sp.dma_start(bv2[:, a:a + 1], v["bqkv"].rearrange("(a p b) -> a p b", p=P, b=1)[4 + a]).then_inc(s["w_in"], 16)
            sp.dma_start(wvo[:], v["Wout"].rearrange("(a p) f -> p a f", p=P)).then_inc(s["w_in"], 16)
            with sp.Fori(0, NB // 2) as i:
                for q in range(2):
                    sp.wait_ge(s["xn"], 2 * i + q + 1)
                    sp.dma_start(xb[:, q, :], x[bass.ds((2 * i + q) * P, P), :]).then_inc(s[f"x{q}"], 16)
            sp.wait_ge(s["sdc"], NB + 1)
            sp.dma_start(score_dst, sd[:]).then_inc(s["sdout"], 16)
            sp.wait_ge(s["sdout"], 16)

        @block.gpsimd
        def _(pool):
            nc.gpsimd.iota(inode[:], pattern=[[P, NB]], base=0, channel_multiplier=1).then_inc(s["mask"], 1)
            with pool.Fori(0, NB // 2) as i:
                for q in range(2):
                    pool.wait_ge(s["mv"], 2 * i + q + 1)
                    nc.gpsimd.tensor_tensor(rstd[:, q:q + 1], epsb[:, q:q + 1], cst[:, 0:1], ALU.pow).then_inc(s["rstd"], 1)
            pool.wait_ge(s["fin"], 1)
            nc.gpsimd.tensor_tensor(inv[:], norm[:], cst[:, 1:2].broadcast_to((P, 2)), ALU.pow).then_inc(s["finp"], 1)

        def normalise(vec, n, q):
            vec.wait_ge(s[f"x{q}"], 16 * (n // 2 + 1) if isinstance(n, int) else 16 * (n[0] + 1))
            at = n if isinstance(n, int) else 2 * n[0] + n[1]
            nc.vector.bn_stats(stats[:, q, :], xb[:, q, :])
            vec.drain()
            nc.vector.bn_aggr(mv[:, q, :], stats[:, q, :])
            vec.drain()
            nc.vector.tensor_single_scalar(epsb[:, q:q + 1], mv[:, q, 1:2], LN_EPS, ALU.add).then_inc(s["mv"], 1)
            vec.wait_ge(s["rstd"], at + 1)
            vec.wait_ge(s["kx"], at + 1)
            nc.vector.tensor_scalar(xn[:, q, 0:F], xb[:, q, :], mv[:, q, 0:1], rstd[:, q:q + 1], ALU.subtract,
                                    ALU.mult).then_inc(s["xn"], 1)

        @block.vector
        def _(vec):
            vec.sem_inc(s["xn"], 2)
            nc.vector.memset(ones[:], 1.0)
            nc.vector.memset(xn[:, :, F:F + 1], 1.0)
            vec.wait_ge(s["mask"], 1)
            nc.vector.tensor_single_scalar(nmask[:], inode[:], N, ALU.is_lt)
            vec.wait_ge(s["w_in"], 80)
            nc.vector.tensor_reduce(kmean[:, 0:2], wk[:], AX.X, ALU.add)
            nc.vector.tensor_reduce(kmean[:, 2:3], bk[:], AX.X, ALU.add)
            vec.drain()
            nc.vector.tensor_single_scalar(kmean[:], kmean[:], 1.0 / F, ALU.mult)
            vec.drain()
            for a in range(2):
                nc.vector.tensor_scalar(wk[:, a, :], wk[:, a, :], kmean[:, a:a + 1], None, ALU.subtract)
            nc.vector.tensor_scalar(bk[:], bk[:], kmean[:, 2:3], None, ALU.subtract).then_inc(s["setup"], 1)
            vec.wait_ge(s["setup"], 1)

            def keys(at, q):
                vec.wait_ge(s["k"], at + 3)
                vec.wait_ge(s["k2"], at + 1)
                nc.vector.tensor_tensor(kc[:, q, :], ps_k[:, 0:F], bk[:], ALU.add).then_inc(s["kc"], 1)
                vec.wait_ge(s["k2"], at + 2)
                nc.vector.tensor_single_scalar(inv[:, q:q + 1], k2s[:, q:q + 1], EPS_DIV, ALU.add)
                vec.drain()
                nc.vector.reciprocal(inv[:, q:q + 1], inv[:, q:q + 1])
                vec.drain()
                nc.vector.tensor_tensor(inv[:, q:q + 1], inv[:, q:q + 1], nmask[:, bass.ds(at, 1)], ALU.mult)
                vec.drain()
                vec.wait_ge(s["kx"], at + 1)
                nc.vector.tensor_scalar(k2r[:, q, :], k2[:, q, :], inv[:, q:q + 1], None, ALU.mult)
                vec.drain()
                nc.vector.tensor_tensor(k4[:, q, :], k2r[:, q, :], k2r[:, q, :], ALU.mult).then_inc(s["k2r"], 1)

            normalise(vec, 0, 0)
            with vec.Fori(0, NB // 2 - 1) as i:
                normalise(vec, (i, 1), 1)
                keys(2 * i, 0)
                normalise(vec, (i + 1, 0), 0)
                keys(2 * i + 1, 1)
            normalise(vec, NB - 1, 1)
            keys(NB - 2, 0)
            keys(NB - 1, 1)
            vec.wait_ge(s["kx"], NB + 2)
            for a in range(2):
                nc.vector.tensor_copy(norm[:, a:a + 1], ps_kx[a][:, F + 1:F + 2])
            vec.drain()
            nc.vector.sem_inc(s["fin"], 1)
            vec.wait_ge(s["finp"], 1)
            nc.vector.tensor_single_scalar(inv[:], inv[:], EPS_NORM, ALU.max)
            vec.drain()
            nc.vector.reciprocal(inv[:], inv[:])
            vec.drain()
            nc.vector.tensor_single_scalar(inv[:], inv[:], float(N) ** -0.5, ALU.mult)
            vec.drain()
            for a in range(2):
                op = nc.vector.tensor_scalar(kxs[:, a, :], ps_kx[a][:, 0:F + 1], inv[:, a:a + 1], None, ALU.mult)
            op.then_inc(s["fin"], 1)
            vec.wait_ge(s["fins"], 1)
            nc.vector.tensor_copy(kxT[:], ps_end[:].rearrange("p (b c) -> p b c", b=2))
            nc.vector.tensor_copy(ksT[:], ps_k[0:1, 0:F])
            nc.vector.tensor_copy(bvwk[:], ps_row[0:1, 0:F]).then_inc(s["fin"], 1)
            vec.wait_ge(s["fins"], 2)
            nc.vector.tensor_copy(kvw[:], turn[0][:].rearrange("p (a f) -> p a f", a=2))

        @block.scalar
        def _(act):
            def copies(at, q):
                act.wait_ge(s["turned"], at + 1)
                act.wait_ge(s["k"], at + 1)
                view = turn[q][:, 0:F].rearrange("p (a n) -> p a n", a=2)
                nc.scalar.activation(xnT[:, q], view, ACT.Copy)
                nc.scalar.activation(hT[:, q], view, ACT.Relu).then_inc(s["copied"], 1)

            def rows(at, q, i):
                act.wait_ge(s["row"], at + 1)
                if i is not None:
                    act.wait_ge(s[f"out{q}"], 16 * i)
                nc.scalar.activation(row[:, q, :], ps_row[:, 0:ROW], ACT.Copy).then_inc(s["rowc"], 1)
                act.wait_ge(s["rowc"], at + 1)
                act.dma_start(table[bass.ds(at * P, P), :], row[:, q, :]).then_inc(s[f"out{q}"], 16)
                act.wait_ge(s["k"], at + 3)
                act.wait_ge(s["setup"], 1)
                nc.scalar.activation(sd[:, bass.ds(at * P, P)], ps_sd[0:H, 0:P], ACT.Copy).then_inc(s["sdc"], 1)
                act.wait_ge(s["kc"], at + 1)
                act.wait_ge(s["kx"], at + 1)
                nc.scalar.activation(k2[:, q, :], kc[:, q, :], ACT.Square, accum_out=k2s[:, q:q + 1]).then_inc(s["k2"], 1)

            act.sem_inc(s["sdc"], 1)
            act.sem_inc(s["k2"], 1)
            copies(0, 0)
            copies(1, 1)
            rows(0, 0, None)
            copies(2, 0)
            rows(1, 1, None)
            with act.Fori(1, NB // 2 - 1) as i:
                for q in range(2):
                    copies(2 * i + q + 1, 1 - q)
                    rows(2 * i + q, q, i)
            copies(NB - 1, 1)
            rows(NB - 2, 0, NB // 2 - 1)
            rows(NB - 1, 1, NB // 2 - 1)
            for q in range(2):
                act.wait_ge(s[f"out{q}"], 16 * (NB // 2))

        @block.tensor
        def _(pe):
            def turns(at, q):
                pe.wait_ge(s["xn"], at + 3)
                pe.wait_ge(s["copied"], at)
                for a in range(2):
                    op = nc.tensor.transpose(turn[q][:, a * P:a * P + P], xn[:, q, a * P:a * P + P], ident[:])
                op.then_inc(s["turned"], 1)

            def products(at, q, first=False):
                pe.wait_ge(s["copied"], at + 1)
                if not first:
                    pe.wait_ge(s["rowc"], at)
                for a in range(2):
                    op = nc.tensor.matmul(ps_row[:, 0:ROW], hT[:, q, a, :], wext[:, a, 0, :], start=(a == 0), stop=(a == 1))
                op.then_inc(s["row"], 1)
                pe.wait_ge(s["sdc"], at + 1)
                for a in range(2):
                    nc.tensor.matmul(ps_sd[0:H, 0:P], wdst[:, a, 0, :], hT[:, q, a, :], start=(a == 0), stop=(a == 1))
                if not first:
                    pe.wait_ge(s["kc"], at)
                for a in range(2):
                    op = nc.tensor.matmul(ps_k[:, 0:F], xnT[:, q, a, :], wk[:, a, :], start=(a == 0), stop=(a == 1))
                op.then_inc(s["k"], 1)

            def sums(at, q, first=False, end=False):
                pe.wait_ge(s["k2r"], at + 1)
                for a in range(2):
                    nc.tensor.matmul(ps_kx[a][:, 0:F + 1], k2r[:, q, a * P:a * P + P], xn[:, q, :], start=first, stop=end,
                                     skip_group_check=True)
                    op = nc.tensor.matmul(ps_kx[a][:, F + 1:F + 2], k4[:, q, a * P:a * P + P], ones[:], start=False,
                                          stop=end, skip_group_check=True)
                op.then_inc(s["kx"], 1)

            pe.sem_inc(s["kx"], 2)
            pe.sem_inc(s["k"], 2)
            pe.wait_ge(s["setup"], 1)
            pe.wait_ge(s["xn"], 3)
            for a in range(2):
                op = nc.tensor.transpose(turn[0][:, a * P:a * P + P], xn[:, 0, a * P:a * P + P], ident[:])
            op.then_inc(s["turned"], 1)
            products(0, 0, first=True)
            turns(1, 1)
            sums(0, 0, first=True)
            products(1, 1)
            turns(2, 0)
            sums(1, 1)
            with pe.Fori(1, NB // 2 - 1) as i:
                for q in range(2):
                    products(2 * i + q, q)
                    turns(2 * i + q + 1, 1 - q)
                    sums(2 * i + q, q)
            products(NB - 2, 0)
            turns(NB - 1, 1)
            sums(NB - 2, 0)
            products(NB - 1, 1)
            sums(NB - 1, 1, end=True)
            pe.wait_ge(s["fin"], 2)
            for b in range(2):
                for a in range(2):
                    nc.tensor.transpose(ps_end[:, b * F + a * P:b * F + a * P + P], kxs[:, a, b * P:b * P + P], ident[:])
            for a in range(2):
                nc.tensor.transpose(ps_k[0:1, a * P:a * P + P], kxs[:, a, F:F + 1], ident[:])
            for b in range(2):
                op = nc.tensor.matmul(ps_row[0:1, 0:F], bv2[:, b:b + 1], wvo[:, b, :], start=(b == 0), stop=(b == 1))
            op.then_inc(s["fins"], 1)
            pe.wait_ge(s["fin"], 3)
            for a in range(2):
                for b in range(2):
                    nc.tensor.matmul(turn[0][:, a * F:a * F + F], kxT[:, b, a * P:a * P + P], vw[:, b, :],
                                     start=(b == 0), stop=False)
                op = nc.tensor.matmul(turn[0][:, a * F:a * F + F], ksT[:, a * P:a * P + P], bvwk[:], start=False, stop=True)
            op.then_inc(s["fins"], 1)


def edges(nc, sb, pb, sem, v):
    layer = v["layer"]
    ident, acc, sep, same, ends = v["ident"], v["acc"], v["sep"], v["same"], v["ends"]
    parts, src_sb, rel, islast = v["parts"], v["src_sb"], v["rel"], v["islast"]
    first_sb, row_iota, wedge = v["first_sb"], v["row_iota"], v["wedge"]
    table, score_dst = v["table"][layer], v["score_dst"][layer]
    with ExitStack() as ctx:
        def tmp(name, shape, dt=F32):
            return sb(f"e{layer}_{name}", shape, dt, ctx)

        idx = tmp("idx", [P, 2, GT], I32)
        rows = [tmp(f"rows{q}", [P, GT, ROW]) for q in range(2)]
        win = tmp("win", [P, 2, P])
        winT = tmp("winT", [P, 2, P])
        eattr = tmp("eattr", [P, 2, 2, P])
        hot = tmp("hot", [P, 2, GT, WIN])
        hotT = tmp("hotT", [P, 4, P])
        sepg = tmp("sepg", [P, P + 1], BF16)
        al = tmp("al", [P, P])
        lr = tmp("lr", [P, P])
        peak = tmp("peak", [P, P])
        seg = tmp("seg", [P, P])
        less = tmp("less", [P, P])
        ex = tmp("ex", [P, P])
        run = tmp("run", [P, P])
        tot = tmp("tot", [P, P])
        prob = tmp("prob", [P, P])
        msg = tmp("msg", [P, 4, F])
        ps_al = pb(f"e{layer}_ps_al", [P, 512], ctx)
        ps_pr = [pb(f"e{layer}_ps_pr{q}", [P, 512], ctx) for q in range(2)]
        ps_hot = pb(f"e{layer}_ps_hot", [P, 512], ctx)
        ps_sum = [pb(f"e{layer}_ps_sum{q}", [P, 2, F], ctx) for q in range(4)]
        names = ("idx", "rows0", "rows1", "win0", "win1", "eattr0", "eattr1", "hot", "winT", "winTc", "hotT", "hotTc",
                 "scores", "leaky", "turned", "less", "ex", "prob", "probT", "msg", "sum", "window", "taken")
        s = {n: sem(f"e{layer}_{n}", ctx) for n in names}
        s_on = sem(f"e{layer}_on", ctx)
        block = ctx.enter_context(nc.Block())

        def plain(eng):
            eng.wait_ge(s_on, 1)


        @block.sync
        def _(sp):
            first = [sp.alloc_register(f"e{layer}_sp{k}") for k in range(GT)]

            def fetch(g, q, h):
                sp.wait_ge(s["scores"], g + 1)
                plain(sp)
                sp.reg_load(first, first_sb[0:1, bass.ds(g * GT, GT)])
                for k in range(GT):
                    at = sp.snap(first[k], min_val=0, max_val=N)
                    sp.dma_start(win[H * k:H * k + H, q, :], score_dst[:, bass.ds(at, P)]).then_inc(s[f"win{q}"], 16)
                sp.dma_start(eattr[:, q], v["edge_b"][:, bass.ds(g * 2, 2), :]).then_inc(s[f"eattr{q}"], 16)

            with sp.Fori(0, NG // 2) as i:
                for q in range(2):
                    fetch(2 * i + q, q, i)

        @block.gpsimd
        def _(pool):
            pool.sem_inc(s_on, 1)

            def gather(g, q):
                pool.wait_ge(s["msg"], 16 * g + 1)
                plain(pool)
                if True:
                    nc.gpsimd.tensor_copy(idx[:, q, :], src_sb[:, bass.ds(g * GT, GT)]).then_inc(s["idx"], 1)
                for k in range(GT):
                    pool.wait_ge(s["msg"], 16 * g + k + 1)
                    if k == 0:
                        pool.wait_ge(s["idx"], g + 1)
                    pool.nop(nofuse=True)
                    nc.gpsimd.indirect_dma_start(
                        out=rows[q][:, k, :], out_offset=None, in_=table,
                        in_offset=bass.IndirectOffsetOnAxis(ap=idx[:, q, k:k + 1], axis=0)).then_inc(s[f"rows{q}"], 16)

            with pool.Fori(0, NG // 2) as i:
                for q in range(2):
                    gather(2 * i + q, q)

        @block.vector
        def _(vec):
            def one_hots(g, q, r):
                if not isinstance(g, int) or g > 1:
                    vec.wait_ge(s["sum"], 16 * g + 4 * r - 12)
                plain(vec)
                nc.vector.tensor_copy(hot[:, q, 4 * r:4 * r + 4, P:P + 1],
                                      islast[:, bass.ds(g * GT + 4 * r, 4)].unsqueeze(2))
                nc.vector.tensor_tensor(hot[:, q, 4 * r:4 * r + 4, 0:P], row_iota[:].unsqueeze(1).broadcast_to((P, 4, P)),
                                        rel[:, bass.ds(g * GT + 4 * r, 4)].unsqueeze(2).broadcast_to((P, 4, P)),
                                        ALU.is_equal).then_inc(s["hot"], 1)

            def message(g, q, k):
                if k == 0:
                    vec.wait_ge(s["probT"], g + 1)
                vec.wait_ge(s["sum"], 16 * g + 16 + k - 3)
                nc.vector.tensor_tensor(
                    msg[:, k % 4, :].rearrange("p (h c) -> p h c", c=C),
                    rows[q][:, k, 0:F].rearrange("p (h c) -> p h c", c=C),
                    ps_pr[q][:, H * k:H * k + H].unsqueeze(2).broadcast_to((P, H, C)), ALU.mult).then_inc(s["msg"], 1)

            def leaky(g, q, i):
                vec.wait_ge(s["scores"], g + 3)
                vec.wait_ge(s[f"rows{q}"], 256 * i + 256)
                nc.vector.tensor_tensor(al[:].rearrange("p (k h) -> p k h", h=H),
                                        ps_al[:, 0:P].rearrange("p (k h) -> p k h", h=H), rows[q][:, :, F:ROW], ALU.add)
                vec.drain()
                nc.vector.scalar_tensor_tensor(lr[:], al[:], 0.2, al[:], ALU.mult, ALU.max).then_inc(s["leaky"], 1)

            def highest(g):
                nc.vector.tensor_copy(sepg[:], sep[:, bass.ds(g, 1), :].rearrange("p a b -> p (a b)"))
                vec.drain()
                vec.wait_ge(s["turned"], g + 1)
                nc.vector.tensor_tensor_scan(peak[:], sepg[:, 0:P], ps_al[:, P:2 * P], -BIG, ALU.add, ALU.max)
                vec.drain()

            def less_highest(g):
                nc.vector.tensor_tensor_scan(seg[:, ::-1], sepg[:, 1:P + 1][:, ::-1], peak[:, ::-1], -BIG, ALU.add, ALU.max)
                vec.drain()
                nc.vector.tensor_tensor(less[:], ps_al[:, P:2 * P], seg[:], ALU.subtract).then_inc(s["less"], 1)
                nc.vector.tensor_copy(ends[:, bass.ds(g, 1), :, 0:1].rearrange("p a b c -> p (a b c)"), seg[:, 0:P:P - 1])

            def running(g):
                vec.wait_ge(s["ex"], g + 2)
                nc.vector.tensor_tensor_scan(run[:], same[:, bass.ds(g, 1), 0:P].rearrange("p a b -> p (a b)"), ex[:],
                                             0.0, ALU.mult, ALU.add)
                vec.drain()

            def whole(g):
                nc.vector.tensor_tensor_scan(tot[:, ::-1], sepg[:, 1:P + 1][:, ::-1], run[:, ::-1], -BIG, ALU.add, ALU.max)
                vec.drain()
                nc.vector.tensor_copy(ends[:, bass.ds(g, 1), :, 1:2].rearrange("p a b c -> p (a b c)"), tot[:, 0:P:P - 1])
                nc.vector.tensor_single_scalar(run[:], tot[:], 1e-16, ALU.add)
                vec.drain()

            def inverse():
                nc.vector.reciprocal(seg[:], run[:])
                vec.drain()

            def probability(g):
                if not isinstance(g, int) or g > 0:
                    vec.wait_ge(s["probT"], g)
                nc.vector.tensor_tensor(prob[:], ex[:], seg[:], ALU.mult).then_inc(s["prob"], 1)

            def step(g, q, i, softmax=True, ahead=True):
                n, p = g + 1, 1 - q
                for k in range(GT):
                    message(g, q, k)
                    if softmax and k == 1:
                        one_hots(n, p, 3)
                    if ahead and k == 5:
                        one_hots(g + 2, q, 0)
                    if softmax and k == 6:
                        leaky(n, p, i if p == 1 else i + 1)
                    if softmax and k == 7:
                        highest(n)
                    if softmax and k == 8:
                        less_highest(n)
                    if ahead and k == 9:
                        one_hots(g + 2, q, 1)
                    if softmax and k == 10:
                        running(n)
                    if softmax and k == 11:
                        whole(n)
                    if softmax and k == 12:
                        inverse()
                    if softmax and k == 13:
                        probability(n)
                    if ahead and k == 14:
                        one_hots(g + 2, q, 2)

            vec.sem_inc(s["msg"], 32)
            vec.wait_ge(s_on, 1)
            for r in range(4):
                one_hots(0, 0, r)
            for r in range(3):
                one_hots(1, 1, r)
            leaky(0, 0, 0)
            highest(0)
            less_highest(0)
            running(0)
            whole(0)
            inverse()
            probability(0)
            with vec.Fori(0, NG // 2 - 1) as i:
                step(2 * i, 0, i)
                step(2 * i + 1, 1, i)
            step(NG - 2, 0, NG // 2 - 1, ahead=False)
            step(NG - 1, 1, NG // 2 - 1, softmax=False, ahead=False)

        @block.scalar
        def _(act):
            first = [act.alloc_register(f"e{layer}_act{k}") for k in range(GT)]

            def win_copy(g):
                act.wait_ge(s["winT"], g + 1)
                act.wait_ge(s["scores"], g + 2)
                nc.scalar.activation(winT[:, 0, :], ps_al[:, 2 * P:3 * P], ACT.Copy).then_inc(s["winTc"], 1)

            def hot_copy(g, r):
                act.wait_ge(s["hotT"], 4 * g + r + 1)
                nc.scalar.activation(hotT[:], ps_hot[:].rearrange("p (k e) -> p k e", k=4), ACT.Copy).then_inc(s["hotTc"], 1)

            def exps(g):
                act.wait_ge(s["less"], g + 1)
                nc.scalar.activation(ex[:], less[:], ACT.Exp).then_inc(s["ex"], 1)

            def window(g, k, at):
                act.wait_ge(s["window"], 16 * g + k + 1)
                act.wait_ge(s["sum"], 16 * g + 16 + k + 1)
                plain(act)
                nc.scalar.activation(acc[:, :, bass.ds(at[k], P)], ps_sum[k % 4][:, :, 0:P], ACT.Copy).then_inc(s["window"], 1)
                nc.scalar.activation(parts[:, bass.ds(g * GT + k, 1)].rearrange("p t a b -> p (t a) b"),
                                     ps_sum[k % 4][:, :, 0:P + 1:P], ACT.Copy).then_inc(s["taken"], 1)

            def step(g, q, softmax=True, ahead=True):
                act.reg_load(first, first_sb[0:1, bass.ds(g * GT, GT)])
                at = [act.snap(first[k], min_val=0, max_val=N) for k in range(GT)]
                for k in range(GT):
                    window(g, k, at)
                    if softmax and k == 1:
                        hot_copy(g + 1, 3)
                    if softmax and k == 8:
                        exps(g + 1)
                    if ahead and k == 8:
                        win_copy(g + 2)
                    if ahead and k in (5, 9, 14):
                        hot_copy(g + 2, {5: 0, 9: 1, 14: 2}[k])

            act.sem_inc(s["window"], 1)
            act.sem_inc(s["taken"], 4)
            act.sem_inc(s["ex"], 1)
            win_copy(0)
            for r in range(4):
                hot_copy(0, r)
            exps(0)
            win_copy(1)
            for r in range(3):
                hot_copy(1, r)
            with act.Fori(0, NG // 2 - 1) as i:
                step(2 * i, 0)
                step(2 * i + 1, 1)
            step(NG - 2, 0, ahead=False)
            step(NG - 1, 1, softmax=False, ahead=False)

        @block.tensor
        def _(pe):
            def turn_win(g, q, i):
                pe.wait_ge(s[f"win{q}"], 256 * i + 256)
                if not isinstance(g, int) or g > 0:
                    pe.wait_ge(s["less"], g)
                nc.tensor.transpose(ps_al[:, 2 * P:3 * P], win[:, q, :], ident[:]).then_inc(s["winT"], 1)

            def turn_hot(g, q, r):
                pe.wait_ge(s["hot"], 4 * g + r + 1)
                for k in range(4):
                    op = nc.tensor.transpose(ps_hot[:, k * P:k * P + P], hot[:, q, 4 * r + k, 0:P], ident[:])
                op.then_inc(s["hotT"], 1)

            def scores(g, q, r, i):
                if r == 0:
                    pe.wait_ge(s["winTc"], g + 1)
                    pe.wait_ge(s[f"eattr{q}"], 16 * i + 16)
                    for a in range(2):
                        nc.tensor.matmul(ps_al[:, 64 * a:64 * a + 64], eattr[:, q, a, :],
                                         wedge[:, layer].rearrange("p b h -> p (b h)"), start=(a == 0), stop=False,
                                         skip_group_check=True)
                pe.wait_ge(s["hotTc"], 4 * g + r + 1)
                for k in range(4):
                    m = H * (4 * r + k)
                    op = nc.tensor.matmul(ps_al[:, m:m + H], hotT[:, k, :], winT[:, 0, m:m + H], start=False,
                                          stop=(r == 3 and k == 3), skip_group_check=True)
                if r == 3:
                    op.then_inc(s["scores"], 1)

            def turn_alpha(g):
                pe.wait_ge(s["leaky"], g + 1)
                nc.tensor.transpose(ps_al[:, P:2 * P], lr[:], ident[:]).then_inc(s["turned"], 1)

            def turn_prob(g, q):
                pe.wait_ge(s["prob"], g + 1)
                nc.tensor.transpose(ps_pr[q][:, 0:P], prob[:], ident[:]).then_inc(s["probT"], 1)

            def total(g, q, k):
                pe.wait_ge(s["msg"], 16 * g + 32 + k + 1)
                pe.wait_ge(s["taken"], 16 * g + k + 1)
                for a in range(2):
                    op = nc.tensor.matmul(ps_sum[k % 4][:, a, 0:WIN], msg[:, k % 4, a * P:a * P + P], hot[:, q, k, :],
                                          start=(a == 0), stop=True, skip_group_check=True)
                op.then_inc(s["sum"], 1)

            def step(g, q, i, softmax=True, ahead=True):
                n, p, m, j = g + 1, 1 - q, g + 2, i + 1
                for k in range(GT):
                    total(g, q, k)
                    if softmax and k == 1:
                        turn_hot(n, p, 3)
                    if softmax and k == 2:
                        scores(n, p, 3, None)
                    if softmax and k == 6:
                        turn_alpha(n)
                    if ahead and k == 8:
                        turn_win(m, q, j)
                    if ahead and k in (9, 10, 15):
                        scores(m, q, {9: 0, 10: 1, 15: 2}[k], j)
                    if ahead and k in (5, 9, 14):
                        turn_hot(m, q, {5: 0, 9: 1, 14: 2}[k])
                    if softmax and k == 13:
                        turn_prob(n, p)

            def ahead_of_all(g, rounds):
                turn_win(g, g, 0)
                for r in range(rounds):
                    turn_hot(g, g, r)
                    scores(g, g, r, 0)

            pe.sem_inc(s["sum"], 16)
            pe.sem_inc(s["scores"], 2)
            ahead_of_all(0, 4)
            turn_alpha(0)
            turn_prob(0, 0)
            ahead_of_all(1, 3)
            with pe.Fori(0, NG // 2 - 1) as i:
                step(2 * i, 0, i)
                step(2 * i + 1, 1, i)
            step(NG - 2, 0, NG // 2 - 1, ahead=False)
            step(NG - 1, 1, NG // 2 - 1, softmax=False, ahead=False)


def join(nc, sb, pb, sem, v):
    layer, acc, ends, parts = v["layer"], v["acc"], v["ends"], v["parts"]
    kmask, hsel, first_sb = v["kmask"], v["hsel"], v["first_sb"]
    L = 2 * T
    with ExitStack() as ctx:
        def tmp(name, shape, dt=F32):
            return sb(f"j{layer}_{name}", shape, dt, ctx)

        picked = tmp("picked", [P, 3, GT, NG, 2])
        dest = tmp("dest", [P, L])
        mx = tmp("mx", [P, L])
        sm = tmp("sm", [P, L])
        begins = tmp("begins", [P, L + 1])
        sep = tmp("sep", [P, L + 1])
        same = tmp("same", [P, L + 1])
        a = tmp("a", [P, L])
        b = tmp("b", [P, L])
        total = tmp("total", [P, T, 2])
        ps = [pb(f"j{layer}_{q}", [P, 4, P], ctx) for q in range(8)]
        s_picked, s_ps, s_free, s_w, s_exp, s_total, s_start, s_put = (
            sem(f"j{layer}_{n}", ctx) for n in ("picked", "ps", "free", "w", "exp", "total", "start", "put"))
        block = ctx.enter_context(nc.Block())
        spreads = [(2, 0), (0, 0), (1, 0), (0, 1), (1, 1)]
        per = GT // 4

        def entries(t):
            return t.rearrange("p (g f k e) -> p f k g e", g=NG, f=per, k=4)

        def put_rows(eng, which):
            first = [eng.alloc_register(f"j{layer}_{which}_{k}") for k in range(8)]
            eng.wait_ge(s_total, 1)
            with eng.Fori(0, NG) as g:
                eng.reg_load(first, first_sb[0:1, bass.ds(g * GT + 8 * which, 8)])
                for k in range(8):
                    at = eng.snap(first[k], min_val=0, max_val=N)
                    to = acc[:, :, bass.ds(at, 1)].rearrange("p a b -> p (a b)")
                    of = total[:, bass.ds(g * GT + 8 * which + k, 1), :].rearrange("p a b -> p (a b)")
                    if which:
                        nc.scalar.activation(to, of, ACT.Copy)
                    else:
                        nc.vector.tensor_copy(to, of)

        @block.tensor
        def _(pe):
            pe.wait_ge(s_picked, 3)
            n = 0
            for j, (what, half) in enumerate(spreads):
                for f in range(per):
                    if n >= 8:
                        pe.wait_ge(s_free, n - 7)
                    for k in range(4):
                        op = nc.tensor.matmul(ps[n % 8][:, k, 0:2 * NG], hsel[:, half, :],
                                              picked[:, what, 4 * f + k].rearrange("p g e -> p (g e)"),
                                              start=True, stop=True, skip_group_check=True)
                    op.then_inc(s_ps, 1)
                    n += 1

        @block.scalar
        def _(act):
            for half in range(2):
                act.wait_ge(s_w, half + 1)
                nc.scalar.activation(a[:], b[:], ACT.Exp).then_inc(s_exp, 1)
            put_rows(act, 1)

        @block.vector
        def _(vec):
            for what in range(3):
                nc.vector.tensor_tensor(picked[:, what].rearrange("p k g e -> p k (g e)"),
                                        ends[:, :, :, what].rearrange("p g e -> p (g e)").unsqueeze(1).broadcast_to((P, GT, 2 * NG)),
                                        kmask[:].unsqueeze(2).broadcast_to((P, GT, 2 * NG)), ALU.mult).then_inc(s_picked, 1)
            taken = [0]

            def take(to):
                for f in range(per):
                    vec.wait_ge(s_ps, taken[0] + 1)
                    nc.vector.tensor_copy(entries(to)[:, f], ps[taken[0] % 8][:, :, 0:2 * NG].rearrange("p k (g e) -> p k g e", e=2)
                                          ).then_inc(s_free, 1)
                    taken[0] += 1

            take(dest[:])
            nc.vector.memset(begins[:], 1.0)
            vec.drain()
            nc.vector.tensor_tensor(begins[:, 1:L], dest[:, 1:L], dest[:, 0:L - 1], ALU.not_equal)
            vec.drain()
            nc.vector.tensor_single_scalar(sep[:], begins[:], -BIG, ALU.mult)
            nc.vector.tensor_scalar(same[:], begins[:], -1.0, 1.0, ALU.mult, ALU.add)
            vec.drain()
            for half in range(2):
                take(mx[:])
                take(sm[:])
                vec.drain()
                nc.vector.tensor_tensor_scan(dest[:], sep[:, 0:L], mx[:], -BIG, ALU.add, ALU.max)
                vec.drain()
                nc.vector.tensor_tensor_scan(b[:, ::-1], sep[:, 1:L + 1][:, ::-1], dest[:, ::-1], -BIG, ALU.add, ALU.max)
                vec.drain()
                nc.vector.tensor_tensor(b[:], mx[:], b[:], ALU.subtract).then_inc(s_w, 1)
                vec.wait_ge(s_exp, half + 1)
                nc.vector.tensor_tensor(a[:], a[:], sm[:], ALU.mult)
                vec.drain()
                nc.vector.tensor_tensor(a[:, 1:L:2], a[:, 1:L:2], begins[:, 1:L:2], ALU.mult)
                vec.drain()
                nc.vector.tensor_tensor_scan(dest[:], same[:, 0:L], a[:], 0.0, ALU.mult, ALU.add)
                vec.drain()
                nc.vector.tensor_tensor_scan(b[:, ::-1], sep[:, 1:L + 1][:, ::-1], dest[:, ::-1], -BIG, ALU.add, ALU.max)
                vec.drain()
                nc.vector.tensor_single_scalar(b[:], b[:], 1e-16, ALU.add)
                vec.drain()
                nc.vector.reciprocal(b[:], b[:])
                vec.drain()
                nc.vector.tensor_tensor(a[:], a[:], b[:], ALU.mult)
                vec.drain()
                nc.vector.tensor_tensor(a[:].rearrange("p (t e) -> p t e", e=2), a[:].rearrange("p (t e) -> p t e", e=2),
                                        parts[:, :, half, :], ALU.mult)
                vec.drain()
                nc.vector.tensor_tensor_scan(b[:], same[:, 0:L], a[:], 0.0, ALU.mult, ALU.add)
                vec.drain()
                nc.vector.tensor_tensor(b[:], b[:], begins[:, 1:L + 1], ALU.mult)
                vec.drain()
                nc.vector.tensor_tensor_scan(a[:, ::-1], same[:, 1:L + 1][:, ::-1], b[:, ::-1], 0.0, ALU.mult, ALU.add)
                vec.drain()
                nc.vector.tensor_copy(total[:, :, half], a[:, 0:L:2])
                vec.drain()
            vec.sem_inc(s_total, 1)
            put_rows(vec, 0)


def second_table(nc, sb, pb, sem, v):
    acc, wext, wdst, gbias = v["acc"], v["wext"], v["wdst"], v["gbias"]
    table, score_dst = v["table"][1], v["score_dst"][1]
    with ExitStack() as ctx:
        hT = sb("h2T", [P, 2, 2, P], F32, ctx)
        row = sb("row2", [P, 2, ROW], F32, ctx)
        sd = sb("sd2", [H, NP], F32, ctx)
        ps_row = [pb(f"ps2_row{q}", [P, 512], ctx) for q in range(2)]
        ps_sd = [pb(f"ps2_sd{q}", [P, 512], ctx) for q in range(2)]
        s_h, s_row, s_rowc, s_sdc, s_sd, s_on = (sem("t2_" + n, ctx) for n in ("h", "row", "rowc", "sdc", "sd", "on"))
        s_out = [sem(f"t2_out{q}", ctx) for q in range(2)]
        block = ctx.enter_context(nc.Block())

        @block.scalar
        def _(act):
            act.sem_inc(s_on, 1)
            with act.Fori(0, NB // 2) as i:
                for q in range(2):
                    at = 2 * i + q
                    act.wait_ge(s_row, at + 1)
                    act.wait_ge(s_on, 1)
                    for a in range(2):
                        op = nc.scalar.activation(hT[:, q, a, :], acc[:, a, bass.ds(at * P, P)], ACT.Relu, bias=gbias[:, 0, a:a + 1])
                    op.then_inc(s_h, 1)

        @block.tensor
        def _(pe):
            pe.sem_inc(s_row, 2)
            with pe.Fori(0, NB // 2) as i:
                for q in range(2):
                    at = 2 * i + q
                    pe.wait_ge(s_h, at + 1)
                    pe.wait_ge(s_rowc, at + 1)
                    pe.wait_ge(s_sdc, at + 1)
                    for a in range(2):
                        nc.tensor.matmul(ps_row[q][:, 0:ROW], hT[:, q, a, :], wext[:, a, 1, :], start=(a == 0), stop=(a == 1))
                    for a in range(2):
                        op = nc.tensor.matmul(ps_sd[q][0:H, 0:P], wdst[:, a, 1, :], hT[:, q, a, :], start=(a == 0), stop=(a == 1))
                    op.then_inc(s_row, 1)

        @block.vector
        def _(vec):
            vec.sem_inc(s_rowc, 2)
            vec.sem_inc(s_sdc, 2)

            def rows(at, q, i):
                vec.wait_ge(s_row, at + 3)
                if i is not None:
                    vec.wait_ge(s_out[q], 16 * i)
                nc.vector.tensor_copy(row[:, q, :], ps_row[q][:, 0:ROW]).then_inc(s_rowc, 1)
                nc.vector.tensor_copy(sd[:, bass.ds(at * P, P)], ps_sd[q][0:H, 0:P]).then_inc(s_sdc, 1)

            rows(0, 0, None)
            rows(1, 1, None)
            with vec.Fori(1, NB // 2) as i:
                for q in range(2):
                    rows(2 * i + q, q, i)

        @block.sync
        def _(sp):
            with sp.Fori(0, NB // 2) as i:
                for q in range(2):
                    sp.wait_ge(s_rowc, 2 * i + q + 3)
                    sp.dma_start(table[bass.ds((2 * i + q) * P, P), :], row[:, q, :]).then_inc(s_out[q], 16)
            sp.wait_ge(s_sdc, NB + 2)
            sp.dma_start(score_dst, sd[:]).then_inc(s_sd, 16)
            sp.wait_ge(s_sd, 16)
            for q in range(2):
                sp.wait_ge(s_out[q], 16 * (NB // 2))


def last(nc, sb, pb, sem, v):
    ident, acc, gbias, cst = v["ident"], v["acc"], v["gbias"], v["cst"]
    wq, bq, vw, bvw, kvw, row_iota = v["wq"], v["bq"], v["vw"], v["bvw"], v["kvw"], v["row_iota"]
    x, out = v["x"], v["out"]
    CH = 2 * P
    with ExitStack() as ctx:
        def tmp(name, shape, dt=F32):
            return sb("l_" + name, shape, dt, ctx)

        ew = tmp("ew", [P, 3, NEXP, 2, F])
        eb = tmp("eb", [P, 2, NEXP, 2])
        eb3 = tmp("eb3", [NEXP, F])
        rw1 = tmp("rw1", [P, 2, P])
        rb1 = tmp("rb1", [P, 1])
        rw2 = tmp("rw2", [P, NEXP])
        rb2 = tmp("rb2", [P, NEXP])
        xb = tmp("xb", [P, 2, 2, F])
        xn = tmp("xn", [P, 2, F])
        base = tmp("base", [P, 2, F])
        stats = tmp("stats", [P, 2, 6])
        mv = tmp("mv", [P, 2, 2])
        eps = tmp("eps", [P, 2])
        rstd = tmp("rstd", [P, 2])
        xnT = tmp("xnT", [P, 2, CH])
        qc = tmp("qc", [P, 2, F])
        q2 = tmp("q2", [P, 2, F])
        q4 = tmp("q4", [P, 2, F])
        qs = tmp("qs", [P, 8])
        q2n = tmp("q2n", [P, 2, F])
        q2T = tmp("q2T", [P, 2, CH])
        gT = tmp("gT", [P, 2, CH])
        x2 = tmp("x2", [P, 2, 2, F])
        yn = tmp("yn", [P, 2, F])
        yT = tmp("yT", [P, 2, 2, CH])
        rhT = tmp("rhT", [P, CH])
        logit = tmp("logit", [P, 2, NEXP])
        prob = tmp("prob", [P, 2, 8])
        small = tmp("small", [P, 2, 8])
        top8 = tmp("top8", [P, 2, 8])
        at8 = tmp("at8", [P, 2, 8], U32)
        at8f = tmp("at8f", [P, 2, 8])
        gate = tmp("gate", [P, 2, 2, NEXP])
        gate2 = tmp("gate2", [P, 2, NEXP])
        gateT = tmp("gateT", [NEXP, CH])
        h1 = tmp("h1", [P, 2, CH])
        h2 = tmp("h2", [P, 2, CH])
        res = tmp("res", [P, 2, 2, F])
        ps_t, ps_q, ps_m, ps_r, ps_h1, ps_h2, ps_o0, ps_o1 = (
            pb("l_ps_" + n, [P, 512], ctx) for n in ("t", "q", "m", "r", "h1", "h2", "o0", "o1"))
        ps_o = [ps_o0, ps_o1]
        names = ("w_in", "x0", "x1", "out0", "out1", "eps", "rstd", "xn", "t", "tc", "g", "q", "qc", "qs", "qss", "qsr", "q2n",
                 "mix", "x2", "eps2", "rstd2", "yn", "rh", "rhc", "lg", "mx", "pe_", "gap", "ge", "gate", "gateT", "gateTc",
                 "b3", "init", "h1", "h1c", "h2", "h2c", "o", "oc", "base")
        s = {n: sem("l_" + n, ctx) for n in names}
        s_on = sem("l_on", ctx)
        block = ctx.enter_context(nc.Block())
        loads = []
        for m, (we, be) in enumerate((("ew1", "eb1"), ("ew2", "eb2"), ("ew3", None))):
            for e in range(NEXP):
                loads.append((ew[:, m, e], v[we][e].rearrange("(a p) f -> p a f", p=P)))
                if be:
                    for a in range(2):
                        loads.append((eb[:, m, e, a:a + 1], v[be].rearrange("e (a p b) -> e a p b", p=P, b=1)[e, a]))
        loads += [(eb3[:], v["eb3"]), (rw1[:], v["rw1"].rearrange("(a p) f -> p a f", p=P)),
                  (rb1[:], v["rb1"].rearrange("(p b) -> p b", b=1)), (rw2[:], v["rw2"]),
                  (rb2[:], v["rb2"].rearrange("(a f) -> a f", a=1).broadcast_to((P, NEXP)))]

        @block.sync
        def _(sp):
            sp.dma_start(xb[:, 0], x[0:CH, :].rearrange("(b p) f -> p b f", p=P)).then_inc(s["x0"], 16)
            for to, of in loads:
                sp.dma_start(to, of).then_inc(s["w_in"], 16)

            def store(n, q, i):
                sp.wait_ge(s["oc"], NEXP * n + NEXP + 2)
                sp.dma_start(out[bass.ds(n * CH, CH), :].rearrange("(b p) f -> p b f", p=P), res[:, q]).then_inc(s[f"out{q}"], 16)

            def fetch(n, q):
                sp.wait_ge(s["base"], n)
                sp.dma_start(xb[:, q], x[bass.ds(n * CH, CH), :].rearrange("(b p) f -> p b f", p=P)).then_inc(s[f"x{q}"], 16)

            with sp.Fori(0, NCH // 2) as i:
                for q in range(2):
                    fetch(2 * i + q + 1, 1 - q)
                    store(2 * i + q, q, i)
            store(NCH - 1, 0, NCH // 2)
            sp.wait_ge(s["out0"], 16 * (NCH // 2 + 1))
            sp.wait_ge(s["out1"], 16 * (NCH // 2))

        @block.gpsimd
        def _(pool):
            pool.sem_inc(s_on, 1)

            def power(o, i_, e, wait, at, done):
                pool.wait_ge(s[wait], at)
                nc.gpsimd.tensor_tensor(o, i_, cst[:, e:e + 1].broadcast_to((P, 2)), ALU.pow).then_inc(s[done], 1)

            def both(n, q):
                power(rstd[:], eps[:], 0, "eps", n + 1, "rstd")
                pool.wait_ge(s["xn"], n + 1)
                pool.wait_ge(s["x2"], n + 1)
                nc.gpsimd.tensor_tensor(base[:], xb[:, q], xn[:], ALU.add)
                pool.drain()
                nc.gpsimd.tensor_tensor(base[:], base[:], bvw[:].unsqueeze(1).broadcast_to((P, 2, F)), ALU.add
                                        ).then_inc(s["base"], 1)
                power(qs[:, 4:6], qs[:, 2:4], 1, "qss", n + 1, "qsr")
                power(rstd[:], eps[:], 0, "eps2", n + 1, "rstd2")

            pool.sem_inc(s["base"], 1)
            both(0, 0)
            with pool.Fori(0, NCH // 2) as i:
                for q in range(2):
                    both(2 * i + q + 1, 1 - q)

        @block.vector
        def _(vec):
            def norm(src, to, n, e, r, done):
                for b in range(2):
                    nc.vector.bn_stats(stats[:, b, :], src[:, b, :])
                vec.drain()
                for b in range(2):
                    nc.vector.bn_aggr(mv[:, b, :], stats[:, b, :])
                vec.drain()
                nc.vector.tensor_single_scalar(eps[:], mv[:, :, 1], LN_EPS, ALU.add).then_inc(s[e], 1)
                vec.wait_ge(s[r], n + 1)
                for b in range(2):
                    op = nc.vector.tensor_scalar(to[:, b, :], src[:, b, :], mv[:, b, 0:1], rstd[:, b:b + 1], ALU.subtract, ALU.mult)
                op.then_inc(s[done], 1)

            def f0(n, q, i):
                vec.wait_ge(s[f"x{q}"], 16 * i + 16)
                vec.wait_ge(s["base"], n + 1)
                norm(xb[:, q], xn, n, "eps", "rstd", "xn")

            def f1(n, q):
                vec.wait_ge(s["q"], n + 1)
                nc.vector.tensor_tensor(qc[:], ps_q[:].rearrange("p (b f) -> p b f", b=2),
                                        bq[:].unsqueeze(1).broadcast_to((P, 2, F)), ALU.add).then_inc(s["qc"], 1)
                vec.wait_ge(s["qss"], n + 1)
                nc.vector.tensor_single_scalar(qs[:, 0:2], qs[:, 0:2], EPS_DIV, ALU.add)
                vec.drain()
                nc.vector.reciprocal(qs[:, 6:8], qs[:, 0:2])
                vec.drain()
                vec.wait_ge(s["qsr"], n + 1)
                nc.vector.tensor_tensor(qs[:, 4:6], qs[:, 4:6], qs[:, 6:8], ALU.mult)
                vec.drain()
                nc.vector.tensor_single_scalar(qs[:, 4:6], qs[:, 4:6], EPS_NORM, ALU.max)
                vec.drain()
                nc.vector.reciprocal(qs[:, 4:6], qs[:, 4:6])
                vec.drain()
                nc.vector.tensor_tensor(qs[:, 4:6], qs[:, 4:6], qs[:, 6:8], ALU.mult)
                vec.drain()
                for b in range(2):
                    op = nc.vector.tensor_scalar(q2n[:, b, :], q2[:, b, :], qs[:, 4 + b:5 + b], None, ALU.mult)
                op.then_inc(s["q2n"], 1)

            def f2(n, q):
                vec.wait_ge(s["mix"], n + 1)
                vec.wait_ge(s["base"], n + 2)
                nc.vector.tensor_tensor(x2[:, q], ps_m[:].rearrange("p (b f) -> p b f", b=2), base[:], ALU.add)
                vec.drain()
                nc.vector.tensor_tensor(x2[:, q], ps_t[:].rearrange("p (b f) -> p b f", b=2), x2[:, q], ALU.add
                                        ).then_inc(s["x2"], 1)
                vec.wait_ge(s["x2"], n + 2)
                norm(x2[:, q], yn, n, "eps2", "rstd2", "yn")

            def f3(n, q):
                vec.wait_ge(s["lg"], n + 1)
                nc.vector.tensor_tensor(logit[:], ps_r[:, CH:CH + 2 * NEXP].rearrange("p (b e) -> p b e", b=2),
                                        rb2[:].unsqueeze(1).broadcast_to((P, 2, NEXP)), ALU.add)
                vec.drain()
                nc.vector.tensor_reduce(small[:, :, 0], logit[:], AX.X, ALU.max)
                vec.drain()
                nc.vector.tensor_tensor(logit[:], logit[:], small[:, :, 0:1].broadcast_to((P, 2, NEXP)), ALU.subtract
                                        ).then_inc(s["mx"], 1)
                vec.wait_ge(s["pe_"], n + 1)
                nc.vector.tensor_reduce(small[:, :, 1], prob[:, :, 0:NEXP], AX.X, ALU.add)
                vec.drain()
                nc.vector.reciprocal(small[:, :, 2], small[:, :, 1])
                vec.drain()
                nc.vector.tensor_tensor(prob[:, :, 0:NEXP], prob[:, :, 0:NEXP], small[:, :, 2:3].broadcast_to((P, 2, NEXP)),
                                        ALU.mult)
                vec.drain()
                for b in range(2):
                    nc.vector.max(top8[:, b, :], prob[:, b, :])
                vec.drain()
                for b in range(2):
                    nc.vector.max_index(at8[:, b, :], top8[:, b, :], prob[:, b, :])
                nc.vector.tensor_tensor(small[:, :, 3], top8[:, :, 1], top8[:, :, 0], ALU.subtract).then_inc(s["gap"], 1)
                vec.wait_ge(s["gap"], n + 1)
                nc.vector.tensor_copy(at8f[:], at8[:])
                vec.wait_ge(s["ge"], n + 1)
                nc.vector.tensor_single_scalar(small[:, :, 5], small[:, :, 4], 1.0, ALU.add)
                vec.drain()
                nc.vector.reciprocal(small[:, :, 6], small[:, :, 5])
                vec.drain()
                nc.vector.tensor_tensor(small[:, :, 7], small[:, :, 6], small[:, :, 4], ALU.mult)
                vec.drain()
                for b in range(2):
                    nc.vector.tensor_scalar(gate[:, q, b, :], row_iota[:, 0:NEXP], at8f[:, b, 0:1], small[:, b, 6:7],
                                            ALU.is_equal, ALU.mult)
                    nc.vector.tensor_scalar(gate2[:, b, :], row_iota[:, 0:NEXP], at8f[:, b, 1:2], small[:, b, 7:8],
                                            ALU.is_equal, ALU.mult)
                vec.drain()
                nc.vector.tensor_tensor(gate[:, q], gate[:, q], gate2[:], ALU.add).then_inc(s["gate"], 1)

            def f4(n, q, i):
                vec.wait_ge(s["b3"], n + 1)
                if i is not None:
                    vec.wait_ge(s[f"out{q}"], 16 * i)
                nc.vector.tensor_tensor(res[:, q], ps_m[:].rearrange("p (b f) -> p b f", b=2), x2[:, q], ALU.add
                                        ).then_inc(s["init"], 1)

            def expert(n, q, e):
                vec.wait_ge(s["o"], NEXP * n + e + 2)
                if e == 0:
                    vec.wait_ge(s["init"], n + 1)
                else:
                    vec.wait_ge(s["oc"], NEXP * n + e + 2)
                for b in range(2):
                    op = nc.vector.scalar_tensor_tensor(res[:, q, b, :], ps_o[e % 2][:, b * F:b * F + F], gate[:, q, b, e:e + 1],
                                                        res[:, q, b, :], ALU.mult, ALU.add)
                op.then_inc(s["oc"], 1)

            def step(n, q, i, j, more=True):
                for e in range(NEXP):
                    expert(n, q, e)
                    if more and e == 0:
                        f0(n + 1, 1 - q, i if q == 0 else i + 1)
                    if more and e == 1:
                        f1(n + 1, 1 - q)
                    if more and e == 2:
                        f2(n + 1, 1 - q)
                    if more and e == 4:
                        f3(n + 1, 1 - q)
                if more:
                    f4(n + 1, 1 - q, j)

            nc.vector.memset(prob[:, :, NEXP:8], -1.0)
            vec.sem_inc(s["x2"], 1)
            vec.sem_inc(s["oc"], 2)
            vec.wait_ge(s["w_in"], 16 * len(loads))
            f0(0, 0, 0)
            f1(0, 0)
            f2(0, 0)
            f3(0, 0)
            f4(0, 0, None)
            step(0, 0, 0, None)
            step(1, 1, 0, 1)
            with vec.Fori(1, NCH // 2) as i:
                step(2 * i, 0, i, i)
                step(2 * i + 1, 1, i, i + 1)
            step(NCH - 1, 0, NCH // 2, None, more=False)

        @block.scalar
        def _(act):
            def turned(n, k, to):
                act.wait_ge(s["t"], 4 * n + k + 1)
                nc.scalar.activation(to, ps_t[:].rearrange("p (a m) -> p a m", a=2), ACT.Copy).then_inc(s["tc"], 1)

            def g0(n):
                for a in range(2):
                    op = nc.scalar.activation(gT[:, a, :], acc[:, a, bass.ds(n * CH, CH)], ACT.Identity, bias=gbias[:, 1, a:a + 1])
                op.then_inc(s["g"], 1)

            def g1(n):
                act.wait_ge(s["qc"], n + 1)
                for b in range(2):
                    nc.scalar.activation(q2[:, b, :], qc[:, b, :], ACT.Square, accum_out=qs[:, b:b + 1])
                act.drain()
                for b in range(2):
                    op = nc.scalar.activation(q4[:, b, :], q2[:, b, :], ACT.Square, accum_out=qs[:, 2 + b:3 + b])
                op.then_inc(s["qss"], 1)

            def g3(n, q):
                turned(n, 3, yT[:, q])
                act.wait_ge(s["rh"], n + 1)
                nc.scalar.activation(rhT[:], ps_r[:, 0:CH], ACT.Relu, bias=rb1[:]).then_inc(s["rhc"], 1)

            def g4(n):
                act.wait_ge(s["mx"], n + 1)
                nc.scalar.activation(prob[:, :, 0:NEXP], logit[:], ACT.Exp).then_inc(s["pe_"], 1)
                act.wait_ge(s["gap"], n + 1)
                nc.scalar.activation(small[:, :, 4], small[:, :, 3], ACT.Exp).then_inc(s["ge"], 1)

            def g5(n):
                act.wait_ge(s["gateT"], n + 1)
                nc.scalar.activation(gateT[:], ps_r[0:NEXP, 0:CH], ACT.Copy).then_inc(s["gateTc"], 1)

            def hidden(n, e, m, ps, to, name):
                act.wait_ge(s[name], NEXP * n + e + 1)
                if m == 1:
                    act.wait_ge(s["o"], NEXP * n + e + 1)
                for a in range(2):
                    op = nc.scalar.activation(to[:, a, :], ps[:, a * CH:a * CH + CH], ACT.Relu, bias=eb[:, m, e, a:a + 1])
                op.then_inc(s[name + "c"], 1)

            def step(n, q, more=True):
                for e in range(NEXP):
                    hidden(n, e, 1, ps_h2, h2, "h2")
                    if more and e == 0:
                        g0(n + 1)
                    if more and e == 1:
                        turned(n + 1, 0, xnT[:])
                    if more and e == 2:
                        g1(n + 1)
                    if more and e == 3:
                        turned(n + 1, 1, q2T[:])
                    if more and e == 4:
                        g3(n + 1, 1 - q)
                    if more and e == 5:
                        g4(n + 1)
                    if e + 1 < NEXP:
                        hidden(n, e + 1, 0, ps_h1, h1, "h1")
                if more:
                    hidden(n + 1, 0, 0, ps_h1, h1, "h1")
                    g5(n + 1)

            act.wait_ge(s["w_in"], 16 * len(loads))
            g0(0)
            turned(0, 0, xnT[:])
            g1(0)
            turned(0, 1, q2T[:])
            g3(0, 0)
            g4(0)
            hidden(0, 0, 0, ps_h1, h1, "h1")
            g5(0)
            with act.Fori(0, NCH // 2) as i:
                for q in range(2):
                    step(2 * i + q, q)
            step(NCH - 1, 0, more=False)

        @block.tensor
        def _(pe):
            def turn(of, name=None, at=None):
                for a in range(2):
                    for b in range(2):
                        op = nc.tensor.transpose(ps_t[:, a * CH + b * P:a * CH + b * P + P], of[:, b, a * P:a * P + P], ident[:])
                op.then_inc(s["t"], 1)

            def p0(n):
                pe.wait_ge(s["xn"], n + 1)
                pe.wait_ge(s["tc"], 3 * n + 1)
                turn(xn)
                pe.wait_ge(s["tc"], 3 * n + 2)
                for b in range(2):
                    for a in range(2):
                        op = nc.tensor.matmul(ps_q[:, b * F:b * F + F], xnT[:, a, b * P:b * P + P], wq[:, a, :],
                                              start=(a == 0), stop=(a == 1))
                op.then_inc(s["q"], 1)

            def p1(n):
                pe.wait_ge(s["q2n"], n + 1)
                turn(q2n)
                pe.wait_ge(s["tc"], 3 * n + 3)
                pe.wait_ge(s["g"], n + 1)
                for b in range(2):
                    for a in range(2):
                        op = nc.tensor.transpose(ps_t[:, b * F + a * P:b * F + a * P + P], gT[:, a, b * P:b * P + P], ident[:])
                op.then_inc(s["t"], 1)
                if not (isinstance(n, int) and n == 0):
                    pe.wait_ge(s["init"], n)
                for b in range(2):
                    for a in range(2):
                        nc.tensor.matmul(ps_m[:, b * F:b * F + F], xnT[:, a, b * P:b * P + P], vw[:, a, :], start=(a == 0), stop=False)
                    for a in range(2):
                        op = nc.tensor.matmul(ps_m[:, b * F:b * F + F], q2T[:, a, b * P:b * P + P], kvw[:, a, :],
                                              start=False, stop=(a == 1))
                op.then_inc(s["mix"], 1)

            def p2(n, q):
                pe.wait_ge(s["yn"], n + 1)
                turn(yn)
                pe.wait_ge(s["tc"], 3 * n + 4)
                for a in range(2):
                    op = nc.tensor.matmul(ps_r[:, 0:CH], rw1[:, a, :], yT[:, q, a, :], start=(a == 0), stop=(a == 1))
                op.then_inc(s["rh"], 1)

            def p3(n):
                pe.wait_ge(s["rhc"], n + 1)
                for b in range(2):
                    op = nc.tensor.matmul(ps_r[:, CH + b * NEXP:CH + b * NEXP + NEXP], rhT[:, b * P:b * P + P], rw2[:],
                                          start=True, stop=True)
                op.then_inc(s["lg"], 1)

            def p4(n, q):
                pe.wait_ge(s["gate"], n + 1)
                for b in range(2):
                    op = nc.tensor.transpose(ps_r[0:NEXP, b * P:b * P + P], gate[:, q, b, :], ident[:])
                op.then_inc(s["gateT"], 1)
                pe.wait_ge(s["gateTc"], n + 1)
                pe.wait_ge(s["x2"], n + 2)
                for b in range(2):
                    op = nc.tensor.matmul(ps_m[:, b * F:b * F + F], gateT[:, b * P:b * P + P], eb3[:], start=True, stop=True)
                op.then_inc(s["b3"], 1)

            def first(n, q, e):
                if e > 0 or not (isinstance(n, int) and n == 0):
                    pe.wait_ge(s["h1c"], NEXP * n + e)
                for a in range(2):
                    for k in range(2):
                        op = nc.tensor.matmul(ps_h1[:, a * CH:a * CH + CH], ew[:, 0, e, k, a * P:a * P + P], yT[:, q, k, :],
                                              start=(k == 0), stop=(k == 1))
                op.then_inc(s["h1"], 1)

            def second(n, e):
                pe.wait_ge(s["h1c"], NEXP * n + e + 1)
                for a in range(2):
                    for k in range(2):
                        op = nc.tensor.matmul(ps_h2[:, a * CH:a * CH + CH], ew[:, 1, e, k, a * P:a * P + P], h1[:, k, :],
                                              start=(k == 0), stop=(k == 1))
                op.then_inc(s["h2"], 1)

            def third(n, e):
                pe.wait_ge(s["h2c"], NEXP * n + e + 1)
                pe.wait_ge(s["oc"], NEXP * n + e + 1)
                for b in range(2):
                    for k in range(2):
                        op = nc.tensor.matmul(ps_o[e % 2][:, b * F:b * F + F], h2[:, k, b * P:b * P + P], ew[:, 2, e, k, :],
                                              start=(k == 0), stop=(k == 1))
                op.then_inc(s["o"], 1)

            def step(n, q, more=True):
                for e in range(NEXP):
                    second(n, e)
                    if more and e == 1:
                        p0(n + 1)
                    if more and e == 3:
                        p1(n + 1)
                    if more and e == 4:
                        p2(n + 1, 1 - q)
                    if more and e == 5:
                        p3(n + 1)
                    if e + 1 < NEXP:
                        first(n, q, e + 1)
                    third(n, e)
                if more:
                    first(n + 1, 1 - q, 0)
                    p4(n + 1, 1 - q)

            pe.sem_inc(s["tc"], 1)
            pe.sem_inc(s["o"], 1)
            pe.wait_ge(s["w_in"], 16 * len(loads))
            p0(0)
            p1(0)
            p2(0, 0)
            p3(0)
            first(0, 0, 0)
            p4(0, 0)
            with pe.Fori(0, NCH // 2) as i:
                for q in range(2):
                    step(2 * i + q, q)
            step(NCH - 1, 0, more=False)


INS = ["x", "src_t", "dst_t", "dst_g", "first_row", "last_row", "edge_b", "W1", "as1", "ad1", "We1", "ae1", "b1", "W2", "as2",
       "ad2", "We2", "ae2", "b2", "Wqkv", "bqkv", "Wout", "bout", "rw1", "rb1", "rw2", "rb2", "ew1", "eb1", "ew2", "eb2",
       "ew3", "eb3"]


def kernel(x, src, dst, edge_attr_16, **w):
    import concourse.bacc as bacc
    from concourse.bass_utils import run_bass_kernel_spmd

    src_p = np.pad(np.asarray(src), (0, EP - E))
    dst_p = np.pad(np.asarray(dst), (0, EP - E), constant_values=N)
    edge_p = np.pad(np.asarray(edge_attr_16), ((0, EP - E), (0, 0)))
    arrays = {
        "x": np.pad(np.asarray(x), ((0, NP - N), (0, 0))),
        "src_t": src_p.reshape(T, P).T,
        "dst_t": dst_p.reshape(T, P).T,
        "dst_g": dst_p.reshape(NG, GT, P),
        "first_row": dst_p[None, ::P],
        "last_row": dst_p[None, P - 1::P],
        "edge_b": edge_p.reshape(T // H, H, P, D_EDGE).transpose(1, 3, 0, 2).reshape(P, T // H, P),
    }
    for l in "12":
        for to, of in (("W", "W"), ("as", "att_src"), ("ad", "att_dst"), ("We", "W_e"), ("ae", "att_e"), ("b", "b")):
            arrays[to + l] = w["L0_gnn_" + of + l]
    for to, of in (("Wqkv", "W_qkv"), ("bqkv", "b_qkv"), ("Wout", "W_out"), ("bout", "b_out")):
        arrays[to] = w["L0_mix_" + of]
    for to, of in (("r", "router"), ("e", "expert")):
        for part in ("w1", "b1", "w2", "b2") + (("w3", "b3") if to == "e" else ()):
            arrays[to + part] = w[f"L0_ffn_{of}_{part}"]
    nc = bacc.Bacc("TRN2", target_bir_lowering=False, num_devices=1)
    maps, args = {}, []
    for name in INS:
        a = np.ascontiguousarray(arrays[name])
        maps["in_" + name] = a
        args.append(nc.dram_tensor("in_" + name, a.shape, mybir.dt.from_np(a.dtype), kind="ExternalInput").ap())
    args.append(nc.dram_tensor("out_x", (NP, F), F32, kind="ExternalOutput").ap())
    build(nc, *args)
    r = run_bass_kernel_spmd(nc, [maps], core_ids=[0])
    return r.results[0]["out_x"][:N]
```

```python
from contextlib import ExitStack

import numpy as np

import concourse.bass as bass
from concourse import mybir

F32 = mybir.dt.float32
BF16 = mybir.dt.bfloat16
I32 = mybir.dt.int32
U32 = mybir.dt.uint32
ALU = mybir.AluOpType
ACT = mybir.ActivationFunctionType
AX = mybir.AxisListType

P = 128
N = 6250
E = 106250
F = 256
H = 8
C = F // H
D_EDGE = 16
NEXP = 6
NB = 50
NP = NB * P
GT = P // H
NG = -(-E // (P * GT))
T = NG * GT
EP = T * P
ROW = F + 2 * H
L = 2 * T
NFIX = -(-T // P)
WIN = P + 1
BIG = 1e38
LN_EPS = 1e-5
EPS_DIV = 1e-7
EPS_NORM = 1e-12
CH = 2 * P
NCH = NP // CH


def ln_stats(nc, vec, x, stats, mv):
    nc.vector.bn_stats(stats, x)
    vec.drain()
    nc.vector.bn_aggr(mv, stats)


def build(nc, x, src_t, dst_t, dst_g, first_row, last_row, edge_b, W1, as1, ad1, We1, ae1, b1, W2, as2, ad2, We2,
          ae2, b2, Wqkv, bqkv, Wout, bout, rw1, rb1, rw2, rb2, ew1, eb1, ew2, eb2, ew3, eb3, out):
    with ExitStack() as top:
        def sb(name, shape, dt=F32, ctx=top):
            return ctx.enter_context(nc.sbuf_tensor(name, shape, dt))

        def pb(name, shape, ctx):
            return ctx.enter_context(nc.psum_tensor(name, shape, F32))

        def sem(name, ctx):
            return ctx.enter_context(nc.semaphore(name))

        table = [nc.dram_tensor(f"table{l}", (NP, ROW), F32).ap() for l in range(2)]
        conv = nc.dram_tensor("conv", (NP, F), F32).ap()

        ident = sb("ident", [P, P])
        acc = sb("acc", [P, 2, NP])
        sep = sb("sep", [P, NG, P + 1], BF16)
        same = sb("same", [P, NG, P + 1], BF16)
        ends = sb("ends", [P, NG, 2, 2])
        begins = sb("begins", [P, L + 1], BF16)
        ends_sep = sb("ends_sep", [P, L + 1], BF16)
        ends_same = sb("ends_same", [P, L + 1], BF16)
        parts = sb("parts", [P, T, 2, 2])
        src_sb = sb("src_sb", [P, T], I32)
        rel = sb("rel", [P, T])
        islast = sb("islast", [P, T])
        first_sb = sb("first_sb", [1, T], I32)
        row_iota = sb("row_iota", [P, P])
        fix_rows = sb("fix_rows", [P, NFIX], I32)
        hsel = sb("hsel", [P, 2, P])
        wext = sb("wext", [P, 2, 2, ROW])
        wedge = sb("wedge", [P, 2, H, H])
        gbias = sb("gbias", [P, 2, 2])
        wq = sb("wq", [P, 2, F])
        bq = sb("bq", [P, F])
        vw = sb("vw", [P, 2, F])
        bvw = sb("bvw", [P, F])
        kvw = sb("kvw", [P, 2, F])
        cst = sb("cst", [P, 4])

        prepare(nc, sb, pb, sem, locals())
        blocks(nc, sb, pb, sem, locals())
        for layer in range(2):
            edges(nc, sb, pb, sem, locals())
            join(nc, sb, pb, sem, locals())
        last(nc, sb, pb, sem, locals())


def prepare(nc, sb, pb, sem, v):
    ident, sep, same = v["ident"], v["sep"], v["same"]
    begins, ends_sep, ends_same, fix_rows = v["begins"], v["ends_sep"], v["ends_same"], v["fix_rows"]
    src_sb, rel, islast, first_sb = v["src_sb"], v["rel"], v["islast"], v["first_sb"]
    row_iota, hsel = v["row_iota"], v["hsel"]
    wext, wedge, gbias = v["wext"], v["wedge"], v["gbias"]
    wq, bq, vw, bvw, cst = v["wq"], v["bq"], v["vw"], v["bvw"], v["cst"]
    with ExitStack() as ctx:
        def tmp(name, shape, dt=F32):
            return sb(name, shape, dt, ctx)

        dst_sb = tmp("dst_sb", [P, T], I32)
        first_b = tmp("first_b", [P, T], I32)
        last_b = tmp("last_b", [P, T], I32)
        dg = tmp("dg", [P, NG, P], I32)
        pcol = tmp("pcol", [P, 1], I32)
        bits = tmp("bits", [P, 3], I32)
        bitsf = tmp("bitsf", [P, 4])
        irow = tmp("irow", [P, P], I32)
        ihead = tmp("ihead", [P, 2, P], I32)
        headf = tmp("headf", [P, 2, P])
        att = tmp("att", [P, 6, F])
        we = tmp("we", [P, 2, F])
        prod = tmp("prod", [P, 2, F])
        we_h = tmp("we_h", [P, 2, H])
        bmask = tmp("bmask", [P, H])
        means = tmp("means", [P, 4])
        wv = tmp("wv", [P, 2, F])
        wvT = tmp("wvT", [P, 2, F])
        wo = tmp("wo", [P, 2, F])
        bv = tmp("bv", [P, 2])
        bvb = tmp("bvb", [P, 2, P])
        ones = tmp("ones", [P, P])
        bo = tmp("bo", [P, F])
        tp = pb("prep_t", [P, 512], ctx)
        mm0 = pb("prep_m0", [P, 512], ctx)
        mm1 = pb("prep_m1", [P, 512], ctx)
        s_in = sem("prep_in", ctx)
        s_iota = sem("prep_iota", ctx)
        s_bits = sem("prep_bits", ctx)
        s_ready = sem("prep_ready", ctx)
        s_t = sem("prep_transposed", ctx)
        s_tc = sem("prep_copied", ctx)
        s_mm = sem("prep_product", ctx)
        block = ctx.enter_context(nc.Block())
        loads = []

        def load(to, of):
            loads.append((to, of))

        load(dst_sb[:], v["dst_t"])
        load(src_sb[:], v["src_t"])
        load(first_b[:], v["first_row"].broadcast_to((P, T)))
        load(last_b[:], v["last_row"].broadcast_to((P, T)))
        load(first_sb[:], v["first_row"])
        for b in range(NFIX):
            n = min(P, T - b * P)
            load(fix_rows[0:n, b:b + 1], v["first_row"][:, b * P:b * P + n].rearrange("a p -> p a"))
        for k in range(GT):
            load(dg[H * k:H * k + H], v["dst_g"][:, k, :].unsqueeze(0).broadcast_to((H, NG, P)))
        for l in range(2):
            W, a_s, a_d, W_e, a_e = ((v[f"{n}{l + 1}"]) for n in ("W", "as", "ad", "We", "ae"))
            load(wext[:, :, l, 0:F], W.rearrange("(a p) f -> p a f", p=P))
            for j, a in enumerate((a_s, a_d, a_e)):
                load(att[:, 3 * l + j, :], a.rearrange("(a h) c -> a (h c)", a=1).broadcast_to((P, F)))
            for b in range(H):
                load(we[D_EDGE * b:D_EDGE * b + D_EDGE, l, :], W_e)
            for a in range(2):
                load(gbias[:, l, a:a + 1], v[f"b{l + 1}"].rearrange("(a p b) -> a p b", p=P, b=1)[a])
        Wqkv, bqkv = v["Wqkv"], v["bqkv"].rearrange("(a f) -> a f", a=1)
        load(wq[:], Wqkv[:, 0:F].rearrange("(a p) f -> p a f", p=P))
        load(bq[:], bqkv[:, 0:F].broadcast_to((P, F)))
        load(wv[:], Wqkv[:, 2 * F:3 * F].rearrange("(a p) f -> p a f", p=P))
        load(wo[:], v["Wout"].rearrange("(a p) f -> p a f", p=P))
        load(bo[:], v["bout"].rearrange("(a f) -> a f", a=1).broadcast_to((P, F)))
        for a in range(2):
            load(bv[:, a:a + 1], v["bqkv"].rearrange("(a p b) -> a p b", p=P, b=1)[4 + a])

        @block.sync
        def _(sp):
            for to, of in loads:
                sp.dma_start(to, of).then_inc(s_in, 16)

        @block.gpsimd
        def _(pool):
            nc.gpsimd.iota(pcol[:], pattern=[[0, 1]], base=0, channel_multiplier=1).then_inc(s_iota, 1)
            nc.gpsimd.iota(irow[:], pattern=[[1, P]], base=0, channel_multiplier=0).then_inc(s_iota, 1)
            nc.gpsimd.iota(ihead[:].rearrange("p a (h c) -> p a h c", c=C), pattern=[[4, 2], [1, 4], [0, C]],
                           base=0, channel_multiplier=0).then_inc(s_iota, 1)
            nc.gpsimd.memset(cst[:, 0:1], -0.5)
            nc.gpsimd.memset(cst[:, 1:2], 0.5)
            nc.gpsimd.memset(cst[:, 2:4], 0.0)
            nc.gpsimd.memset(ones[:], 1.0).then_inc(s_iota, 1)

        @block.vector
        def _(vec):
            vec.wait_ge(s_iota, 4)
            nc.vector.tensor_single_scalar(bits[:, 0:1], pcol[:], 3, ALU.logical_shift_right)
            nc.vector.tensor_single_scalar(bits[:, 1:2], pcol[:], 7, ALU.bitwise_and)
            nc.vector.tensor_single_scalar(bits[:, 2:3], pcol[:], 4, ALU.logical_shift_right)
            nc.vector.tensor_copy(bitsf[:, 3:4], pcol[:])
            nc.vector.tensor_copy(row_iota[:], irow[:])
            nc.vector.tensor_copy(headf[:], ihead[:])
            vec.drain()
            nc.vector.tensor_copy(bitsf[:, 0:3], bits[:])
            vec.drain()
            nc.vector.tensor_scalar(ident[:], row_iota[:], bitsf[:, 3:4], None, ALU.is_equal)
            nc.vector.tensor_scalar(bmask[:], row_iota[:, 0:H], bitsf[:, 2:3], None, ALU.is_equal)
            nc.vector.tensor_scalar(hsel[:], headf[:], bitsf[:, 1:2], None, ALU.is_equal)
            vec.wait_ge(s_in, 16 * len(loads))
            nc.vector.tensor_tensor(rel[:], dst_sb[:], first_b[:], ALU.subtract)
            nc.vector.tensor_tensor(islast[:], dst_sb[:], last_b[:], ALU.is_equal)
            nc.vector.memset(same[:], 0.0)
            nc.vector.memset(v["acc"][:, :, N:NP], 0.0)
            nc.vector.memset(begins[:], 1.0)
            vec.drain()
            nc.vector.tensor_tensor(begins[:, 1:L:2], first_b[:], last_b[:], ALU.not_equal)
            nc.vector.tensor_tensor(begins[:, 2:L:2], first_b[:, 1:T], last_b[:, 0:T - 1], ALU.not_equal)
            nc.vector.tensor_tensor(same[:, :, 1:P], dg[:, :, 1:P], dg[:, :, 0:P - 1], ALU.is_equal)
            vec.drain()
            nc.vector.tensor_scalar(sep[:], same[:], BIG, -BIG, ALU.mult, ALU.add)
            nc.vector.tensor_single_scalar(ends_sep[:], begins[:], -BIG, ALU.mult)
            nc.vector.tensor_scalar(ends_same[:], begins[:], -1.0, 1.0, ALU.mult, ALU.add)
            for l in range(2):
                for j, to in ((0, wext[:, :, l, F:F + H]), (1, wext[:, :, l, F + H:ROW])):
                    nc.vector.tensor_tensor(prod[:], wext[:, :, l, 0:F],
                                            att[:, 3 * l + j, :].unsqueeze(1).broadcast_to((P, 2, F)), ALU.mult)
                    vec.drain()
                    nc.vector.tensor_reduce(to, prod[:].rearrange("p a (h c) -> p a h c", c=C), AX.X, ALU.add)
                    vec.drain()
                nc.vector.tensor_tensor(prod[:, 0, :], we[:, l, :], att[:, 3 * l + 2, :], ALU.mult)
                vec.drain()
                nc.vector.tensor_reduce(we_h[:, l, :], prod[:, 0, :].rearrange("p (h c) -> p h c", c=C), AX.X, ALU.add)
                vec.drain()
                nc.vector.tensor_tensor(wedge[:, l], we_h[:, l, :].unsqueeze(1).broadcast_to((P, H, H)),
                                        bmask[:].unsqueeze(2).broadcast_to((P, H, H)), ALU.mult)
            nc.vector.tensor_reduce(means[:, 0:2], wq[:], AX.X, ALU.add)
            nc.vector.tensor_reduce(means[:, 2:3], bq[:], AX.X, ALU.add)
            vec.drain()
            nc.vector.tensor_single_scalar(means[:, 0:3], means[:, 0:3], 1.0 / F, ALU.mult)
            vec.drain()
            for a in range(2):
                nc.vector.tensor_scalar(wq[:, a, :], wq[:, a, :], means[:, a:a + 1], None, ALU.subtract)
            nc.vector.tensor_scalar(bq[:], bq[:], means[:, 2:3], None, ALU.subtract)
            for a in range(2):
                nc.vector.tensor_scalar(bvb[:, a, :], ones[:], bv[:, a:a + 1], None, ALU.mult)
            nc.vector.memset(means[:, 3:4], 0.0).then_inc(s_ready, 1)
            vec.wait_ge(s_t, 1)
            nc.vector.tensor_copy(wvT[:], tp[:].rearrange("p (b f) -> p b f", b=2)).then_inc(s_tc, 1)
            vec.wait_ge(s_mm, 1)
            nc.vector.tensor_copy(vw[:], mm0[:].rearrange("p (b f) -> p b f", b=2))
            nc.vector.tensor_tensor(bvw[:], mm1[:, 0:F], bo[:], ALU.add)

        @block.tensor
        def _(pe):
            pe.wait_ge(s_ready, 1)
            for b in range(2):
                for a in range(2):
                    last = nc.tensor.transpose(tp[:, b * F + a * P:b * F + a * P + P], wv[:, a, b * P:b * P + P], ident[:])
            last.then_inc(s_t, 1)
            pe.wait_ge(s_tc, 1)
            for a in range(2):
                for b in range(2):
                    nc.tensor.matmul(mm0[:, a * F:a * F + F], wvT[:, b, a * P:a * P + P], wo[:, b, :],
                                     start=(b == 0), stop=(b == 1))
            for b in range(2):
                last = nc.tensor.matmul(mm1[:, 0:F], bvb[:, b, :], wo[:, b, :], start=(b == 0), stop=(b == 1))
            last.then_inc(s_mm, 1)


def blocks(nc, sb, pb, sem, v):
    ident, wext, cst = v["ident"], v["wext"], v["cst"]
    vw, kvw, x = v["vw"], v["kvw"], v["x"]
    table = v["table"][0]
    with ExitStack() as ctx:
        def tmp(name, shape, dt=F32):
            return sb(name, shape, dt, ctx)

        wk = tmp("wk", [P, 2, F])
        bk = tmp("bk", [P, F])
        kmean = tmp("kmean", [P, 3])
        wvo = tmp("wvo", [P, 2, F])
        bvwk = tmp("bvwk", [1, F])
        bv2 = tmp("bv2", [P, 2])
        xb = tmp("xb", [P, 2, 2, F])
        xn = tmp("xn", [P, 2, 2, F + 1])
        stats = tmp("stats", [P, 2, 6])
        mv = tmp("mv", [P, 2, 2])
        rstd = tmp("rstd", [P, 2])
        epsb = tmp("epsb", [P, 2])
        xnT = tmp("xnT", [P, 2, 2 * P])
        hT = tmp("hT", [P, 2, 2 * P])
        row = tmp("row", [P, 2, 2, ROW])
        kc = tmp("kc", [P, 2, F])
        k2 = tmp("k2", [P, 2, F])
        k2r = tmp("k2r", [P, 2, 2, F])
        k4 = tmp("k4", [P, 2, 2, F])
        k2s = tmp("k2s", [P, 2])
        inv = tmp("inv", [P, 2])
        nmask = tmp("nmask", [P, NB])
        inode = tmp("inode", [P, NB], I32)
        ones = tmp("ones_b", [P, 1])
        norm = tmp("norm", [P, 2])
        kxs = tmp("kxs", [P, 2, F + 1])
        kxT = tmp("kxT", [P, 2, F])
        ksT = tmp("ksT", [1, F])
        turn = pb("turn", [P, 512], ctx)
        ps_row = [pb(f"ps_row{b}", [P, 512], ctx) for b in range(2)]
        ps_k = pb("ps_k", [P, 512], ctx)
        ps_kx = [pb(f"ps_kx{a}", [P, 512], ctx) for a in range(2)]
        ps_end = pb("ps_end", [P, 512], ctx)
        names = ("w_in", "x0", "x1", "mv", "rstd", "xn", "turned", "copied", "rectified", "row", "rowc", "k", "kc", "k2", "k2r",
                 "kx", "out0", "out1", "setup", "fin", "fins", "finp", "mask")
        s = {n: sem("blk_" + n, ctx) for n in names}
        block = ctx.enter_context(nc.Block())

        @block.sync
        def _(sp):
            sp.dma_start(wk[:], v["Wqkv"][:, F:2 * F].rearrange("(a p) f -> p a f", p=P)).then_inc(s["w_in"], 16)
            sp.dma_start(bk[:], v["bqkv"].rearrange("(a f) -> a f", a=1)[:, F:2 * F].broadcast_to((P, F))).then_inc(s["w_in"], 16)
            for a in range(2):
                sp.dma_start(bv2[:, a:a + 1], v["bqkv"].rearrange("(a p b) -> a p b", p=P, b=1)[4 + a]).then_inc(s["w_in"], 16)
            sp.dma_start(wvo[:], v["Wout"].rearrange("(a p) f -> p a f", p=P)).then_inc(s["w_in"], 16)

            def fetch(n, q):
                sp.wait_ge(s["xn"], n + 1)
                sp.dma_start(xb[:, q], x[bass.ds(n * CH, CH), :].rearrange("(b p) f -> p b f", p=P)).then_inc(s[f"x{q}"], 16)

            with sp.Fori(0, NCH // 2) as i:
                fetch(2 * i, 0)
                fetch(2 * i + 1, 1)
            fetch(NCH - 1, 0)

        @block.gpsimd
        def _(pool):
            nc.gpsimd.iota(inode[:], pattern=[[P, NB]], base=0, channel_multiplier=1).then_inc(s["mask"], 1)
            with pool.Fori(0, NCH) as n:
                pool.wait_ge(s["mv"], n + 1)
                nc.gpsimd.tensor_tensor(rstd[:], epsb[:], cst[:, 0:1].broadcast_to((P, 2)), ALU.pow).then_inc(s["rstd"], 1)
            pool.wait_ge(s["fin"], 1)
            nc.gpsimd.tensor_tensor(inv[:], norm[:], cst[:, 1:2].broadcast_to((P, 2)), ALU.pow).then_inc(s["finp"], 1)

        @block.vector
        def _(vec):
            vec.sem_inc(s["xn"], 2)
            nc.vector.memset(ones[:], 1.0)
            nc.vector.memset(xn[:, :, :, F:F + 1], 1.0)
            vec.wait_ge(s["mask"], 1)
            nc.vector.tensor_single_scalar(nmask[:], inode[:], N, ALU.is_lt)
            vec.wait_ge(s["w_in"], 80)
            nc.vector.tensor_reduce(kmean[:, 0:2], wk[:], AX.X, ALU.add)
            nc.vector.tensor_reduce(kmean[:, 2:3], bk[:], AX.X, ALU.add)
            vec.drain()
            nc.vector.tensor_single_scalar(kmean[:], kmean[:], 1.0 / F, ALU.mult)
            vec.drain()
            for a in range(2):
                nc.vector.tensor_scalar(wk[:, a, :], wk[:, a, :], kmean[:, a:a + 1], None, ALU.subtract)
            nc.vector.tensor_scalar(bk[:], bk[:], kmean[:, 2:3], None, ALU.subtract).then_inc(s["setup"], 1)
            vec.wait_ge(s["setup"], 1)

            def moments(q, h):
                vec.wait_ge(s[f"x{q}"], 16 * h + 16)
                for b in range(2):
                    nc.vector.bn_stats(stats[:, b, :], xb[:, q, b, :])
                vec.drain()
                for b in range(2):
                    nc.vector.bn_aggr(mv[:, b, :], stats[:, b, :])
                vec.drain()
                nc.vector.tensor_single_scalar(epsb[:], mv[:, :, 1], LN_EPS, ALU.add).then_inc(s["mv"], 1)

            def normalise(n, q):
                vec.wait_ge(s["rstd"], n + 1)
                vec.wait_ge(s["kx"], n + 1)
                for b in range(2):
                    op = nc.vector.tensor_scalar(xn[:, q, b, 0:F], xb[:, q, b, :], mv[:, b, 0:1], rstd[:, b:b + 1],
                                                 ALU.subtract, ALU.mult)
                op.then_inc(s["xn"], 1)

            def centre(n):
                vec.wait_ge(s["k"], n + 1)
                nc.vector.tensor_tensor(kc[:], ps_k[:].rearrange("p (b f) -> p b f", b=2),
                                        bk[:].unsqueeze(1).broadcast_to((P, 2, F)), ALU.add).then_inc(s["kc"], 1)

            def keys(n, q):
                vec.wait_ge(s["k2"], n + 1)
                nc.vector.tensor_single_scalar(inv[:], k2s[:], EPS_DIV, ALU.add)
                vec.drain()
                nc.vector.reciprocal(inv[:], inv[:])
                vec.drain()
                nc.vector.tensor_tensor(inv[:], inv[:], nmask[:, bass.ds(2 * n, 2)], ALU.mult)
                vec.drain()
                vec.wait_ge(s["kx"], n + 1)
                for b in range(2):
                    nc.vector.tensor_scalar(k2r[:, q, b, :], k2[:, b, :], inv[:, b:b + 1], None, ALU.mult)
                vec.drain()
                nc.vector.tensor_tensor(k4[:, q], k2r[:, q], k2r[:, q], ALU.mult).then_inc(s["k2r"], 1)

            def step(n, q, h, more=True):
                centre(n)
                if more:
                    moments(1 - q, h + q)
                keys(n, q)
                if more:
                    normalise(n + 1, 1 - q)

            moments(0, 0)
            normalise(0, 0)
            step(0, 0, 0)
            with vec.Fori(0, NCH // 2 - 1) as i:
                step(2 * i + 1, 1, i)
                step(2 * i + 2, 0, i + 1)
            step(NCH - 2, 1, NCH // 2 - 1)
            step(NCH - 1, 0, NCH // 2, more=False)
            vec.wait_ge(s["kx"], NCH + 2)
            for a in range(2):
                nc.vector.tensor_copy(norm[:, a:a + 1], ps_kx[a][:, F + 1:F + 2])
            vec.drain()
            nc.vector.sem_inc(s["fin"], 1)
            vec.wait_ge(s["finp"], 1)
            nc.vector.tensor_single_scalar(inv[:], inv[:], EPS_NORM, ALU.max)
            vec.drain()
            nc.vector.reciprocal(inv[:], inv[:])
            vec.drain()
            nc.vector.tensor_single_scalar(inv[:], inv[:], float(N) ** -0.5, ALU.mult)
            vec.drain()
            for a in range(2):
                op = nc.vector.tensor_scalar(kxs[:, a, :], ps_kx[a][:, 0:F + 1], inv[:, a:a + 1], None, ALU.mult)
            op.then_inc(s["fin"], 1)
            vec.wait_ge(s["fins"], 1)
            nc.vector.tensor_copy(kxT[:], ps_end[:].rearrange("p (b c) -> p b c", b=2))
            nc.vector.tensor_copy(ksT[:], ps_k[0:1, 0:F])
            nc.vector.tensor_copy(bvwk[:], ps_row[0][0:1, 0:F]).then_inc(s["fin"], 1)
            vec.wait_ge(s["fins"], 2)
            nc.vector.tensor_copy(kvw[:], turn[:].rearrange("p (a f) -> p a f", a=2))

        @block.scalar
        def _(act):
            def copies(n):
                act.wait_ge(s["turned"], n + 1)
                act.wait_ge(s["row"], n + 1)
                view = turn[:].rearrange("p (a n) -> p a n", a=2)
                nc.scalar.activation(xnT[:], view, ACT.Copy).then_inc(s["copied"], 1)
                nc.scalar.activation(hT[:], view, ACT.Relu).then_inc(s["rectified"], 1)

            def squares(n):
                act.wait_ge(s["kc"], n + 1)
                act.wait_ge(s["k2r"], n + 1)
                for b in range(2):
                    op = nc.scalar.activation(k2[:, b, :], kc[:, b, :], ACT.Square, accum_out=k2s[:, b:b + 1])
                op.then_inc(s["k2"], 1)

            def rows(n, q, h):
                act.wait_ge(s["row"], n + 2)
                if not isinstance(h, int) or h > 0:
                    act.wait_ge(s[f"out{q}"], 16 * h)
                for b in range(2):
                    op = nc.scalar.activation(row[:, q, b, :], ps_row[b][:, 0:ROW], ACT.Copy)
                op.then_inc(s["rowc"], 1)
                act.wait_ge(s["rowc"], n + 1)
                act.dma_start(table[bass.ds(n * CH, CH), :].rearrange("(b p) f -> p b f", p=P), row[:, q]
                              ).then_inc(s[f"out{q}"], 16)

            def step(n, q, h, more=True):
                squares(n)
                if more:
                    copies(n + 1)
                rows(n, q, h)

            act.sem_inc(s["k2r"], 1)
            copies(0)
            step(0, 0, 0)
            step(1, 1, 0)
            step(2, 0, 1)
            with act.Fori(1, NCH // 2 - 1) as i:
                step(2 * i + 1, 1, i)
                step(2 * i + 2, 0, i + 1)
            step(NCH - 2, 1, NCH // 2 - 1)
            step(NCH - 1, 0, NCH // 2, more=False)
            act.wait_ge(s["out0"], 16 * (NCH // 2 + 1))
            act.wait_ge(s["out1"], 16 * (NCH // 2))

        @block.tensor
        def _(pe):
            def turns(n, q):
                pe.wait_ge(s["xn"], n + 3)
                if not isinstance(n, int) or n > 0:
                    pe.wait_ge(s["rectified"], n)
                for a in range(2):
                    for b in range(2):
                        op = nc.tensor.transpose(turn[:, a * CH + b * P:a * CH + b * P + P], xn[:, q, b, a * P:a * P + P], ident[:])
                op.then_inc(s["turned"], 1)

            def key_products(n):
                pe.wait_ge(s["copied"], n + 1)
                if not isinstance(n, int) or n > 0:
                    pe.wait_ge(s["kc"], n)
                for b in range(2):
                    for a in range(2):
                        op = nc.tensor.matmul(ps_k[:, b * F:b * F + F], xnT[:, a, b * P:b * P + P], wk[:, a, :],
                                              start=(a == 0), stop=(a == 1))
                op.then_inc(s["k"], 1)

            def row_products(n):
                pe.wait_ge(s["rectified"], n + 1)
                if not isinstance(n, int) or n > 0:
                    pe.wait_ge(s["rowc"], n)
                for b in range(2):
                    for a in range(2):
                        op = nc.tensor.matmul(ps_row[b][:, 0:ROW], hT[:, a, b * P:b * P + P], wext[:, a, 0, :],
                                              start=(a == 0), stop=(a == 1))
                op.then_inc(s["row"], 1)

            def sums(n, q, first=False, end=False):
                pe.wait_ge(s["k2r"], n + 2)
                for b in range(2):
                    for a in range(2):
                        nc.tensor.matmul(ps_kx[a][:, 0:F + 1], k2r[:, q, b, a * P:a * P + P], xn[:, q, b, :],
                                         start=first and b == 0, stop=end and b == 1, skip_group_check=True)
                        op = nc.tensor.matmul(ps_kx[a][:, F + 1:F + 2], k4[:, q, b, a * P:a * P + P], ones[:], start=False,
                                              stop=end and b == 1, skip_group_check=True)
                op.then_inc(s["kx"], 1)

            def step(n, q, more=True, second=False):
                key_products(n)
                if not isinstance(n, int) or n > 0:
                    sums(n - 1, 1 - q, first=second)
                row_products(n)
                if more:
                    turns(n + 1, 1 - q)

            pe.sem_inc(s["kx"], 2)
            pe.sem_inc(s["row"], 1)
            pe.wait_ge(s["setup"], 1)
            turns(0, 0)
            step(0, 0)
            step(1, 1, second=True)
            step(2, 0)
            with pe.Fori(1, NCH // 2 - 1) as i:
                step(2 * i + 1, 1)
                step(2 * i + 2, 0)
            step(NCH - 2, 1)
            step(NCH - 1, 0, more=False)
            sums(NCH - 1, 0, end=True)
            pe.wait_ge(s["fin"], 2)
            pe.wait_ge(s["rowc"], NCH)
            for b in range(2):
                for a in range(2):
                    nc.tensor.transpose(ps_end[:, b * F + a * P:b * F + a * P + P], kxs[:, a, b * P:b * P + P], ident[:])
            for a in range(2):
                nc.tensor.transpose(ps_k[0:1, a * P:a * P + P], kxs[:, a, F:F + 1], ident[:])
            for b in range(2):
                op = nc.tensor.matmul(ps_row[0][0:1, 0:F], bv2[:, b:b + 1], wvo[:, b, :], start=(b == 0), stop=(b == 1))
            op.then_inc(s["fins"], 1)
            pe.wait_ge(s["fin"], 3)
            for a in range(2):
                for b in range(2):
                    nc.tensor.matmul(turn[:, a * F:a * F + F], kxT[:, b, a * P:a * P + P], vw[:, b, :],
                                     start=(b == 0), stop=False)
                op = nc.tensor.matmul(turn[:, a * F:a * F + F], ksT[:, a * P:a * P + P], bvwk[:], start=False, stop=True)
            op.then_inc(s["fins"], 1)


def edges(nc, sb, pb, sem, v):
    layer = v["layer"]
    ident, acc, sep, same, ends = v["ident"], v["acc"], v["sep"], v["same"], v["ends"]
    parts, src_sb, rel, islast = v["parts"], v["src_sb"], v["rel"], v["islast"]
    first_sb, row_iota, wedge = v["first_sb"], v["row_iota"], v["wedge"]
    table = v["table"][layer]
    with ExitStack() as ctx:
        def tmp(name, shape, dt=F32):
            return sb(f"e{layer}_{name}", shape, dt, ctx)

        idx = tmp("idx", [P, 2, GT], I32)
        rows = [tmp(f"rows{q}", [P, GT, ROW]) for q in range(2)]
        win = tmp("win", [P, 2, GT, H])
        eattr = tmp("eattr", [P, 2, 2, P])
        hot = tmp("hot", [P, 2, GT, WIN])
        hotT = tmp("hotT", [P, 4, P])
        sepg = tmp("sepg", [P, P + 1], BF16)
        al = tmp("al", [P, P])
        lr = tmp("lr", [P, P])
        peak = tmp("peak", [P, P])
        seg = tmp("seg", [P, P])
        less = tmp("less", [P, P])
        ex = tmp("ex", [P, P])
        run = tmp("run", [P, P])
        tot = tmp("tot", [P, P])
        prob = tmp("prob", [P, P])
        msg = tmp("msg", [P, 4, F])
        ps_al = pb(f"e{layer}_ps_al", [P, 512], ctx)
        ps_pr = [pb(f"e{layer}_ps_pr{q}", [P, 512], ctx) for q in range(2)]
        ps_hot = pb(f"e{layer}_ps_hot", [P, 512], ctx)
        ps_sum = [pb(f"e{layer}_ps_sum{q}", [P, 2, F], ctx) for q in range(4)]
        names = ("idx", "rows0", "rows1", "win0", "win1", "eattr0", "eattr1", "hot", "hotT", "hotTc",
                 "scores", "leaky", "turned", "less", "ex", "prob", "probT", "msg", "sum", "window", "taken")
        s = {n: sem(f"e{layer}_{n}", ctx) for n in names}
        s_on = sem(f"e{layer}_on", ctx)
        block = ctx.enter_context(nc.Block())

        def plain(eng):
            eng.wait_ge(s_on, 1)


        @block.sync
        def _(sp):
            first = [sp.alloc_register(f"e{layer}_sp{k}") for k in range(GT)]

            def fetch(g, q, h):
                sp.wait_ge(s["scores"], g + 1)
                plain(sp)
                sp.reg_load(first, first_sb[0:1, bass.ds(g * GT, GT)])
                for k in range(GT):
                    at = sp.snap(first[k], min_val=0, max_val=N)
                    sp.dma_start(win[:, q, k, :], table[bass.ds(at, P), F + H:ROW]).then_inc(s[f"win{q}"], 16)
                sp.dma_start(eattr[:, q], v["edge_b"][:, bass.ds(g * 2, 2), :]).then_inc(s[f"eattr{q}"], 16)

            with sp.Fori(0, NG // 2) as i:
                for q in range(2):
                    fetch(2 * i + q, q, i)

        @block.gpsimd
        def _(pool):
            pool.sem_inc(s_on, 1)

            def gather(g, q):
                pool.wait_ge(s["msg"], 16 * g + 1)
                plain(pool)
                if True:
                    nc.gpsimd.tensor_copy(idx[:, q, :], src_sb[:, bass.ds(g * GT, GT)]).then_inc(s["idx"], 1)
                for k in range(GT):
                    pool.wait_ge(s["msg"], 16 * g + k + 1)
                    if k == 0:
                        pool.wait_ge(s["idx"], g + 1)
                    pool.nop(nofuse=True)
                    nc.gpsimd.indirect_dma_start(
                        out=rows[q][:, k, :], out_offset=None, in_=table,
                        in_offset=bass.IndirectOffsetOnAxis(ap=idx[:, q, k:k + 1], axis=0)).then_inc(s[f"rows{q}"], 16)

            with pool.Fori(0, NG // 2) as i:
                for q in range(2):
                    gather(2 * i + q, q)

        @block.vector
        def _(vec):
            def one_hots(g, q, r):
                if not isinstance(g, int) or g > 1:
                    vec.wait_ge(s["sum"], 16 * g + 4 * r - 12)
                plain(vec)
                nc.vector.tensor_copy(hot[:, q, 4 * r:4 * r + 4, P:P + 1],
                                      islast[:, bass.ds(g * GT + 4 * r, 4)].unsqueeze(2))
                nc.vector.tensor_tensor(hot[:, q, 4 * r:4 * r + 4, 0:P], row_iota[:].unsqueeze(1).broadcast_to((P, 4, P)),
                                        rel[:, bass.ds(g * GT + 4 * r, 4)].unsqueeze(2).broadcast_to((P, 4, P)),
                                        ALU.is_equal).then_inc(s["hot"], 1)

            def message(g, q, k):
                if k == 0:
                    vec.wait_ge(s["probT"], g + 1)
                vec.wait_ge(s["sum"], 16 * g + 16 + k - 3)
                nc.vector.tensor_tensor(
                    msg[:, k % 4, :].rearrange("p (h c) -> p h c", c=C),
                    rows[q][:, k, 0:F].rearrange("p (h c) -> p h c", c=C),
                    ps_pr[q][:, H * k:H * k + H].unsqueeze(2).broadcast_to((P, H, C)), ALU.mult).then_inc(s["msg"], 1)

            def leaky(g, q, i):
                vec.wait_ge(s["scores"], g + 3)
                vec.wait_ge(s[f"rows{q}"], 256 * i + 256)
                nc.vector.tensor_tensor(al[:].rearrange("p (k h) -> p k h", h=H),
                                        ps_al[:, 0:P].rearrange("p (k h) -> p k h", h=H), rows[q][:, :, F:F + H], ALU.add)
                vec.drain()
                nc.vector.scalar_tensor_tensor(lr[:], al[:], 0.2, al[:], ALU.mult, ALU.max).then_inc(s["leaky"], 1)

            def highest(g):
                nc.vector.tensor_copy(sepg[:], sep[:, bass.ds(g, 1), :].rearrange("p a b -> p (a b)"))
                vec.drain()
                vec.wait_ge(s["turned"], g + 1)
                nc.vector.tensor_tensor_scan(peak[:], sepg[:, 0:P], ps_al[:, P:2 * P], -BIG, ALU.add, ALU.max)
                vec.drain()

            def less_highest(g):
                nc.vector.tensor_tensor_scan(seg[:, ::-1], sepg[:, 1:P + 1][:, ::-1], peak[:, ::-1], -BIG, ALU.add, ALU.max)
                vec.drain()
                nc.vector.tensor_tensor(less[:], ps_al[:, P:2 * P], seg[:], ALU.subtract).then_inc(s["less"], 1)
                nc.vector.tensor_copy(ends[:, bass.ds(g, 1), :, 0:1].rearrange("p a b c -> p (a b c)"), seg[:, 0:P:P - 1])

            def running(g):
                vec.wait_ge(s["ex"], g + 2)
                nc.vector.tensor_tensor_scan(run[:], same[:, bass.ds(g, 1), 0:P].rearrange("p a b -> p (a b)"), ex[:],
                                             0.0, ALU.mult, ALU.add)
                vec.drain()

            def whole(g):
                nc.vector.tensor_tensor_scan(tot[:, ::-1], sepg[:, 1:P + 1][:, ::-1], run[:, ::-1], -BIG, ALU.add, ALU.max)
                vec.drain()
                nc.vector.tensor_copy(ends[:, bass.ds(g, 1), :, 1:2].rearrange("p a b c -> p (a b c)"), tot[:, 0:P:P - 1])
                nc.vector.tensor_single_scalar(run[:], tot[:], 1e-16, ALU.add)
                vec.drain()

            def inverse():
                nc.vector.reciprocal(seg[:], run[:])
                vec.drain()

            def probability(g):
                if not isinstance(g, int) or g > 0:
                    vec.wait_ge(s["probT"], g)
                nc.vector.tensor_tensor(prob[:], ex[:], seg[:], ALU.mult).then_inc(s["prob"], 1)

            def step(g, q, i, softmax=True, ahead=True):
                n, p = g + 1, 1 - q
                for k in range(GT):
                    message(g, q, k)
                    if softmax and k == 1:
                        one_hots(n, p, 3)
                    if ahead and k == 5:
                        one_hots(g + 2, q, 0)
                    if softmax and k == 6:
                        leaky(n, p, i if p == 1 else i + 1)
                    if softmax and k == 7:
                        highest(n)
                    if softmax and k == 8:
                        less_highest(n)
                    if ahead and k == 9:
                        one_hots(g + 2, q, 1)
                    if softmax and k == 10:
                        running(n)
                    if softmax and k == 11:
                        whole(n)
                    if softmax and k == 12:
                        inverse()
                    if softmax and k == 13:
                        probability(n)
                    if ahead and k == 14:
                        one_hots(g + 2, q, 2)

            vec.sem_inc(s["msg"], 32)
            vec.wait_ge(s_on, 1)
            for r in range(4):
                one_hots(0, 0, r)
            for r in range(3):
                one_hots(1, 1, r)
            leaky(0, 0, 0)
            highest(0)
            less_highest(0)
            running(0)
            whole(0)
            inverse()
            probability(0)
            with vec.Fori(0, NG // 2 - 1) as i:
                step(2 * i, 0, i)
                step(2 * i + 1, 1, i)
            step(NG - 2, 0, NG // 2 - 1, ahead=False)
            step(NG - 1, 1, NG // 2 - 1, softmax=False, ahead=False)

        @block.scalar
        def _(act):
            first = [act.alloc_register(f"e{layer}_act{k}") for k in range(GT)]

            def hot_copy(g, r):
                act.wait_ge(s["hotT"], 4 * g + r + 1)
                nc.scalar.activation(hotT[:], ps_hot[:].rearrange("p (k e) -> p k e", k=4), ACT.Copy).then_inc(s["hotTc"], 1)

            def exps(g):
                act.wait_ge(s["less"], g + 1)
                nc.scalar.activation(ex[:], less[:], ACT.Exp).then_inc(s["ex"], 1)

            def window(g, k, at):
                act.wait_ge(s["window"], 16 * g + k + 1)
                act.wait_ge(s["sum"], 16 * g + 16 + k + 1)
                plain(act)
                nc.scalar.activation(acc[:, :, bass.ds(at[k], P)], ps_sum[k % 4][:, :, 0:P], ACT.Copy).then_inc(s["window"], 1)
                nc.scalar.activation(parts[:, bass.ds(g * GT + k, 1)].rearrange("p t a b -> p (t a) b"),
                                     ps_sum[k % 4][:, :, 0:P + 1:P], ACT.Copy).then_inc(s["taken"], 1)

            def step(g, q, softmax=True, ahead=True):
                act.reg_load(first, first_sb[0:1, bass.ds(g * GT, GT)])
                at = [act.snap(first[k], min_val=0, max_val=N) for k in range(GT)]
                for k in range(GT):
                    window(g, k, at)
                    if softmax and k == 1:
                        hot_copy(g + 1, 3)
                    if softmax and k == 8:
                        exps(g + 1)
                    if ahead and k in (5, 9, 14):
                        hot_copy(g + 2, {5: 0, 9: 1, 14: 2}[k])

            act.sem_inc(s["window"], 1)
            act.sem_inc(s["taken"], 4)
            act.sem_inc(s["ex"], 1)
            for r in range(4):
                hot_copy(0, r)
            exps(0)
            for r in range(3):
                hot_copy(1, r)
            with act.Fori(0, NG // 2 - 1) as i:
                step(2 * i, 0)
                step(2 * i + 1, 1)
            step(NG - 2, 0, ahead=False)
            step(NG - 1, 1, softmax=False, ahead=False)

        @block.tensor
        def _(pe):
            def turn_hot(g, q, r):
                pe.wait_ge(s["hot"], 4 * g + r + 1)
                for k in range(4):
                    op = nc.tensor.transpose(ps_hot[:, k * P:k * P + P], hot[:, q, 4 * r + k, 0:P], ident[:])
                op.then_inc(s["hotT"], 1)

            def scores(g, q, r, i):
                if r == 0:
                    if not isinstance(g, int) or g > 0:
                        pe.wait_ge(s["less"], g)
                    pe.wait_ge(s[f"win{q}"], 256 * i + 256)
                    pe.wait_ge(s[f"eattr{q}"], 16 * i + 16)
                    for a in range(2):
                        nc.tensor.matmul(ps_al[:, 64 * a:64 * a + 64], eattr[:, q, a, :],
                                         wedge[:, layer].rearrange("p b h -> p (b h)"), start=(a == 0), stop=False,
                                         skip_group_check=True)
                pe.wait_ge(s["hotTc"], 4 * g + r + 1)
                for k in range(4):
                    m = H * (4 * r + k)
                    op = nc.tensor.matmul(ps_al[:, m:m + H], hotT[:, k, :], win[:, q, 4 * r + k, :], start=False,
                                          stop=(r == 3 and k == 3), skip_group_check=True)
                if r == 3:
                    op.then_inc(s["scores"], 1)

            def turn_alpha(g):
                pe.wait_ge(s["leaky"], g + 1)
                nc.tensor.transpose(ps_al[:, P:2 * P], lr[:], ident[:]).then_inc(s["turned"], 1)

            def turn_prob(g, q):
                pe.wait_ge(s["prob"], g + 1)
                nc.tensor.transpose(ps_pr[q][:, 0:P], prob[:], ident[:]).then_inc(s["probT"], 1)

            def total(g, q, k):
                pe.wait_ge(s["msg"], 16 * g + 32 + k + 1)
                pe.wait_ge(s["taken"], 16 * g + k + 1)
                for a in range(2):
                    op = nc.tensor.matmul(ps_sum[k % 4][:, a, 0:WIN], msg[:, k % 4, a * P:a * P + P], hot[:, q, k, :],
                                          start=(a == 0), stop=True, skip_group_check=True)
                op.then_inc(s["sum"], 1)

            def step(g, q, i, softmax=True, ahead=True):
                n, p, m, j = g + 1, 1 - q, g + 2, i + 1
                for k in range(GT):
                    total(g, q, k)
                    if softmax and k == 1:
                        turn_hot(n, p, 3)
                    if softmax and k == 2:
                        scores(n, p, 3, None)
                    if softmax and k == 6:
                        turn_alpha(n)
                    if ahead and k in (9, 10, 15):
                        scores(m, q, {9: 0, 10: 1, 15: 2}[k], j)
                    if ahead and k in (5, 9, 14):
                        turn_hot(m, q, {5: 0, 9: 1, 14: 2}[k])
                    if softmax and k == 13:
                        turn_prob(n, p)

            def ahead_of_all(g, rounds):
                for r in range(rounds):
                    turn_hot(g, g, r)
                    scores(g, g, r, 0)

            pe.sem_inc(s["sum"], 16)
            pe.sem_inc(s["scores"], 2)
            ahead_of_all(0, 4)
            turn_alpha(0)
            turn_prob(0, 0)
            ahead_of_all(1, 3)
            with pe.Fori(0, NG // 2 - 1) as i:
                step(2 * i, 0, i)
                step(2 * i + 1, 1, i)
            step(NG - 2, 0, NG // 2 - 1, ahead=False)
            step(NG - 1, 1, NG // 2 - 1, softmax=False, ahead=False)


def join(nc, sb, pb, sem, v):
    layer, acc, ends, parts = v["layer"], v["acc"], v["ends"], v["parts"]
    ident, hsel, wext, gbias, fix_rows = v["ident"], v["hsel"], v["wext"], v["gbias"], v["fix_rows"]
    begins, sep, same = v["begins"], v["ends_sep"], v["ends_same"]
    result = v["table"][1] if layer == 0 else v["conv"]
    WIDTH = ROW if layer == 0 else F
    FUNC = ACT.Relu if layer == 0 else ACT.Identity
    Q = L // 4
    with ExitStack() as ctx:
        def tmp(name, shape, dt=F32):
            return sb(f"j{layer}_{name}", shape, dt, ctx)

        mx = tmp("mx", [H, L])
        sm = tmp("sm", [H, L])
        fwd = tmp("fwd", [H, L])
        top = tmp("top", [H, L])
        ex, weight = fwd, mx
        inv = tmp("inv", [H, T])
        a = tmp("a", [P, L])
        b = tmp("b", [P, L])
        total = tmp("total", [P, 2, T])
        hT = tmp("hT", [P, 2, 2, CH])
        fixT = tmp("fixT", [P, 2, T])
        row = tmp("row", [P, 2, 2, WIDTH])
        fix = tmp("fix", [P, NFIX, WIDTH])
        ps = [pb(f"j{layer}_{q}", [P, 512], ctx) for q in range(4)]
        ps_row = [[pb(f"j{layer}_row{q}{k}", [P, 512], ctx) for k in range(2)] for q in range(2)]
        names = ("pick", "picked", "less", "ex", "weight", "inv", "spread", "taken", "total", "hT", "row", "rowc",
                 "out0", "out1", "fixT", "fix", "fixc", "put", "on")
        s = {n: sem(f"j{layer}_{n}", ctx) for n in names}
        block = ctx.enter_context(nc.Block())
        HALF = NCH // 2

        @block.sync
        def _(sp):
            def store(n, q):
                sp.wait_ge(s["rowc"], n + 3)
                sp.dma_start(result[bass.ds(n * CH, CH), :].rearrange("(b p) f -> p b f", p=P), row[:, q]
                             ).then_inc(s[f"out{q}"], 16)

            with sp.Fori(0, HALF) as i:
                store(2 * i, 0)
                store(2 * i + 1, 1)
            store(NCH - 1, 0)

        @block.gpsimd
        def _(pool):
            pool.wait_ge(s["out0"], 16 * (HALF + 1))
            pool.wait_ge(s["out1"], 16 * HALF)
            for f in range(NFIX):
                n = min(P, T - f * P)
                pool.wait_ge(s["fixc"], f + 1)
                nc.gpsimd.indirect_dma_start(
                    out=result, out_offset=bass.IndirectOffsetOnAxis(ap=fix_rows[0:n, f:f + 1], axis=0),
                    in_=fix[0:n, f, :], in_offset=None).then_inc(s["put"], 16)
            pool.wait_ge(s["put"], 16 * NFIX)

        @block.tensor
        def _(pe):
            def pick(what, f):
                n = 4 * what + f
                if n >= 4:
                    pe.wait_ge(s["picked"], n - 3)
                for k in range(4):
                    m = H * (4 * f + k)
                    op = nc.tensor.matmul(ps[f][0:H, 2 * NG * k:2 * NG * k + 2 * NG], ident[:, m:m + H], ends[:, :, :, what],
                                          start=True, stop=True, skip_group_check=True)
                op.then_inc(s["pick"], 1)

            def spread(of, half, f, bank):
                nc.tensor.matmul(ps[bank][:, 0:Q], hsel[0:H, half, :], of[:, f * Q:f * Q + Q], start=True, stop=True
                                 ).then_inc(s["spread"], 1)

            def project(n, q):
                pe.wait_ge(s["hT"], n + 1)
                pe.wait_ge(s["rowc"], n + 1)
                for k in range(2):
                    for h in range(2):
                        if layer == 0:
                            op = nc.tensor.matmul(ps_row[q][k][:, 0:ROW], hT[:, q, h, k * P:k * P + P], wext[:, h, 1, :],
                                                  start=(h == 0), stop=(h == 1))
                        else:
                            op = nc.tensor.transpose(ps_row[q][k][:, h * P:h * P + P], hT[:, q, h, k * P:k * P + P], ident[:])
                op.then_inc(s["row"], 1)

            pe.sem_inc(s["row"], 2)
            for what in range(2):
                for f in range(4):
                    pick(what, f)
            with pe.Fori(0, HALF // 2) as i:
                project(2 * i, 0)
                project(2 * i + 1, 1)
            pe.wait_ge(s["weight"], 1)
            for half in range(2):
                for f in range(4):
                    pe.wait_ge(s["taken" if half else "picked"], f + 1 if half else f + 5)
                    spread(weight, half, f, f)
            with pe.Fori(HALF // 2, HALF) as i:
                project(2 * i, 0)
                project(2 * i + 1, 1)
            project(NCH - 1, 0)
            pe.wait_ge(s["inv"], 1)
            for half in range(2):
                for f in range(2):
                    pe.wait_ge(s["taken"], 4 + 2 * half + f + 1)
                    spread(inv, half, f, 2 * half + f)
            for f in range(NFIX):
                n = min(P, T - f * P)
                if f == 0:
                    pe.wait_ge(s["fixT"], 1)
                slot, k = divmod(f % 4, 2)
                pe.wait_ge(s["rowc"], NCH + 2)
                if f >= 4:
                    pe.wait_ge(s["fixc"], f - 3)
                for h in range(2):
                    if layer == 0:
                        op = nc.tensor.matmul(ps_row[slot][k][0:n, 0:ROW], fixT[:, h, f * P:f * P + n], wext[:, h, 1, :],
                                              start=(h == 0), stop=(h == 1))
                    else:
                        op = nc.tensor.transpose(ps_row[slot][k][0:n, h * P:h * P + P], fixT[:, h, f * P:f * P + n], ident[:])
                op.then_inc(s["fix"], 1)

        @block.scalar
        def _(act):
            def entries(t):
                return t.rearrange("p (g f k e) -> p f k g e", g=NG, f=4, k=4)

            def picked(what, f):
                act.wait_ge(s["pick"], 4 * what + f + 1)
                nc.scalar.activation(entries((mx, sm)[what][:])[:, f],
                                     ps[f][0:H, 0:Q].rearrange("p (k g e) -> p k g e", k=4, e=2), ACT.Copy
                                     ).then_inc(s["picked"], 1)

            def biased(n, q):
                act.wait_ge(s["row"], n + 1)
                act.wait_ge(s["on"], 1)
                for h in range(2):
                    op = nc.scalar.activation(hT[:, q, h, :], acc[:, h, bass.ds(n * CH, CH)], FUNC,
                                              bias=gbias[:, layer, h:h + 1])
                op.then_inc(s["hT"], 1)

            def rows(n, q, i):
                act.wait_ge(s["row"], n + 3)
                if not isinstance(i, int) or i > 0:
                    act.wait_ge(s[f"out{q}"], 16 * i)
                for k in range(2):
                    op = nc.scalar.activation(row[:, q, k, :], ps_row[q][k][:, 0:WIDTH], ACT.Copy)
                op.then_inc(s["rowc"], 1)

            def pair(i):
                biased(2 * i + 1, 1)
                rows(2 * i, 0, i)
                biased(2 * i + 2, 0)
                rows(2 * i + 1, 1, i)

            act.sem_inc(s["on"], 1)
            act.sem_inc(s["rowc"], 2)
            for what in range(2):
                for f in range(4):
                    picked(what, f)
            biased(0, 0)
            pair(0)
            act.wait_ge(s["less"], 1)
            nc.scalar.activation(ex[:], top[:], ACT.Exp).then_inc(s["ex"], 1)
            with act.Fori(1, HALF) as i:
                pair(i)
            rows(NCH - 1, 0, HALF)
            for h in range(2):
                act.wait_ge(s["total"], h + 1)
                op = nc.scalar.activation(fixT[:, h, :], total[:, h, :], FUNC, bias=gbias[:, layer, h:h + 1])
            op.then_inc(s["fixT"], 1)
            for f in range(NFIX):
                n = min(P, T - f * P)
                slot, k = divmod(f % 4, 2)
                act.wait_ge(s["fix"], f + 1)
                nc.scalar.activation(fix[0:n, f, :], ps_row[slot][k][0:n, 0:WIDTH], ACT.Copy).then_inc(s["fixc"], 1)

        @block.vector
        def _(vec):
            vec.wait_ge(s["picked"], 4)
            nc.vector.tensor_tensor_scan(fwd[:], sep[0:H, 0:L], mx[:], -BIG, ALU.add, ALU.max)
            vec.drain()
            nc.vector.tensor_tensor_scan(top[:, ::-1], sep[0:H, 1:L + 1][:, ::-1], fwd[:, ::-1], -BIG, ALU.add, ALU.max)
            vec.drain()
            nc.vector.tensor_tensor(top[:], mx[:], top[:], ALU.subtract).then_inc(s["less"], 1)
            vec.wait_ge(s["picked"], 8)
            vec.wait_ge(s["ex"], 1)
            nc.vector.tensor_tensor(weight[:], ex[:], sm[:], ALU.mult)
            vec.drain()
            nc.vector.tensor_tensor(weight[:, 1:L:2], weight[:, 1:L:2], begins[0:H, 1:L:2], ALU.mult).then_inc(s["weight"], 1)
            vec.wait_ge(s["weight"], 1)
            nc.vector.tensor_tensor_scan(fwd[:], same[0:H, 0:L], weight[:], 0.0, ALU.mult, ALU.add)
            vec.drain()
            nc.vector.tensor_tensor_scan(top[:, ::-1], sep[0:H, 1:L + 1][:, ::-1], fwd[:, ::-1], -BIG, ALU.add, ALU.max)
            vec.drain()
            nc.vector.tensor_single_scalar(inv[:], top[:, 0:L:2], 1e-16, ALU.add)
            vec.drain()
            nc.vector.reciprocal(inv[:], inv[:]).then_inc(s["inv"], 1)
            for half in range(2):
                for f in range(4):
                    vec.wait_ge(s["spread"], 4 * half + f + 1)
                    nc.vector.tensor_tensor(
                        a[:, f * Q:f * Q + Q].rearrange("p (t e) -> p t e", e=2),
                        ps[f][:, 0:Q].rearrange("p (t e) -> p t e", e=2),
                        parts[:, f * Q // 2:f * Q // 2 + Q // 2, half, :], ALU.mult).then_inc(s["taken"], 1)
                vec.drain()
                nc.vector.tensor_tensor_scan(b[:], same[:, 0:L], a[:], 0.0, ALU.mult, ALU.add)
                vec.drain()
                nc.vector.tensor_tensor(b[:], b[:], begins[:, 1:L + 1], ALU.mult)
                vec.drain()
                nc.vector.tensor_tensor_scan(a[:, ::-1], same[:, 1:L + 1][:, ::-1], b[:, ::-1], 0.0, ALU.mult, ALU.add)
                vec.drain()
                nc.vector.tensor_copy(total[:, half, :], a[:, 0:L:2])
                vec.drain()
            for half in range(2):
                for f in range(2):
                    vec.wait_ge(s["spread"], 8 + 2 * half + f + 1)
                    op = nc.vector.tensor_tensor(total[:, half, f * Q:f * Q + Q], total[:, half, f * Q:f * Q + Q],
                                                 ps[2 * half + f][:, 0:Q], ALU.mult)
                op.then_inc(s["total"], 1)


def last(nc, sb, pb, sem, v):
    ident, cst = v["ident"], v["cst"]
    wq, bq, vw, bvw, kvw, row_iota = v["wq"], v["bq"], v["vw"], v["bvw"], v["kvw"], v["row_iota"]
    x, out = v["x"], v["out"]
    with ExitStack() as ctx:
        def tmp(name, shape, dt=F32):
            return sb("l_" + name, shape, dt, ctx)

        ew = tmp("ew", [P, 3, NEXP, 2, F])
        eb = tmp("eb", [P, 2, NEXP, 2])
        eb3 = tmp("eb3", [NEXP, F])
        rw1 = tmp("rw1", [P, 2, P])
        rb1 = tmp("rb1", [P, 1])
        rw2 = tmp("rw2", [P, NEXP])
        rb2 = tmp("rb2", [P, NEXP])
        xb = tmp("xb", [P, 2, 2, F])
        xn = tmp("xn", [P, 2, F])
        base = tmp("base", [P, 2, F])
        stats = tmp("stats", [P, 2, 6])
        mv = tmp("mv", [P, 2, 2])
        eps = tmp("eps", [P, 2])
        rstd = tmp("rstd", [P, 2])
        xnT = tmp("xnT", [P, 2, CH])
        qc = tmp("qc", [P, 2, F])
        q2 = tmp("q2", [P, 2, F])
        q4 = tmp("q4", [P, 2, F])
        qs = tmp("qs", [P, 8])
        q2n = tmp("q2n", [P, 2, F])
        q2T = tmp("q2T", [P, 2, CH])
        cb = tmp("cb", [P, 2, 2, F])
        x2, res = (v["acc"][:, h, 0:4 * F].rearrange("p (q b f) -> p q b f", q=2, b=2) for h in range(2))
        yn = tmp("yn", [P, 2, F])
        yT = tmp("yT", [P, 2, 2, CH])
        rhT = tmp("rhT", [P, CH])
        logit = tmp("logit", [P, 2, NEXP])
        prob = tmp("prob", [P, 2, 8])
        small = tmp("small", [P, 2, 8])
        top8 = tmp("top8", [P, 2, 8])
        at8 = tmp("at8", [P, 2, 8], U32)
        at8f = tmp("at8f", [P, 2, 8])
        gate = tmp("gate", [P, 2, 2, NEXP])
        gate2 = tmp("gate2", [P, 2, NEXP])
        gateT = tmp("gateT", [NEXP, CH])
        h1 = tmp("h1", [P, 2, CH])
        h2 = tmp("h2", [P, 2, CH])
        ps_t, ps_q, ps_m, ps_r, ps_h1, ps_h2, ps_o0, ps_o1 = (
            pb("l_ps_" + n, [P, 512], ctx) for n in ("t", "q", "m", "r", "h1", "h2", "o0", "o1"))
        ps_o = [ps_o0, ps_o1]
        names = ("w_in", "x0", "x1", "out0", "out1", "eps", "rstd", "xn", "t", "tc", "g", "q", "qc", "qs", "qss", "qsr", "q2n",
                 "mix", "x2", "eps2", "rstd2", "yn", "rh", "rhc", "lg", "mx", "pe_", "gap", "ge", "gate", "gateT", "gateTc",
                 "b3", "init", "h1", "h1c", "h2", "h2c", "o", "oc", "base", "c0", "c1")
        s = {n: sem("l_" + n, ctx) for n in names}
        s_on = sem("l_on", ctx)
        block = ctx.enter_context(nc.Block())
        loads = []
        for m, (we, be) in enumerate((("ew1", "eb1"), ("ew2", "eb2"), ("ew3", None))):
            for e in range(NEXP):
                loads.append((ew[:, m, e], v[we][e].rearrange("(a p) f -> p a f", p=P)))
                if be:
                    for a in range(2):
                        loads.append((eb[:, m, e, a:a + 1], v[be].rearrange("e (a p b) -> e a p b", p=P, b=1)[e, a]))
        loads += [(eb3[:], v["eb3"]), (rw1[:], v["rw1"].rearrange("(a p) f -> p a f", p=P)),
                  (rb1[:], v["rb1"].rearrange("(p b) -> p b", b=1)), (rw2[:], v["rw2"]),
                  (rb2[:], v["rb2"].rearrange("(a f) -> a f", a=1).broadcast_to((P, NEXP)))]

        @block.sync
        def _(sp):
            sp.dma_start(xb[:, 0], x[0:CH, :].rearrange("(b p) f -> p b f", p=P)).then_inc(s["x0"], 16)
            sp.dma_start(cb[:, 0], v["conv"][0:CH, :].rearrange("(b p) f -> p b f", p=P)).then_inc(s["c0"], 16)
            for to, of in loads:
                sp.dma_start(to, of).then_inc(s["w_in"], 16)

            def store(n, q, i):
                sp.wait_ge(s["oc"], NEXP * n + NEXP + 2)
                sp.dma_start(out[bass.ds(n * CH, CH), :].rearrange("(b p) f -> p b f", p=P), res[:, q]).then_inc(s[f"out{q}"], 16)

            def fetch(n, q):
                sp.wait_ge(s["base"], n)
                sp.dma_start(xb[:, q], x[bass.ds(n * CH, CH), :].rearrange("(b p) f -> p b f", p=P)).then_inc(s[f"x{q}"], 16)
                sp.dma_start(cb[:, q], v["conv"][bass.ds(n * CH, CH), :].rearrange("(b p) f -> p b f", p=P)
                             ).then_inc(s[f"c{q}"], 16)

            with sp.Fori(0, NCH // 2) as i:
                for q in range(2):
                    fetch(2 * i + q + 1, 1 - q)
                    store(2 * i + q, q, i)
            store(NCH - 1, 0, NCH // 2)
            sp.wait_ge(s["out0"], 16 * (NCH // 2 + 1))
            sp.wait_ge(s["out1"], 16 * (NCH // 2))

        @block.gpsimd
        def _(pool):
            pool.sem_inc(s_on, 1)

            def power(o, i_, e, wait, at, done):
                pool.wait_ge(s[wait], at)
                nc.gpsimd.tensor_tensor(o, i_, cst[:, e:e + 1].broadcast_to((P, 2)), ALU.pow).then_inc(s[done], 1)

            def both(n, q, h):
                power(rstd[:], eps[:], 0, "eps", n + 1, "rstd")
                pool.wait_ge(s["xn"], n + 1)
                pool.wait_ge(s["x2"], n + 1)
                nc.gpsimd.tensor_tensor(base[:], xb[:, q], xn[:], ALU.add)
                pool.drain()
                pool.wait_ge(s[f"c{q}"], 16 * h + 16)
                nc.gpsimd.tensor_tensor(base[:], base[:], cb[:, q], ALU.add)
                pool.drain()
                nc.gpsimd.tensor_tensor(base[:], base[:], bvw[:].unsqueeze(1).broadcast_to((P, 2, F)), ALU.add
                                        ).then_inc(s["base"], 1)
                power(qs[:, 4:6], qs[:, 2:4], 1, "qss", n + 1, "qsr")
                power(rstd[:], eps[:], 0, "eps2", n + 1, "rstd2")

            pool.sem_inc(s["base"], 1)
            both(0, 0, 0)
            with pool.Fori(0, NCH // 2) as i:
                for q in range(2):
                    both(2 * i + q + 1, 1 - q, i + q)

        @block.vector
        def _(vec):
            def norm(src, to, n, e, r, done):
                for b in range(2):
                    nc.vector.bn_stats(stats[:, b, :], src[:, b, :])
                vec.drain()
                for b in range(2):
                    nc.vector.bn_aggr(mv[:, b, :], stats[:, b, :])
                vec.drain()
                nc.vector.tensor_single_scalar(eps[:], mv[:, :, 1], LN_EPS, ALU.add).then_inc(s[e], 1)
                vec.wait_ge(s[r], n + 1)
                for b in range(2):
                    op = nc.vector.tensor_scalar(to[:, b, :], src[:, b, :], mv[:, b, 0:1], rstd[:, b:b + 1], ALU.subtract, ALU.mult)
                op.then_inc(s[done], 1)

            def f0(n, q, i):
                vec.wait_ge(s[f"x{q}"], 16 * i + 16)
                vec.wait_ge(s["base"], n + 1)
                norm(xb[:, q], xn, n, "eps", "rstd", "xn")

            def f1a(n):
                vec.wait_ge(s["q"], n + 1)
                nc.vector.tensor_tensor(qc[:], ps_q[:].rearrange("p (b f) -> p b f", b=2),
                                        bq[:].unsqueeze(1).broadcast_to((P, 2, F)), ALU.add).then_inc(s["qc"], 1)

            def f1b(n):
                vec.wait_ge(s["qss"], n + 1)
                nc.vector.tensor_single_scalar(qs[:, 0:2], qs[:, 0:2], EPS_DIV, ALU.add)
                vec.drain()
                nc.vector.reciprocal(qs[:, 6:8], qs[:, 0:2])
                vec.drain()
                vec.wait_ge(s["qsr"], n + 1)
                nc.vector.tensor_tensor(qs[:, 4:6], qs[:, 4:6], qs[:, 6:8], ALU.mult)
                vec.drain()
                nc.vector.tensor_single_scalar(qs[:, 4:6], qs[:, 4:6], EPS_NORM, ALU.max)
                vec.drain()
                nc.vector.reciprocal(qs[:, 4:6], qs[:, 4:6])
                vec.drain()
                nc.vector.tensor_tensor(qs[:, 4:6], qs[:, 4:6], qs[:, 6:8], ALU.mult)
                vec.drain()
                for b in range(2):
                    op = nc.vector.tensor_scalar(q2n[:, b, :], q2[:, b, :], qs[:, 4 + b:5 + b], None, ALU.mult)
                op.then_inc(s["q2n"], 1)

            def f2(n, q):
                vec.wait_ge(s["mix"], n + 1)
                vec.wait_ge(s["base"], n + 2)
                nc.vector.tensor_tensor(x2[:, q], ps_m[:].rearrange("p (b f) -> p b f", b=2), base[:], ALU.add
                                        ).then_inc(s["x2"], 1)
                vec.wait_ge(s["x2"], n + 2)
                norm(x2[:, q], yn, n, "eps2", "rstd2", "yn")

            def f3(n, q):
                vec.wait_ge(s["lg"], n + 1)
                nc.vector.tensor_tensor(logit[:], ps_r[:, CH:CH + 2 * NEXP].rearrange("p (b e) -> p b e", b=2),
                                        rb2[:].unsqueeze(1).broadcast_to((P, 2, NEXP)), ALU.add)
                vec.drain()
                nc.vector.tensor_reduce(small[:, :, 0], logit[:], AX.X, ALU.max)
                vec.drain()
                nc.vector.tensor_tensor(logit[:], logit[:], small[:, :, 0:1].broadcast_to((P, 2, NEXP)), ALU.subtract
                                        ).then_inc(s["mx"], 1)
                vec.wait_ge(s["pe_"], n + 1)
                nc.vector.tensor_reduce(small[:, :, 1], prob[:, :, 0:NEXP], AX.X, ALU.add)
                vec.drain()
                nc.vector.reciprocal(small[:, :, 2], small[:, :, 1])
                vec.drain()
                nc.vector.tensor_tensor(prob[:, :, 0:NEXP], prob[:, :, 0:NEXP], small[:, :, 2:3].broadcast_to((P, 2, NEXP)),
                                        ALU.mult)
                vec.drain()
                for b in range(2):
                    nc.vector.max(top8[:, b, :], prob[:, b, :])
                vec.drain()
                for b in range(2):
                    nc.vector.max_index(at8[:, b, :], top8[:, b, :], prob[:, b, :])
                nc.vector.tensor_tensor(small[:, :, 3], top8[:, :, 1], top8[:, :, 0], ALU.subtract).then_inc(s["gap"], 1)
                vec.wait_ge(s["gap"], n + 1)
                nc.vector.tensor_copy(at8f[:], at8[:])
                vec.wait_ge(s["ge"], n + 1)
                nc.vector.tensor_single_scalar(small[:, :, 5], small[:, :, 4], 1.0, ALU.add)
                vec.drain()
                nc.vector.reciprocal(small[:, :, 6], small[:, :, 5])
                vec.drain()
                nc.vector.tensor_tensor(small[:, :, 7], small[:, :, 6], small[:, :, 4], ALU.mult)
                vec.drain()
                for b in range(2):
                    nc.vector.tensor_scalar(gate[:, q, b, :], row_iota[:, 0:NEXP], at8f[:, b, 0:1], small[:, b, 6:7],
                                            ALU.is_equal, ALU.mult)
                    nc.vector.tensor_scalar(gate2[:, b, :], row_iota[:, 0:NEXP], at8f[:, b, 1:2], small[:, b, 7:8],
                                            ALU.is_equal, ALU.mult)
                vec.drain()
                nc.vector.tensor_tensor(gate[:, q], gate[:, q], gate2[:], ALU.add).then_inc(s["gate"], 1)

            def f4(n, q, i):
                vec.wait_ge(s["b3"], n + 1)
                if i is not None:
                    vec.wait_ge(s[f"out{q}"], 16 * i)
                nc.vector.tensor_tensor(res[:, q], ps_m[:].rearrange("p (b f) -> p b f", b=2), x2[:, q], ALU.add
                                        ).then_inc(s["init"], 1)

            def expert(n, q, e):
                vec.wait_ge(s["o"], NEXP * n + e + 2)
                if e == 0:
                    vec.wait_ge(s["init"], n + 1)
                else:
                    vec.wait_ge(s["oc"], NEXP * n + e + 2)
                for b in range(2):
                    op = nc.vector.scalar_tensor_tensor(res[:, q, b, :], ps_o[e % 2][:, b * F:b * F + F], gate[:, q, b, e:e + 1],
                                                        res[:, q, b, :], ALU.mult, ALU.add)
                op.then_inc(s["oc"], 1)

            def step(n, q, i, more=True):
                m, p = n + 1, 1 - q
                f3(n, q)
                if more:
                    f0(m, p, i if q == 0 else i + 1)
                f4(n, q, None if isinstance(n, int) and n < 2 else i)
                for e in range(NEXP):
                    expert(n, q, e)
                    if more and e == 1:
                        f1a(m)
                        f1b(m)
                    if more and e == 3:
                        f2(m, p)

            nc.vector.memset(prob[:, :, NEXP:8], -1.0)
            vec.sem_inc(s["x2"], 1)
            vec.sem_inc(s["oc"], 2)
            vec.wait_ge(s["w_in"], 16 * len(loads))
            f0(0, 0, 0)
            f1a(0)
            f1b(0)
            f2(0, 0)
            step(0, 0, 0)
            step(1, 1, 0)
            with vec.Fori(1, NCH // 2) as i:
                step(2 * i, 0, i)
                step(2 * i + 1, 1, i)
            step(NCH - 1, 0, NCH // 2, more=False)

        @block.scalar
        def _(act):
            def turned(n, k, to):
                act.wait_ge(s["t"], 3 * n + k + 1)
                nc.scalar.activation(to, ps_t[:].rearrange("p (a m) -> p a m", a=2), ACT.Copy).then_inc(s["tc"], 1)

            def g1(n):
                act.wait_ge(s["qc"], n + 1)
                for b in range(2):
                    nc.scalar.activation(q2[:, b, :], qc[:, b, :], ACT.Square, accum_out=qs[:, b:b + 1])
                act.drain()
                for b in range(2):
                    op = nc.scalar.activation(q4[:, b, :], q2[:, b, :], ACT.Square, accum_out=qs[:, 2 + b:3 + b])
                op.then_inc(s["qss"], 1)

            def g3(n):
                act.wait_ge(s["rh"], n + 1)
                nc.scalar.activation(rhT[:], ps_r[:, 0:CH], ACT.Relu, bias=rb1[:]).then_inc(s["rhc"], 1)

            def g4a(n):
                act.wait_ge(s["mx"], n + 1)
                nc.scalar.activation(prob[:, :, 0:NEXP], logit[:], ACT.Exp).then_inc(s["pe_"], 1)

            def g4b(n):
                act.wait_ge(s["gap"], n + 1)
                nc.scalar.activation(small[:, :, 4], small[:, :, 3], ACT.Exp).then_inc(s["ge"], 1)

            def g5(n):
                act.wait_ge(s["gateT"], n + 1)
                nc.scalar.activation(gateT[:], ps_r[0:NEXP, 0:CH], ACT.Copy).then_inc(s["gateTc"], 1)

            def hidden(n, e, m, ps, to, name):
                act.wait_ge(s[name], NEXP * n + e + 1)
                if m == 1:
                    act.wait_ge(s["o"], NEXP * n + e + 1)
                for a in range(2):
                    op = nc.scalar.activation(to[:, a, :], ps[:, a * CH:a * CH + CH], ACT.Relu, bias=eb[:, m, e, a:a + 1])
                op.then_inc(s[name + "c"], 1)

            def step(n, q, more=True):
                for e in range(NEXP):
                    hidden(n, e, 1, ps_h2, h2, "h2")
                    if e == 0:
                        g4a(n)
                    if more and e == 2:
                        turned(n + 1, 0, xnT[:])
                    if e + 1 < NEXP:
                        hidden(n, e + 1, 0, ps_h1, h1, "h1")
                    if e == 0:
                        g4b(n)
                    if e == 1:
                        g5(n)
                    if more and e == 2:
                        g1(n + 1)
                    if more and e == 3:
                        turned(n + 1, 1, q2T[:])
                    if more and e == 4:
                        turned(n + 1, 2, yT[:, 1 - q])
                if more:
                    hidden(n + 1, 0, 0, ps_h1, h1, "h1")
                    g3(n + 1)

            act.wait_ge(s["w_in"], 16 * len(loads))
            turned(0, 0, xnT[:])
            g1(0)
            turned(0, 1, q2T[:])
            turned(0, 2, yT[:, 0])
            hidden(0, 0, 0, ps_h1, h1, "h1")
            g3(0)
            with act.Fori(0, NCH // 2) as i:
                for q in range(2):
                    step(2 * i + q, q)
            step(NCH - 1, 0, more=False)

        @block.tensor
        def _(pe):
            def turn(of, name=None, at=None):
                for a in range(2):
                    for b in range(2):
                        op = nc.tensor.transpose(ps_t[:, a * CH + b * P:a * CH + b * P + P], of[:, b, a * P:a * P + P], ident[:])
                op.then_inc(s["t"], 1)

            def p0(n):
                pe.wait_ge(s["xn"], n + 1)
                pe.wait_ge(s["tc"], 3 * n + 1)
                turn(xn)

            def p1(n):
                pe.wait_ge(s["tc"], 3 * n + 2)
                if not isinstance(n, int) or n > 0:
                    pe.wait_ge(s["qc"], n)
                for b in range(2):
                    for a in range(2):
                        op = nc.tensor.matmul(ps_q[:, b * F:b * F + F], xnT[:, a, b * P:b * P + P], wq[:, a, :],
                                              start=(a == 0), stop=(a == 1))
                op.then_inc(s["q"], 1)

            def turn_q2(n):
                pe.wait_ge(s["q2n"], n + 1)
                turn(q2n)

            def mix(n):
                pe.wait_ge(s["tc"], 3 * n + 3)
                if not (isinstance(n, int) and n == 0):
                    pe.wait_ge(s["init"], n)
                for b in range(2):
                    for a in range(2):
                        nc.tensor.matmul(ps_m[:, b * F:b * F + F], xnT[:, a, b * P:b * P + P], vw[:, a, :], start=(a == 0), stop=False)
                    for a in range(2):
                        op = nc.tensor.matmul(ps_m[:, b * F:b * F + F], q2T[:, a, b * P:b * P + P], kvw[:, a, :],
                                              start=False, stop=(a == 1))
                op.then_inc(s["mix"], 1)

            def turn_y(n):
                pe.wait_ge(s["yn"], n + 1)
                turn(yn)

            def router(n, q):
                for a in range(2):
                    op = nc.tensor.matmul(ps_r[:, 0:CH], rw1[:, a, :], yT[:, q, a, :], start=(a == 0), stop=(a == 1))
                op.then_inc(s["rh"], 1)

            def p3(n):
                pe.wait_ge(s["rhc"], n + 1)
                for b in range(2):
                    op = nc.tensor.matmul(ps_r[:, CH + b * NEXP:CH + b * NEXP + NEXP], rhT[:, b * P:b * P + P], rw2[:],
                                          start=True, stop=True)
                op.then_inc(s["lg"], 1)

            def p4(n, q):
                pe.wait_ge(s["gate"], n + 1)
                for b in range(2):
                    op = nc.tensor.transpose(ps_r[0:NEXP, b * P:b * P + P], gate[:, q, b, :], ident[:])
                op.then_inc(s["gateT"], 1)

            def p5(n):
                pe.wait_ge(s["gateTc"], n + 1)
                pe.wait_ge(s["x2"], n + 2)
                for b in range(2):
                    op = nc.tensor.matmul(ps_m[:, b * F:b * F + F], gateT[:, b * P:b * P + P], eb3[:], start=True, stop=True)
                op.then_inc(s["b3"], 1)

            def first(n, q, e):
                if e == 0:
                    pe.wait_ge(s["tc"], 3 * n + 4)
                if e > 0 or not (isinstance(n, int) and n == 0):
                    pe.wait_ge(s["h1c"], NEXP * n + e)
                for a in range(2):
                    for k in range(2):
                        op = nc.tensor.matmul(ps_h1[:, a * CH:a * CH + CH], ew[:, 0, e, k, a * P:a * P + P], yT[:, q, k, :],
                                              start=(k == 0), stop=(k == 1))
                op.then_inc(s["h1"], 1)

            def second(n, e):
                pe.wait_ge(s["h1c"], NEXP * n + e + 1)
                for a in range(2):
                    for k in range(2):
                        op = nc.tensor.matmul(ps_h2[:, a * CH:a * CH + CH], ew[:, 1, e, k, a * P:a * P + P], h1[:, k, :],
                                              start=(k == 0), stop=(k == 1))
                op.then_inc(s["h2"], 1)

            def third(n, e):
                pe.wait_ge(s["h2c"], NEXP * n + e + 1)
                pe.wait_ge(s["oc"], NEXP * n + e + 1)
                for b in range(2):
                    for k in range(2):
                        op = nc.tensor.matmul(ps_o[e % 2][:, b * F:b * F + F], h2[:, k, b * P:b * P + P], ew[:, 2, e, k, :],
                                              start=(k == 0), stop=(k == 1))
                op.then_inc(s["o"], 1)

            def step(n, q, more=True):
                for e in range(NEXP):
                    second(n, e)
                    if e == 0:
                        p3(n)
                    if more and e == 2:
                        p0(n + 1)
                    if e + 1 < NEXP:
                        first(n, q, e + 1)
                    elif more:
                        first(n + 1, 1 - q, 0)
                    if e == 1:
                        p4(n, q)
                    if more and e == 2:
                        p1(n + 1)
                    if more and e == 3:
                        turn_q2(n + 1)
                    third(n, e)
                    if e == 1:
                        p5(n)
                    if more and e == 3:
                        mix(n + 1)
                    if more and e == 4:
                        turn_y(n + 1)
                if more:
                    router(n + 1, 1 - q)

            pe.sem_inc(s["tc"], 1)
            pe.sem_inc(s["o"], 1)
            pe.wait_ge(s["w_in"], 16 * len(loads))
            p0(0)
            p1(0)
            turn_q2(0)
            mix(0)
            turn_y(0)
            first(0, 0, 0)
            router(0, 0)
            with pe.Fori(0, NCH // 2) as i:
                for q in range(2):
                    step(2 * i + q, q)
            step(NCH - 1, 0, more=False)


INS = ["x", "src_t", "dst_t", "dst_g", "first_row", "last_row", "edge_b", "W1", "as1", "ad1", "We1", "ae1", "b1", "W2", "as2",
       "ad2", "We2", "ae2", "b2", "Wqkv", "bqkv", "Wout", "bout", "rw1", "rb1", "rw2", "rb2", "ew1", "eb1", "ew2", "eb2",
       "ew3", "eb3"]


def kernel(x, src, dst, edge_attr_16, **w):
    import concourse.bacc as bacc
    from concourse.bass_utils import run_bass_kernel_spmd

    src_p = np.pad(np.asarray(src), (0, EP - E))
    dst_p = np.pad(np.asarray(dst), (0, EP - E), constant_values=N)
    edge_p = np.pad(np.asarray(edge_attr_16), ((0, EP - E), (0, 0)))
    arrays = {
        "x": np.pad(np.asarray(x), ((0, NP - N), (0, 0))),
        "src_t": src_p.reshape(T, P).T,
        "dst_t": dst_p.reshape(T, P).T,
        "dst_g": dst_p.reshape(NG, GT, P),
        "first_row": dst_p[None, ::P],
        "last_row": dst_p[None, P - 1::P],
        "edge_b": edge_p.reshape(T // H, H, P, D_EDGE).transpose(1, 3, 0, 2).reshape(P, T // H, P),
    }
    for l in "12":
        for to, of in (("W", "W"), ("as", "att_src"), ("ad", "att_dst"), ("We", "W_e"), ("ae", "att_e"), ("b", "b")):
            arrays[to + l] = w["L0_gnn_" + of + l]
    for to, of in (("Wqkv", "W_qkv"), ("bqkv", "b_qkv"), ("Wout", "W_out"), ("bout", "b_out")):
        arrays[to] = w["L0_mix_" + of]
    for to, of in (("r", "router"), ("e", "expert")):
        for part in ("w1", "b1", "w2", "b2") + (("w3", "b3") if to == "e" else ()):
            arrays[to + part] = w[f"L0_ffn_{of}_{part}"]
    nc = bacc.Bacc("TRN2", target_bir_lowering=False, num_devices=1)
    maps, args = {}, []
    for name in INS:
        a = np.ascontiguousarray(arrays[name])
        maps["in_" + name] = a
        args.append(nc.dram_tensor("in_" + name, a.shape, mybir.dt.from_np(a.dtype), kind="ExternalInput").ap())
    args.append(nc.dram_tensor("out_x", (NP, F), F32, kind="ExternalOutput").ap())
    build(nc, *args)
    r = run_bass_kernel_spmd(nc, [maps], core_ids=[0])
    return r.results[0]["out_x"][:N]
```

```python
from contextlib import ExitStack

import numpy as np

import concourse.bass as bass
from concourse import mybir

F32 = mybir.dt.float32
BF16 = mybir.dt.bfloat16
I32 = mybir.dt.int32
U32 = mybir.dt.uint32
ALU = mybir.AluOpType
ACT = mybir.ActivationFunctionType
AX = mybir.AxisListType

P = 128
N = 6250
E = 106250
F = 256
H = 8
C = F // H
D_EDGE = 16
NEXP = 6
NB = 50
NP = NB * P
GT = P // H
NG = -(-E // (P * GT))
T = NG * GT
EP = T * P
ROW = F + 2 * H
L = 2 * T
NFIX = -(-T // P)
WIN = P + 1
BIG = 1e38
LN_EPS = 1e-5
EPS_DIV = 1e-7
EPS_NORM = 1e-12
CH = 2 * P
NCH = NP // CH
TT = -(-(2 * NB + NEXP - 1) // 12) * 12


def clear_semaphores(nc, sems):
    block = nc.Block()
    with block:
        @block.gpsimd
        def _(pool):
            for one in sems:
                pool.sem_clear(one)


def build(nc, x, src_t, dst_t, dst_g, first_row, last_row, edge_b, W1, as1, ad1, We1, ae1, b1, W2, as2, ad2, We2,
          ae2, b2, Wqkv, bqkv, Wout, bout, rw1, rb1, rw2, rb2, ew1, eb1, ew2, eb2, ew3, eb3, out):
    with ExitStack() as top:
        def sb(name, shape, dt=F32, ctx=top):
            return ctx.enter_context(nc.sbuf_tensor(name, shape, dt))

        def pb(name, shape, ctx):
            return ctx.enter_context(nc.psum_tensor(name, shape, F32))

        def sem(name, ctx):
            return ctx.enter_context(nc.semaphore(name))

        table = [nc.dram_tensor(f"table{l}", (NP, ROW), F32).ap() for l in range(2)]
        conv = nc.dram_tensor("conv", (NP, F), F32).ap()

        ident = sb("ident", [P, P])
        acc = sb("acc", [P, 2, NP])
        sep = sb("sep", [P, NG, P + 1], BF16)
        same = sb("same", [P, NG, P + 1], BF16)
        ends = sb("ends", [P, NG, 2, 2])
        begins = sb("begins", [P, L + 1], BF16)
        ends_sep = sb("ends_sep", [P, L + 1], BF16)
        ends_same = sb("ends_same", [P, L + 1], BF16)
        parts = sb("parts", [P, T, 2, 2])
        src_sb = sb("src_sb", [P, T], I32)
        rel = sb("rel", [P, T])
        islast = sb("islast", [P, T])
        first_sb = sb("first_sb", [1, T], I32)
        row_iota = sb("row_iota", [P, P])
        fix_rows = sb("fix_rows", [P, NFIX], I32)
        hsel = sb("hsel", [P, 2, P])
        wext = sb("wext", [P, 2, 2, ROW])
        wedge = sb("wedge", [P, 2, H, H])
        gbias = sb("gbias", [P, 2, 2])
        wq = sb("wq", [P, 2, F])
        bq = sb("bq", [P, F])
        vw = sb("vw", [P, 2, F])
        bvw = sb("bvw", [P, F])
        kvw = sb("kvw", [P, 2, F])
        cst = sb("cst", [P, 4])

        prepare(nc, sb, pb, sem, locals())
        blocks(nc, sb, pb, sem, locals())
        for layer in range(2):
            edges(nc, sb, pb, sem, locals())
            join(nc, sb, pb, sem, locals())
        x2_out = nc.dram_tensor("x2", (NP, F), F32).ap()
        slots = nc.dram_tensor("slots", (TT * P, F), F32).ap()
        made = nc.dram_tensor("made", (TT * P, F), F32).ap()
        yn_all = acc[:].rearrange("p a n -> p (a n)").rearrange("p (b f) -> p b f", f=F)
        ew = sb("ew", [P, 3, NEXP, 2, F])
        eb = sb("eb", [P, 2, NEXP, 2])
        eb3b = sb("eb3b", [P, NEXP, F])
        logits = sb("logits", [P, NB, NEXP])
        weight = sb("weight", [P, NB, 2])
        place = sb("place", [P, NB, 2], I32)
        owner = sb("owner", [1, TT + 4], I32)
        front(nc, sb, pb, sem, locals())
        dispatch(nc, sb, pb, sem, locals())
        experts(nc, sb, pb, sem, locals())
        combine(nc, sb, pb, sem, locals())


def prepare(nc, sb, pb, sem, v):
    ident, sep, same = v["ident"], v["sep"], v["same"]
    begins, ends_sep, ends_same, fix_rows = v["begins"], v["ends_sep"], v["ends_same"], v["fix_rows"]
    src_sb, rel, islast, first_sb = v["src_sb"], v["rel"], v["islast"], v["first_sb"]
    row_iota, hsel = v["row_iota"], v["hsel"]
    wext, wedge, gbias = v["wext"], v["wedge"], v["gbias"]
    wq, bq, vw, bvw, cst = v["wq"], v["bq"], v["vw"], v["bvw"], v["cst"]
    with ExitStack() as ctx:
        def tmp(name, shape, dt=F32):
            return sb(name, shape, dt, ctx)

        dst_sb = tmp("dst_sb", [P, T], I32)
        first_b = tmp("first_b", [P, T], I32)
        last_b = tmp("last_b", [P, T], I32)
        dg = tmp("dg", [P, NG, P], I32)
        pcol = tmp("pcol", [P, 1], I32)
        bits = tmp("bits", [P, 3], I32)
        bitsf = tmp("bitsf", [P, 4])
        irow = tmp("irow", [P, P], I32)
        ihead = tmp("ihead", [P, 2, P], I32)
        headf = tmp("headf", [P, 2, P])
        att = tmp("att", [P, 6, F])
        we = tmp("we", [P, 2, F])
        prod = tmp("prod", [P, 2, F])
        we_h = tmp("we_h", [P, 2, H])
        bmask = tmp("bmask", [P, H])
        means = tmp("means", [P, 4])
        wv = tmp("wv", [P, 2, F])
        wvT = tmp("wvT", [P, 2, F])
        wo = tmp("wo", [P, 2, F])
        bv = tmp("bv", [P, 2])
        bvb = tmp("bvb", [P, 2, P])
        ones = tmp("ones", [P, P])
        bo = tmp("bo", [P, F])
        tp = pb("prep_t", [P, 512], ctx)
        mm0 = pb("prep_m0", [P, 512], ctx)
        mm1 = pb("prep_m1", [P, 512], ctx)
        s_in = sem("prep_in", ctx)
        s_iota = sem("prep_iota", ctx)
        s_same = sem("prep_same", ctx)
        s_sep = sem("prep_sep", ctx)
        s_ready = sem("prep_ready", ctx)
        s_t = sem("prep_transposed", ctx)
        s_tc = sem("prep_copied", ctx)
        s_mm = sem("prep_product", ctx)
        ctx.callback(clear_semaphores, nc, [s_in, s_iota, s_same, s_sep, s_ready, s_t, s_tc, s_mm])
        block = ctx.enter_context(nc.Block())
        loads = []

        def load(to, of):
            loads.append((to, of))

        load(dst_sb[:], v["dst_t"])
        load(src_sb[:], v["src_t"])
        load(first_b[:], v["first_row"].broadcast_to((P, T)))
        load(last_b[:], v["last_row"].broadcast_to((P, T)))
        load(first_sb[:], v["first_row"])
        for b in range(NFIX):
            n = min(P, T - b * P)
            load(fix_rows[0:n, b:b + 1], v["first_row"][:, b * P:b * P + n].rearrange("a p -> p a"))
        for k in range(GT):
            load(dg[H * k:H * k + H], v["dst_g"][:, k, :].unsqueeze(0).broadcast_to((H, NG, P)))
        for l in range(2):
            W, a_s, a_d, W_e, a_e = ((v[f"{n}{l + 1}"]) for n in ("W", "as", "ad", "We", "ae"))
            load(wext[:, :, l, 0:F], W.rearrange("(a p) f -> p a f", p=P))
            for j, a in enumerate((a_s, a_d, a_e)):
                load(att[:, 3 * l + j, :], a.rearrange("(a h) c -> a (h c)", a=1).broadcast_to((P, F)))
            for b in range(H):
                load(we[D_EDGE * b:D_EDGE * b + D_EDGE, l, :], W_e)
            for a in range(2):
                load(gbias[:, l, a:a + 1], v[f"b{l + 1}"].rearrange("(a p b) -> a p b", p=P, b=1)[a])
        Wqkv, bqkv = v["Wqkv"], v["bqkv"].rearrange("(a f) -> a f", a=1)
        load(wq[:], Wqkv[:, 0:F].rearrange("(a p) f -> p a f", p=P))
        load(bq[:], bqkv[:, 0:F].broadcast_to((P, F)))
        load(wv[:], Wqkv[:, 2 * F:3 * F].rearrange("(a p) f -> p a f", p=P))
        load(wo[:], v["Wout"].rearrange("(a p) f -> p a f", p=P))
        load(bo[:], v["bout"].rearrange("(a f) -> a f", a=1).broadcast_to((P, F)))
        for a in range(2):
            load(bv[:, a:a + 1], v["bqkv"].rearrange("(a p b) -> a p b", p=P, b=1)[4 + a])

        @block.sync
        def _(sp):
            for to, of in loads[0::2]:
                sp.dma_start(to, of).then_inc(s_in, 16)

        @block.scalar
        def _(act):
            for to, of in loads[1::2]:
                act.dma_start(to, of).then_inc(s_in, 16)

        @block.gpsimd
        def _(pool):
            nc.gpsimd.iota(pcol[:], pattern=[[0, 1]], base=0, channel_multiplier=1).then_inc(s_iota, 1)
            nc.gpsimd.iota(irow[:], pattern=[[1, P]], base=0, channel_multiplier=0).then_inc(s_iota, 1)
            nc.gpsimd.iota(ihead[:].rearrange("p a (h c) -> p a h c", c=C), pattern=[[4, 2], [1, 4], [0, C]],
                           base=0, channel_multiplier=0).then_inc(s_iota, 1)
            nc.gpsimd.memset(cst[:, 0:1], -0.5)
            nc.gpsimd.memset(cst[:, 1:2], 0.5)
            nc.gpsimd.memset(cst[:, 2:4], 0.0)
            nc.gpsimd.memset(ones[:], 1.0).then_inc(s_iota, 1)
            pool.wait_ge(s_same, 1)
            nc.gpsimd.tensor_scalar(sep[:], same[:], BIG, -BIG, ALU.mult, ALU.add).then_inc(s_sep, 1)

        @block.vector
        def _(vec):
            vec.wait_ge(s_iota, 4)
            nc.vector.tensor_single_scalar(bits[:, 0:1], pcol[:], 3, ALU.logical_shift_right)
            nc.vector.tensor_single_scalar(bits[:, 1:2], pcol[:], 7, ALU.bitwise_and)
            nc.vector.tensor_single_scalar(bits[:, 2:3], pcol[:], 4, ALU.logical_shift_right)
            nc.vector.tensor_copy(bitsf[:, 3:4], pcol[:])
            nc.vector.tensor_copy(row_iota[:], irow[:])
            nc.vector.tensor_copy(headf[:], ihead[:])
            vec.drain()
            nc.vector.tensor_copy(bitsf[:, 0:3], bits[:])
            vec.drain()
            nc.vector.tensor_scalar(ident[:], row_iota[:], bitsf[:, 3:4], None, ALU.is_equal)
            nc.vector.tensor_scalar(bmask[:], row_iota[:, 0:H], bitsf[:, 2:3], None, ALU.is_equal)
            nc.vector.tensor_scalar(hsel[:], headf[:], bitsf[:, 1:2], None, ALU.is_equal)
            vec.wait_ge(s_in, 16 * len(loads))
            nc.vector.tensor_tensor(rel[:], dst_sb[:], first_b[:], ALU.subtract)
            nc.vector.tensor_tensor(islast[:], dst_sb[:], last_b[:], ALU.is_equal)
            nc.vector.memset(same[:, :, 0:1], 0.0)
            nc.vector.memset(same[:, :, P:P + 1], 0.0)
            nc.vector.memset(v["acc"][:, :, N:NP], 0.0)
            nc.vector.memset(begins[:], 1.0)
            vec.drain()
            nc.vector.tensor_tensor(begins[:, 1:L:2], first_b[:], last_b[:], ALU.not_equal)
            nc.vector.tensor_tensor(begins[:, 2:L:2], first_b[:, 1:T], last_b[:, 0:T - 1], ALU.not_equal)
            nc.vector.tensor_tensor(same[:, :, 1:P], dg[:, :, 1:P], dg[:, :, 0:P - 1], ALU.is_equal).then_inc(s_same, 1)
            vec.drain()
            nc.vector.tensor_single_scalar(ends_sep[:], begins[:], -BIG, ALU.mult)
            nc.vector.tensor_scalar(ends_same[:], begins[:], -1.0, 1.0, ALU.mult, ALU.add)
            for l in range(2):
                for j, to in ((0, wext[:, :, l, F:F + H]), (1, wext[:, :, l, F + H:ROW])):
                    nc.vector.tensor_tensor(prod[:], wext[:, :, l, 0:F],
                                            att[:, 3 * l + j, :].unsqueeze(1).broadcast_to((P, 2, F)), ALU.mult)
                    vec.drain()
                    nc.vector.tensor_reduce(to, prod[:].rearrange("p a (h c) -> p a h c", c=C), AX.X, ALU.add)
                    vec.drain()
                nc.vector.tensor_tensor(prod[:, 0, :], we[:, l, :], att[:, 3 * l + 2, :], ALU.mult)
                vec.drain()
                nc.vector.tensor_reduce(we_h[:, l, :], prod[:, 0, :].rearrange("p (h c) -> p h c", c=C), AX.X, ALU.add)
                vec.drain()
                nc.vector.tensor_tensor(wedge[:, l], we_h[:, l, :].unsqueeze(1).broadcast_to((P, H, H)),
                                        bmask[:].unsqueeze(2).broadcast_to((P, H, H)), ALU.mult)
            nc.vector.tensor_reduce(means[:, 0:2], wq[:], AX.X, ALU.add)
            nc.vector.tensor_reduce(means[:, 2:3], bq[:], AX.X, ALU.add)
            vec.drain()
            nc.vector.tensor_single_scalar(means[:, 0:3], means[:, 0:3], 1.0 / F, ALU.mult)
            vec.drain()
            for a in range(2):
                nc.vector.tensor_scalar(wq[:, a, :], wq[:, a, :], means[:, a:a + 1], None, ALU.subtract)
            nc.vector.tensor_scalar(bq[:], bq[:], means[:, 2:3], None, ALU.subtract)
            for a in range(2):
                nc.vector.tensor_scalar(bvb[:, a, :], ones[:], bv[:, a:a + 1], None, ALU.mult)
            nc.vector.memset(means[:, 3:4], 0.0).then_inc(s_ready, 1)
            vec.wait_ge(s_t, 1)
            nc.vector.tensor_copy(wvT[:], tp[:].rearrange("p (b f) -> p b f", b=2)).then_inc(s_tc, 1)
            vec.wait_ge(s_mm, 1)
            nc.vector.tensor_copy(vw[:], mm0[:].rearrange("p (b f) -> p b f", b=2))
            nc.vector.tensor_tensor(bvw[:], mm1[:, 0:F], bo[:], ALU.add)

        @block.tensor
        def _(pe):
            pe.wait_ge(s_ready, 1)
            for b in range(2):
                for a in range(2):
                    last = nc.tensor.transpose(tp[:, b * F + a * P:b * F + a * P + P], wv[:, a, b * P:b * P + P], ident[:])
            last.then_inc(s_t, 1)
            pe.wait_ge(s_tc, 1)
            for a in range(2):
                for b in range(2):
                    nc.tensor.matmul(mm0[:, a * F:a * F + F], wvT[:, b, a * P:a * P + P], wo[:, b, :],
                                     start=(b == 0), stop=(b == 1))
            for b in range(2):
                last = nc.tensor.matmul(mm1[:, 0:F], bvb[:, b, :], wo[:, b, :], start=(b == 0), stop=(b == 1))
            last.then_inc(s_mm, 1)


def blocks(nc, sb, pb, sem, v):
    ident, wext, cst = v["ident"], v["wext"], v["cst"]
    vw, kvw, x = v["vw"], v["kvw"], v["x"]
    table = v["table"][0]
    with ExitStack() as ctx:
        def tmp(name, shape, dt=F32):
            return sb(name, shape, dt, ctx)

        wk = tmp("wk", [P, 2, F])
        bk = tmp("bk", [P, F])
        kmean = tmp("kmean", [P, 3])
        wvo = tmp("wvo", [P, 2, F])
        bvwk = tmp("bvwk", [1, F])
        bv2 = tmp("bv2", [P, 2])
        xb = tmp("xb", [P, 2, 2, F])
        xn = tmp("xn", [P, 4, 2, F + 1])
        stats = tmp("stats", [P, 2, 6])
        mv = tmp("mv", [P, 2, 2])
        rstd = tmp("rstd", [P, 2])
        epsb = tmp("epsb", [P, 2])
        xnT = tmp("xnT", [P, 2, 2 * P])
        hT = tmp("hT", [P, 2, 2 * P])
        row = tmp("row", [P, 2, 2, ROW])
        kc = tmp("kc", [P, 2, F])
        k2 = tmp("k2", [P, 2, F])
        k2r = tmp("k2r", [P, 2, 2, F])
        k4 = tmp("k4", [P, 2, 2, F])
        k2s = tmp("k2s", [P, 2])
        inv = tmp("inv", [P, 2])
        nmask = tmp("nmask", [P, NB])
        inode = tmp("inode", [P, NB], I32)
        ones = tmp("ones_b", [P, 1])
        norm = tmp("norm", [P, 2])
        kxs = tmp("kxs", [P, 2, F + 1])
        kxT = tmp("kxT", [P, 2, F])
        ksT = tmp("ksT", [1, F])
        turn = pb("turn", [P, 512], ctx)
        ps_row = [pb(f"ps_row{b}", [P, 512], ctx) for b in range(2)]
        ps_k = pb("ps_k", [P, 512], ctx)
        ps_kx = [pb(f"ps_kx{a}", [P, 512], ctx) for a in range(2)]
        ps_end = pb("ps_end", [P, 512], ctx)
        names = ("w_in", "x0", "x1", "mv", "rstd", "xn", "turned", "copied", "rectified", "row", "rowc", "k", "kc", "k2", "k2r",
                 "kx", "out0", "out1", "setup", "fin", "fins", "finp", "mask")
        s = {n: sem("blk_" + n, ctx) for n in names}
        ctx.callback(clear_semaphores, nc, list(s.values()))
        block = ctx.enter_context(nc.Block())

        def run(eng, step):
            for n in range(5):
                step(n, n % 4, n // 2)
            with eng.Fori(1, NCH // 4 - 1) as i:
                for k in range(1, 5):
                    step(4 * i + k, k % 4, 2 * i + k // 2)
            for n in range(NCH - 4, NCH):
                step(n, n % 4, n // 2, more=n < NCH - 1)

        @block.sync
        def _(sp):
            sp.dma_start(wk[:], v["Wqkv"][:, F:2 * F].rearrange("(a p) f -> p a f", p=P)).then_inc(s["w_in"], 16)
            sp.dma_start(bk[:], v["bqkv"].rearrange("(a f) -> a f", a=1)[:, F:2 * F].broadcast_to((P, F))).then_inc(s["w_in"], 16)
            for a in range(2):
                sp.dma_start(bv2[:, a:a + 1], v["bqkv"].rearrange("(a p b) -> a p b", p=P, b=1)[4 + a]).then_inc(s["w_in"], 16)
            sp.dma_start(wvo[:], v["Wout"].rearrange("(a p) f -> p a f", p=P)).then_inc(s["w_in"], 16)

            def fetch(n, q):
                sp.wait_ge(s["xn"], n + 1)
                sp.dma_start(xb[:, q], x[bass.ds(n * CH, CH), :].rearrange("(b p) f -> p b f", p=P)).then_inc(s[f"x{q}"], 16)

            with sp.Fori(0, NCH // 2) as i:
                fetch(2 * i, 0)
                fetch(2 * i + 1, 1)
            fetch(NCH - 1, 0)

        @block.gpsimd
        def _(pool):
            nc.gpsimd.iota(inode[:], pattern=[[P, NB]], base=0, channel_multiplier=1).then_inc(s["mask"], 1)
            with pool.Fori(0, NCH) as n:
                pool.wait_ge(s["mv"], n + 1)
                nc.gpsimd.tensor_tensor(rstd[:], epsb[:], cst[:, 0:1].broadcast_to((P, 2)), ALU.pow).then_inc(s["rstd"], 1)
            pool.wait_ge(s["fin"], 1)
            nc.gpsimd.tensor_tensor(inv[:], norm[:], cst[:, 1:2].broadcast_to((P, 2)), ALU.pow).then_inc(s["finp"], 1)

        @block.vector
        def _(vec):
            vec.sem_inc(s["xn"], 2)
            nc.vector.memset(ones[:], 1.0)
            nc.vector.memset(xn[:, :, :, F:F + 1], 1.0)
            vec.wait_ge(s["mask"], 1)
            nc.vector.tensor_single_scalar(nmask[:], inode[:], N, ALU.is_lt)
            vec.wait_ge(s["w_in"], 80)
            nc.vector.tensor_reduce(kmean[:, 0:2], wk[:], AX.X, ALU.add)
            nc.vector.tensor_reduce(kmean[:, 2:3], bk[:], AX.X, ALU.add)
            vec.drain()
            nc.vector.tensor_single_scalar(kmean[:], kmean[:], 1.0 / F, ALU.mult)
            vec.drain()
            for a in range(2):
                nc.vector.tensor_scalar(wk[:, a, :], wk[:, a, :], kmean[:, a:a + 1], None, ALU.subtract)
            nc.vector.tensor_scalar(bk[:], bk[:], kmean[:, 2:3], None, ALU.subtract).then_inc(s["setup"], 1)
            vec.wait_ge(s["setup"], 1)

            def moments(q, h):
                vec.wait_ge(s[f"x{q}"], 16 * h + 16)
                for b in range(2):
                    nc.vector.bn_stats(stats[:, b, :], xb[:, q, b, :])
                vec.drain()
                for b in range(2):
                    nc.vector.bn_aggr(mv[:, b, :], stats[:, b, :])
                vec.drain()
                nc.vector.tensor_single_scalar(epsb[:], mv[:, :, 1], LN_EPS, ALU.add).then_inc(s["mv"], 1)

            def normalise(n, u):
                q = u % 2
                vec.wait_ge(s["rstd"], n + 1)
                if not isinstance(n, int) or n > 1:
                    vec.wait_ge(s["kx"], n - 1)
                for b in range(2):
                    op = nc.vector.tensor_scalar(xn[:, u, b, 0:F], xb[:, q, b, :], mv[:, b, 0:1], rstd[:, b:b + 1],
                                                 ALU.subtract, ALU.mult)
                op.then_inc(s["xn"], 1)

            def centre(n):
                vec.wait_ge(s["k"], n + 1)
                nc.vector.tensor_tensor(kc[:], ps_k[:].rearrange("p (b f) -> p b f", b=2),
                                        bk[:].unsqueeze(1).broadcast_to((P, 2, F)), ALU.add).then_inc(s["kc"], 1)

            def keys(n, q):
                vec.wait_ge(s["k2"], n + 1)
                nc.vector.tensor_single_scalar(inv[:], k2s[:], EPS_DIV, ALU.add)
                vec.drain()
                nc.vector.reciprocal(inv[:], inv[:])
                vec.drain()
                nc.vector.tensor_tensor(inv[:], inv[:], nmask[:, bass.ds(2 * n, 2)], ALU.mult)
                vec.drain()
                vec.wait_ge(s["kx"], n + 1)
                for b in range(2):
                    nc.vector.tensor_scalar(k2r[:, q, b, :], k2[:, b, :], inv[:, b:b + 1], None, ALU.mult)
                vec.drain()
                nc.vector.tensor_tensor(k4[:, q], k2r[:, q], k2r[:, q], ALU.mult).then_inc(s["k2r"], 1)

            def step(n, u, h, more=True):
                q = u % 2
                if more:
                    moments(1 - q, h + q)
                centre(n)
                if more:
                    normalise(n + 1, (u + 1) % 4)
                keys(n, q)

            moments(0, 0)
            normalise(0, 0)
            run(vec, step)
            vec.wait_ge(s["kx"], NCH + 2)
            for a in range(2):
                nc.vector.tensor_copy(norm[:, a:a + 1], ps_kx[a][:, F + 1:F + 2])
            vec.drain()
            nc.vector.sem_inc(s["fin"], 1)
            vec.wait_ge(s["finp"], 1)
            nc.vector.tensor_single_scalar(inv[:], inv[:], EPS_NORM, ALU.max)
            vec.drain()
            nc.vector.reciprocal(inv[:], inv[:])
            vec.drain()
            nc.vector.tensor_single_scalar(inv[:], inv[:], float(N) ** -0.5, ALU.mult)
            vec.drain()
            for a in range(2):
                op = nc.vector.tensor_scalar(kxs[:, a, :], ps_kx[a][:, 0:F + 1], inv[:, a:a + 1], None, ALU.mult)
            op.then_inc(s["fin"], 1)
            vec.wait_ge(s["fins"], 1)
            nc.vector.tensor_copy(kxT[:], ps_end[:].rearrange("p (b c) -> p b c", b=2))
            nc.vector.tensor_copy(ksT[:], ps_k[0:1, 0:F])
            nc.vector.tensor_copy(bvwk[:], ps_row[0][0:1, 0:F]).then_inc(s["fin"], 1)
            vec.wait_ge(s["fins"], 2)
            nc.vector.tensor_copy(kvw[:], turn[:].rearrange("p (a f) -> p a f", a=2))

        @block.scalar
        def _(act):
            def copy(n):
                act.wait_ge(s["turned"], n + 1)
                if not isinstance(n, int) or n > 0:
                    act.wait_ge(s["k"], n)
                nc.scalar.activation(xnT[:], turn[:].rearrange("p (a n) -> p a n", a=2), ACT.Copy).then_inc(s["copied"], 1)

            def rectify(n):
                act.wait_ge(s["row"], n + 1)
                nc.scalar.activation(hT[:], turn[:].rearrange("p (a n) -> p a n", a=2), ACT.Relu).then_inc(s["rectified"], 1)

            def squares(n):
                act.wait_ge(s["kc"], n + 1)
                act.wait_ge(s["k2r"], n + 1)
                for b in range(2):
                    op = nc.scalar.activation(k2[:, b, :], kc[:, b, :], ACT.Square, accum_out=k2s[:, b:b + 1])
                op.then_inc(s["k2"], 1)

            def rows(n, q, h):
                act.wait_ge(s["row"], n + 2)
                if not isinstance(h, int) or h > 0:
                    act.wait_ge(s[f"out{q}"], 16 * h)
                for b in range(2):
                    op = nc.scalar.activation(row[:, q, b, :], ps_row[b][:, 0:ROW], ACT.Copy)
                op.then_inc(s["rowc"], 1)
                act.wait_ge(s["rowc"], n + 1)
                act.dma_start(table[bass.ds(n * CH, CH), :].rearrange("(b p) f -> p b f", p=P), row[:, q]
                              ).then_inc(s[f"out{q}"], 16)

            def step(n, u, h, more=True):
                squares(n)
                if more:
                    copy(n + 1)
                rows(n, u % 2, h)
                if more:
                    rectify(n + 1)

            act.sem_inc(s["k2r"], 1)
            copy(0)
            rectify(0)
            run(act, step)
            act.wait_ge(s["out0"], 16 * (NCH // 2 + 1))
            act.wait_ge(s["out1"], 16 * (NCH // 2))

        @block.tensor
        def _(pe):
            def turns(n, u):
                pe.wait_ge(s["xn"], n + 3)
                if not isinstance(n, int) or n > 0:
                    pe.wait_ge(s["rectified"], n)
                for a in range(2):
                    for b in range(2):
                        op = nc.tensor.transpose(turn[:, a * CH + b * P:a * CH + b * P + P], xn[:, u, b, a * P:a * P + P], ident[:])
                op.then_inc(s["turned"], 1)

            def key_products(n):
                pe.wait_ge(s["copied"], n + 1)
                if not isinstance(n, int) or n > 0:
                    pe.wait_ge(s["kc"], n)
                for b in range(2):
                    for a in range(2):
                        op = nc.tensor.matmul(ps_k[:, b * F:b * F + F], xnT[:, a, b * P:b * P + P], wk[:, a, :],
                                              start=(a == 0), stop=(a == 1))
                op.then_inc(s["k"], 1)

            def row_products(n):
                pe.wait_ge(s["rectified"], n + 1)
                if not isinstance(n, int) or n > 0:
                    pe.wait_ge(s["rowc"], n)
                for b in range(2):
                    for a in range(2):
                        op = nc.tensor.matmul(ps_row[b][:, 0:ROW], hT[:, a, b * P:b * P + P], wext[:, a, 0, :],
                                              start=(a == 0), stop=(a == 1))
                op.then_inc(s["row"], 1)

            def sums(n, u, first=False, end=False):
                pe.wait_ge(s["k2r"], n + 2)
                for b in range(2):
                    for a in range(2):
                        nc.tensor.matmul(ps_kx[a][:, 0:F + 1], k2r[:, u % 2, b, a * P:a * P + P], xn[:, u, b, :],
                                         start=first and b == 0, stop=end and b == 1, skip_group_check=True)
                        op = nc.tensor.matmul(ps_kx[a][:, F + 1:F + 2], k4[:, u % 2, b, a * P:a * P + P], ones[:], start=False,
                                              stop=end and b == 1, skip_group_check=True)
                op.then_inc(s["kx"], 1)

            def step(n, u, h, more=True):
                key_products(n)
                if not isinstance(n, int) or n > 0:
                    sums(n - 1, (u + 3) % 4, first=isinstance(n, int) and n == 1)
                if more:
                    turns(n + 1, (u + 1) % 4)
                row_products(n)

            pe.sem_inc(s["kx"], 2)
            pe.sem_inc(s["row"], 1)
            pe.wait_ge(s["setup"], 1)
            turns(0, 0)
            run(pe, step)
            sums(NCH - 1, (NCH - 1) % 4, end=True)
            pe.wait_ge(s["fin"], 2)
            pe.wait_ge(s["rowc"], NCH)
            for b in range(2):
                for a in range(2):
                    nc.tensor.transpose(ps_end[:, b * F + a * P:b * F + a * P + P], kxs[:, a, b * P:b * P + P], ident[:])
            for a in range(2):
                nc.tensor.transpose(ps_k[0:1, a * P:a * P + P], kxs[:, a, F:F + 1], ident[:])
            for b in range(2):
                op = nc.tensor.matmul(ps_row[0][0:1, 0:F], bv2[:, b:b + 1], wvo[:, b, :], start=(b == 0), stop=(b == 1))
            op.then_inc(s["fins"], 1)
            pe.wait_ge(s["fin"], 3)
            for a in range(2):
                for b in range(2):
                    nc.tensor.matmul(turn[:, a * F:a * F + F], kxT[:, b, a * P:a * P + P], vw[:, b, :],
                                     start=(b == 0), stop=False)
                op = nc.tensor.matmul(turn[:, a * F:a * F + F], ksT[:, a * P:a * P + P], bvwk[:], start=False, stop=True)
            op.then_inc(s["fins"], 1)


def edges(nc, sb, pb, sem, v):
    layer = v["layer"]
    ident, acc, sep, same, ends = v["ident"], v["acc"], v["sep"], v["same"], v["ends"]
    parts, src_sb, rel, islast = v["parts"], v["src_sb"], v["rel"], v["islast"]
    first_sb, row_iota, wedge = v["first_sb"], v["row_iota"], v["wedge"]
    table = v["table"][layer]
    with ExitStack() as ctx:
        def tmp(name, shape, dt=F32):
            return sb(f"e{layer}_{name}", shape, dt, ctx)

        idx = tmp("idx", [P, 2, GT], I32)
        rows = [tmp(f"rows{q}", [P, GT, ROW]) for q in range(2)]
        win = tmp("win", [P, 2, GT, H])
        eattr = tmp("eattr", [P, 2, 2, P])
        hot = tmp("hot", [P, 2, GT, WIN])
        hotT = tmp("hotT", [P, 4, P])
        sepg = tmp("sepg", [P, P + 1], BF16)
        al = tmp("al", [P, P])
        lr = tmp("lr", [P, P])
        peak = tmp("peak", [P, P])
        seg = tmp("seg", [P, P])
        less = tmp("less", [P, P])
        ex = tmp("ex", [P, P])
        run = tmp("run", [P, P])
        tot = tmp("tot", [P, P])
        prob = tmp("prob", [P, P])
        msg = tmp("msg", [P, 4, F])
        ps_al = pb(f"e{layer}_ps_al", [P, 512], ctx)
        ps_pr = [pb(f"e{layer}_ps_pr{q}", [P, 512], ctx) for q in range(2)]
        ps_hot = pb(f"e{layer}_ps_hot", [P, 512], ctx)
        ps_sum = [pb(f"e{layer}_ps_sum{q}", [P, 2, F], ctx) for q in range(4)]
        names = ("idx", "rows0", "rows1", "win0", "win1", "eattr0", "eattr1", "hot", "hotT", "hotTc",
                 "scores", "leaky", "turned", "less", "ex", "prob", "probT", "msg", "sum", "window", "taken")
        s = {n: sem(f"e{layer}_{n}", ctx) for n in names}
        s_on = sem(f"e{layer}_on", ctx)
        ctx.callback(clear_semaphores, nc, [*s.values(), s_on])
        block = ctx.enter_context(nc.Block())

        def plain(eng):
            eng.wait_ge(s_on, 1)


        @block.sync
        def _(sp):
            first = [sp.alloc_register(f"e{layer}_sp{k}") for k in range(GT)]

            def fetch(g, q):
                sp.wait_ge(s["scores"], g + 1)
                plain(sp)
                sp.reg_load(first, first_sb[0:1, bass.ds(g * GT, GT)])
                for k in range(GT):
                    at = sp.snap(first[k], min_val=0, max_val=N)
                    sp.dma_start(win[:, q, k, :], table[bass.ds(at, P), F + H:ROW]).then_inc(s[f"win{q}"], 16)
                sp.dma_start(eattr[:, q], v["edge_b"][:, bass.ds(g * 2, 2), :]).then_inc(s[f"eattr{q}"], 16)

            with sp.Fori(0, NG // 2) as i:
                for q in range(2):
                    fetch(2 * i + q, q)

        @block.gpsimd
        def _(pool):
            pool.sem_inc(s_on, 1)

            def gather(g, q):
                pool.wait_ge(s["msg"], 16 * g + 1)
                plain(pool)
                nc.gpsimd.tensor_copy(idx[:, q, :], src_sb[:, bass.ds(g * GT, GT)]).then_inc(s["idx"], 1)
                for k in range(GT):
                    pool.wait_ge(s["msg"], 16 * g + k + 1)
                    if k == 0:
                        pool.wait_ge(s["idx"], g + 1)
                    pool.nop(nofuse=True)
                    nc.gpsimd.indirect_dma_start(
                        out=rows[q][:, k, :], out_offset=None, in_=table,
                        in_offset=bass.IndirectOffsetOnAxis(ap=idx[:, q, k:k + 1], axis=0)).then_inc(s[f"rows{q}"], 16)

            with pool.Fori(0, NG // 2) as i:
                for q in range(2):
                    gather(2 * i + q, q)

        @block.vector
        def _(vec):
            def one_hots(g, q, r):
                if not isinstance(g, int) or g > 1:
                    vec.wait_ge(s["sum"], 16 * g + 4 * r - 12)
                plain(vec)
                nc.vector.tensor_copy(hot[:, q, 4 * r:4 * r + 4, P:P + 1],
                                      islast[:, bass.ds(g * GT + 4 * r, 4)].unsqueeze(2))
                nc.vector.tensor_tensor(hot[:, q, 4 * r:4 * r + 4, 0:P], row_iota[:].unsqueeze(1).broadcast_to((P, 4, P)),
                                        rel[:, bass.ds(g * GT + 4 * r, 4)].unsqueeze(2).broadcast_to((P, 4, P)),
                                        ALU.is_equal).then_inc(s["hot"], 1)

            def message(g, q, k):
                if k == 0:
                    vec.wait_ge(s["probT"], g + 1)
                vec.wait_ge(s["sum"], 16 * g + 16 + k - 3)
                nc.vector.tensor_tensor(
                    msg[:, k % 4, :].rearrange("p (h c) -> p h c", c=C),
                    rows[q][:, k, 0:F].rearrange("p (h c) -> p h c", c=C),
                    ps_pr[q][:, H * k:H * k + H].unsqueeze(2).broadcast_to((P, H, C)), ALU.mult).then_inc(s["msg"], 1)

            def leaky(g, q, i):
                vec.wait_ge(s["scores"], g + 3)
                vec.wait_ge(s[f"rows{q}"], 256 * i + 256)
                nc.vector.tensor_tensor(al[:].rearrange("p (k h) -> p k h", h=H),
                                        ps_al[:, 0:P].rearrange("p (k h) -> p k h", h=H), rows[q][:, :, F:F + H], ALU.add)
                vec.drain()
                nc.vector.scalar_tensor_tensor(lr[:], al[:], 0.2, al[:], ALU.mult, ALU.max).then_inc(s["leaky"], 1)

            def highest(g):
                nc.vector.tensor_copy(sepg[:], sep[:, bass.ds(g, 1), :].rearrange("p a b -> p (a b)"))
                vec.drain()
                vec.wait_ge(s["turned"], g + 1)
                nc.vector.tensor_tensor_scan(peak[:], sepg[:, 0:P], ps_al[:, P:2 * P], -BIG, ALU.add, ALU.max)
                vec.drain()

            def less_highest(g):
                nc.vector.tensor_tensor_scan(seg[:, ::-1], sepg[:, 1:P + 1][:, ::-1], peak[:, ::-1], -BIG, ALU.add, ALU.max)
                vec.drain()
                nc.vector.tensor_tensor(less[:], ps_al[:, P:2 * P], seg[:], ALU.subtract).then_inc(s["less"], 1)
                nc.vector.tensor_copy(ends[:, bass.ds(g, 1), :, 0:1].rearrange("p a b c -> p (a b c)"), seg[:, 0:P:P - 1])

            def running(g):
                vec.wait_ge(s["ex"], g + 2)
                nc.vector.tensor_tensor_scan(run[:], same[:, bass.ds(g, 1), 0:P].rearrange("p a b -> p (a b)"), ex[:],
                                             0.0, ALU.mult, ALU.add)
                vec.drain()

            def whole(g):
                nc.vector.tensor_tensor_scan(tot[:, ::-1], sepg[:, 1:P + 1][:, ::-1], run[:, ::-1], -BIG, ALU.add, ALU.max)
                vec.drain()
                nc.vector.tensor_copy(ends[:, bass.ds(g, 1), :, 1:2].rearrange("p a b c -> p (a b c)"), tot[:, 0:P:P - 1])
                nc.vector.tensor_single_scalar(run[:], tot[:], 1e-16, ALU.add)
                vec.drain()

            def inverse():
                nc.vector.reciprocal(seg[:], run[:])
                vec.drain()

            def probability(g):
                if not isinstance(g, int) or g > 0:
                    vec.wait_ge(s["probT"], g)
                nc.vector.tensor_tensor(prob[:], ex[:], seg[:], ALU.mult).then_inc(s["prob"], 1)

            def step(g, q, i, softmax=True, ahead=True):
                n, p = g + 1, 1 - q
                for k in range(GT):
                    message(g, q, k)
                    if softmax and k == 1:
                        one_hots(n, p, 3)
                    if ahead and k == 5:
                        one_hots(g + 2, q, 0)
                    if softmax and k == 6:
                        leaky(n, p, i if p == 1 else i + 1)
                    if softmax and k == 7:
                        highest(n)
                    if softmax and k == 8:
                        less_highest(n)
                    if ahead and k == 9:
                        one_hots(g + 2, q, 1)
                    if softmax and k == 10:
                        running(n)
                    if softmax and k == 11:
                        whole(n)
                    if softmax and k == 12:
                        inverse()
                    if softmax and k == 13:
                        probability(n)
                    if ahead and k == 14:
                        one_hots(g + 2, q, 2)

            vec.sem_inc(s["msg"], 32)
            vec.wait_ge(s_on, 1)
            for r in range(4):
                one_hots(0, 0, r)
            for r in range(3):
                one_hots(1, 1, r)
            leaky(0, 0, 0)
            highest(0)
            less_highest(0)
            running(0)
            whole(0)
            inverse()
            probability(0)
            with vec.Fori(0, NG // 2 - 1) as i:
                step(2 * i, 0, i)
                step(2 * i + 1, 1, i)
            step(NG - 2, 0, NG // 2 - 1, ahead=False)
            step(NG - 1, 1, NG // 2 - 1, softmax=False, ahead=False)

        @block.scalar
        def _(act):
            first = [act.alloc_register(f"e{layer}_act{k}") for k in range(GT)]

            def hot_copy(g, r):
                act.wait_ge(s["hotT"], 4 * g + r + 1)
                nc.scalar.activation(hotT[:], ps_hot[:].rearrange("p (k e) -> p k e", k=4), ACT.Copy).then_inc(s["hotTc"], 1)

            def exps(g):
                act.wait_ge(s["less"], g + 1)
                nc.scalar.activation(ex[:], less[:], ACT.Exp).then_inc(s["ex"], 1)

            def window(g, k, at):
                act.wait_ge(s["window"], 16 * g + k + 1)
                act.wait_ge(s["sum"], 16 * g + 16 + k + 1)
                plain(act)
                nc.scalar.activation(acc[:, :, bass.ds(at[k], P)], ps_sum[k % 4][:, :, 0:P], ACT.Copy).then_inc(s["window"], 1)
                nc.scalar.activation(parts[:, bass.ds(g * GT + k, 1)].rearrange("p t a b -> p (t a) b"),
                                     ps_sum[k % 4][:, :, 0:P + 1:P], ACT.Copy).then_inc(s["taken"], 1)

            def step(g, q, softmax=True, ahead=True):
                act.reg_load(first, first_sb[0:1, bass.ds(g * GT, GT)])
                at = [act.snap(first[k], min_val=0, max_val=N) for k in range(GT)]
                for k in range(GT):
                    window(g, k, at)
                    if softmax and k == 1:
                        hot_copy(g + 1, 3)
                    if softmax and k == 8:
                        exps(g + 1)
                    if ahead and k in (5, 9, 14):
                        hot_copy(g + 2, {5: 0, 9: 1, 14: 2}[k])

            act.sem_inc(s["window"], 1)
            act.sem_inc(s["taken"], 4)
            act.sem_inc(s["ex"], 1)
            for r in range(4):
                hot_copy(0, r)
            exps(0)
            for r in range(3):
                hot_copy(1, r)
            with act.Fori(0, NG // 2 - 1) as i:
                step(2 * i, 0)
                step(2 * i + 1, 1)
            step(NG - 2, 0, ahead=False)
            step(NG - 1, 1, softmax=False, ahead=False)

        @block.tensor
        def _(pe):
            def turn_hot(g, q, r):
                pe.wait_ge(s["hot"], 4 * g + r + 1)
                for k in range(4):
                    op = nc.tensor.transpose(ps_hot[:, k * P:k * P + P], hot[:, q, 4 * r + k, 0:P], ident[:])
                op.then_inc(s["hotT"], 1)

            def scores(g, q, r, i):
                if r == 0:
                    if not isinstance(g, int) or g > 0:
                        pe.wait_ge(s["less"], g)
                    pe.wait_ge(s[f"win{q}"], 256 * i + 256)
                    pe.wait_ge(s[f"eattr{q}"], 16 * i + 16)
                    for a in range(2):
                        nc.tensor.matmul(ps_al[:, 64 * a:64 * a + 64], eattr[:, q, a, :],
                                         wedge[:, layer].rearrange("p b h -> p (b h)"), start=(a == 0), stop=False,
                                         skip_group_check=True)
                pe.wait_ge(s["hotTc"], 4 * g + r + 1)
                for k in range(4):
                    m = H * (4 * r + k)
                    op = nc.tensor.matmul(ps_al[:, m:m + H], hotT[:, k, :], win[:, q, 4 * r + k, :], start=False,
                                          stop=(r == 3 and k == 3), skip_group_check=True)
                if r == 3:
                    op.then_inc(s["scores"], 1)

            def turn_alpha(g):
                pe.wait_ge(s["leaky"], g + 1)
                nc.tensor.transpose(ps_al[:, P:2 * P], lr[:], ident[:]).then_inc(s["turned"], 1)

            def turn_prob(g, q):
                pe.wait_ge(s["prob"], g + 1)
                nc.tensor.transpose(ps_pr[q][:, 0:P], prob[:], ident[:]).then_inc(s["probT"], 1)

            def total(g, q, k):
                pe.wait_ge(s["msg"], 16 * g + 32 + k + 1)
                pe.wait_ge(s["taken"], 16 * g + k + 1)
                for a in range(2):
                    op = nc.tensor.matmul(ps_sum[k % 4][:, a, 0:WIN], msg[:, k % 4, a * P:a * P + P], hot[:, q, k, :],
                                          start=(a == 0), stop=True, skip_group_check=True)
                op.then_inc(s["sum"], 1)

            def step(g, q, i, softmax=True, ahead=True):
                n, p, m, j = g + 1, 1 - q, g + 2, i + 1
                for k in range(GT):
                    total(g, q, k)
                    if softmax and k == 1:
                        turn_hot(n, p, 3)
                    if softmax and k == 2:
                        scores(n, p, 3, None)
                    if softmax and k == 6:
                        turn_alpha(n)
                    if ahead and k in (9, 10, 15):
                        scores(m, q, {9: 0, 10: 1, 15: 2}[k], j)
                    if ahead and k in (5, 9, 14):
                        turn_hot(m, q, {5: 0, 9: 1, 14: 2}[k])
                    if softmax and k == 13:
                        turn_prob(n, p)

            def ahead_of_all(g, rounds):
                for r in range(rounds):
                    turn_hot(g, g, r)
                    scores(g, g, r, 0)

            pe.sem_inc(s["sum"], 16)
            pe.sem_inc(s["scores"], 2)
            ahead_of_all(0, 4)
            turn_alpha(0)
            turn_prob(0, 0)
            ahead_of_all(1, 3)
            with pe.Fori(0, NG // 2 - 1) as i:
                step(2 * i, 0, i)
                step(2 * i + 1, 1, i)
            step(NG - 2, 0, NG // 2 - 1, ahead=False)
            step(NG - 1, 1, NG // 2 - 1, softmax=False, ahead=False)


def join(nc, sb, pb, sem, v):
    layer, acc, ends, parts = v["layer"], v["acc"], v["ends"], v["parts"]
    ident, hsel, wext, gbias, fix_rows = v["ident"], v["hsel"], v["wext"], v["gbias"], v["fix_rows"]
    begins, sep, same = v["begins"], v["ends_sep"], v["ends_same"]
    result = v["table"][1] if layer == 0 else v["conv"]
    WIDTH = ROW if layer == 0 else F
    FUNC = ACT.Relu if layer == 0 else ACT.Identity
    Q = L // 4
    with ExitStack() as ctx:
        def tmp(name, shape, dt=F32):
            return sb(f"j{layer}_{name}", shape, dt, ctx)

        mx = tmp("mx", [H, L])
        sm = tmp("sm", [H, L])
        fwd = tmp("fwd", [H, L])
        top = tmp("top", [H, L])
        ex, weight = fwd, mx
        inv = tmp("inv", [H, T])
        a = tmp("a", [P, L])
        b = tmp("b", [P, L])
        total = tmp("total", [P, 2, T])
        hT = tmp("hT", [P, 2, 2, CH])
        fixT = tmp("fixT", [P, 2, T])
        row = tmp("row", [P, 2, 2, WIDTH])
        fix = tmp("fix", [P, NFIX, WIDTH])
        ps = [pb(f"j{layer}_{q}", [P, 512], ctx) for q in range(4)]
        ps_row = [[pb(f"j{layer}_row{q}{k}", [P, 512], ctx) for k in range(2)] for q in range(2)]
        names = ("pick", "picked", "less", "ex", "weight", "inv", "spread", "taken", "total", "hT", "row", "rowc",
                 "out0", "out1", "fixT", "fix", "fixc", "put", "on")
        s = {n: sem(f"j{layer}_{n}", ctx) for n in names}
        block = ctx.enter_context(nc.Block())
        HALF = NCH // 2

        @block.sync
        def _(sp):
            def store(n, q):
                sp.wait_ge(s["rowc"], n + 3)
                sp.dma_start(result[bass.ds(n * CH, CH), :].rearrange("(b p) f -> p b f", p=P), row[:, q]
                             ).then_inc(s[f"out{q}"], 16)

            with sp.Fori(0, HALF) as i:
                store(2 * i, 0)
                store(2 * i + 1, 1)
            store(NCH - 1, 0)

        @block.gpsimd
        def _(pool):
            pool.wait_ge(s["out0"], 16 * (HALF + 1))
            pool.wait_ge(s["out1"], 16 * HALF)
            for f in range(NFIX):
                n = min(P, T - f * P)
                pool.wait_ge(s["fixc"], f + 1)
                nc.gpsimd.indirect_dma_start(
                    out=result, out_offset=bass.IndirectOffsetOnAxis(ap=fix_rows[0:n, f:f + 1], axis=0),
                    in_=fix[0:n, f, :], in_offset=None).then_inc(s["put"], 16)
            pool.wait_ge(s["put"], 16 * NFIX)

        @block.tensor
        def _(pe):
            def pick(what, f):
                n = 4 * what + f
                if n >= 4:
                    pe.wait_ge(s["picked"], n - 3)
                for k in range(4):
                    m = H * (4 * f + k)
                    op = nc.tensor.matmul(ps[f][0:H, 2 * NG * k:2 * NG * k + 2 * NG], ident[:, m:m + H], ends[:, :, :, what],
                                          start=True, stop=True, skip_group_check=True)
                op.then_inc(s["pick"], 1)

            def spread(of, half, f, bank):
                nc.tensor.matmul(ps[bank][:, 0:Q], hsel[0:H, half, :], of[:, f * Q:f * Q + Q], start=True, stop=True
                                 ).then_inc(s["spread"], 1)

            def project(n, q):
                pe.wait_ge(s["hT"], n + 1)
                pe.wait_ge(s["rowc"], n + 1)
                for k in range(2):
                    for h in range(2):
                        if layer == 0:
                            op = nc.tensor.matmul(ps_row[q][k][:, 0:ROW], hT[:, q, h, k * P:k * P + P], wext[:, h, 1, :],
                                                  start=(h == 0), stop=(h == 1))
                        else:
                            op = nc.tensor.transpose(ps_row[q][k][:, h * P:h * P + P], hT[:, q, h, k * P:k * P + P], ident[:])
                op.then_inc(s["row"], 1)

            pe.sem_inc(s["row"], 2)
            for what in range(2):
                for f in range(4):
                    pick(what, f)

            def projects(i0, i1):
                with pe.Fori(i0, i1) as i:
                    project(2 * i, 0)
                    project(2 * i + 1, 1)

            def spreads(half):
                for f in range(4):
                    pe.wait_ge(s["taken" if half else "picked"], f + 1 if half else f + 5)
                    spread(weight, half, f, f)

            projects(0, 3)
            pe.wait_ge(s["weight"], 1)
            spreads(0)
            projects(3, 5)
            spreads(1)
            projects(5, 9)
            pe.wait_ge(s["inv"], 1)
            for half in range(2):
                for f in range(2):
                    pe.wait_ge(s["taken"], 4 + 2 * half + f + 1)
                    spread(inv, half, f, 2 * half + f)
            projects(9, HALF)
            project(NCH - 1, 0)
            for f in range(NFIX):
                n = min(P, T - f * P)
                if f == 0:
                    pe.wait_ge(s["fixT"], 1)
                slot, k = divmod(f % 4, 2)
                pe.wait_ge(s["rowc"], NCH + 2)
                if f >= 4:
                    pe.wait_ge(s["fixc"], f - 3)
                for h in range(2):
                    if layer == 0:
                        op = nc.tensor.matmul(ps_row[slot][k][0:n, 0:ROW], fixT[:, h, f * P:f * P + n], wext[:, h, 1, :],
                                              start=(h == 0), stop=(h == 1))
                    else:
                        op = nc.tensor.transpose(ps_row[slot][k][0:n, h * P:h * P + P], fixT[:, h, f * P:f * P + n], ident[:])
                op.then_inc(s["fix"], 1)

        @block.scalar
        def _(act):
            def entries(t):
                return t.rearrange("p (g f k e) -> p f k g e", g=NG, f=4, k=4)

            def picked(what, f):
                act.wait_ge(s["pick"], 4 * what + f + 1)
                nc.scalar.activation(entries((mx, sm)[what][:])[:, f],
                                     ps[f][0:H, 0:Q].rearrange("p (k g e) -> p k g e", k=4, e=2), ACT.Copy
                                     ).then_inc(s["picked"], 1)

            def biased(n, q):
                act.wait_ge(s["row"], n + 1)
                act.wait_ge(s["on"], 1)
                for h in range(2):
                    op = nc.scalar.activation(hT[:, q, h, :], acc[:, h, bass.ds(n * CH, CH)], FUNC,
                                              bias=gbias[:, layer, h:h + 1])
                op.then_inc(s["hT"], 1)

            def rows(n, q, i):
                act.wait_ge(s["row"], n + 3)
                if not isinstance(i, int) or i > 0:
                    act.wait_ge(s[f"out{q}"], 16 * i)
                for k in range(2):
                    op = nc.scalar.activation(row[:, q, k, :], ps_row[q][k][:, 0:WIDTH], ACT.Copy)
                op.then_inc(s["rowc"], 1)

            def pair(i):
                biased(2 * i + 1, 1)
                rows(2 * i, 0, i)
                biased(2 * i + 2, 0)
                rows(2 * i + 1, 1, i)

            act.sem_inc(s["on"], 1)
            act.sem_inc(s["rowc"], 2)
            for what in range(2):
                for f in range(4):
                    picked(what, f)
            biased(0, 0)
            pair(0)
            act.wait_ge(s["less"], 1)
            nc.scalar.activation(ex[:], top[:], ACT.Exp).then_inc(s["ex"], 1)
            with act.Fori(1, HALF) as i:
                pair(i)
            rows(NCH - 1, 0, HALF)
            for h in range(2):
                act.wait_ge(s["total"], h + 1)
                op = nc.scalar.activation(fixT[:, h, :], total[:, h, :], FUNC, bias=gbias[:, layer, h:h + 1])
            op.then_inc(s["fixT"], 1)
            for f in range(NFIX):
                n = min(P, T - f * P)
                slot, k = divmod(f % 4, 2)
                act.wait_ge(s["fix"], f + 1)
                nc.scalar.activation(fix[0:n, f, :], ps_row[slot][k][0:n, 0:WIDTH], ACT.Copy).then_inc(s["fixc"], 1)

        @block.vector
        def _(vec):
            vec.wait_ge(s["picked"], 4)
            nc.vector.tensor_tensor_scan(fwd[:], sep[0:H, 0:L], mx[:], -BIG, ALU.add, ALU.max)
            vec.drain()
            nc.vector.tensor_tensor_scan(top[:, ::-1], sep[0:H, 1:L + 1][:, ::-1], fwd[:, ::-1], -BIG, ALU.add, ALU.max)
            vec.drain()
            nc.vector.tensor_tensor(top[:], mx[:], top[:], ALU.subtract).then_inc(s["less"], 1)
            vec.wait_ge(s["picked"], 8)
            vec.wait_ge(s["ex"], 1)
            nc.vector.tensor_tensor(weight[:], ex[:], sm[:], ALU.mult)
            vec.drain()
            nc.vector.tensor_tensor(weight[:, 1:L:2], weight[:, 1:L:2], begins[0:H, 1:L:2], ALU.mult).then_inc(s["weight"], 1)
            vec.wait_ge(s["weight"], 1)
            nc.vector.tensor_tensor_scan(fwd[:], same[0:H, 0:L], weight[:], 0.0, ALU.mult, ALU.add)
            vec.drain()
            nc.vector.tensor_tensor_scan(top[:, ::-1], sep[0:H, 1:L + 1][:, ::-1], fwd[:, ::-1], -BIG, ALU.add, ALU.max)
            vec.drain()
            nc.vector.tensor_single_scalar(inv[:], top[:, 0:L:2], 1e-16, ALU.add)
            vec.drain()
            nc.vector.reciprocal(inv[:], inv[:]).then_inc(s["inv"], 1)
            for half in range(2):
                for f in range(4):
                    vec.wait_ge(s["spread"], 4 * half + f + 1)
                    nc.vector.tensor_tensor(
                        a[:, f * Q:f * Q + Q].rearrange("p (t e) -> p t e", e=2),
                        ps[f][:, 0:Q].rearrange("p (t e) -> p t e", e=2),
                        parts[:, f * Q // 2:f * Q // 2 + Q // 2, half, :], ALU.mult).then_inc(s["taken"], 1)
                vec.drain()
                nc.vector.tensor_tensor_scan(b[:], same[:, 0:L], a[:], 0.0, ALU.mult, ALU.add)
                vec.drain()
                nc.vector.tensor_tensor(b[:], b[:], begins[:, 1:L + 1], ALU.mult)
                vec.drain()
                nc.vector.tensor_tensor_scan(a[:, ::-1], same[:, 1:L + 1][:, ::-1], b[:, ::-1], 0.0, ALU.mult, ALU.add)
                vec.drain()
                nc.vector.tensor_copy(total[:, half, :], a[:, 0:L:2])
                vec.drain()
            for half in range(2):
                for f in range(2):
                    vec.wait_ge(s["spread"], 8 + 2 * half + f + 1)
                    op = nc.vector.tensor_tensor(total[:, half, f * Q:f * Q + Q], total[:, half, f * Q:f * Q + Q],
                                                 ps[2 * half + f][:, 0:Q], ALU.mult)
                op.then_inc(s["total"], 1)


def run_chunks(eng, step):
    for n in range(-2, 5):
        step(n, 0, n)
    with eng.Fori(1, NCH // 4 - 1) as i:
        for k in range(1, 5):
            step(4 * i + k, i, k)
    for n in range(NCH - 4, NCH + 2):
        step(n, 0, n)


def there(n):
    return not isinstance(n, int) or 0 <= n < NCH


def front(nc, sb, pb, sem, v):
    ident, cst, wq, bq, vw, bvw, kvw = (v[k] for k in ("ident", "cst", "wq", "bq", "vw", "bvw", "kvw"))
    yn_all, logits, x, conv, x2_out, slots = (v[k] for k in ("yn_all", "logits", "x", "conv", "x2_out", "slots"))
    ew, eb, eb3 = v["ew"], v["eb"], v["eb3b"]
    with ExitStack() as ctx:
        def tmp(name, shape, dt=F32):
            return sb("f_" + name, shape, dt, ctx)

        rw1 = tmp("rw1", [P, 2, P])
        rb1 = tmp("rb1", [P, 1])
        rw2 = tmp("rw2", [P, NEXP])
        rb2 = tmp("rb2", [P, NEXP])
        zero = tmp("zero", [P, F])
        spare = v["parts"][:].rearrange("p t a b -> p (t a b)")
        xb, cb, yn = (spare[:, h * 4 * F:(h + 1) * 4 * F].rearrange("p (q b f) -> p q b f", q=2, b=2) for h in range(3))
        xn = tmp("xn", [P, 2, F])
        stats = tmp("stats", [P, 2, 6])
        mv = tmp("mv", [P, 2, 2, 2])
        eps = tmp("eps", [P, 2, 2])
        rstd = tmp("rstd", [P, 2, 2])
        xnT = tmp("xnT", [P, 2, 2, CH])
        qc = tmp("qc", [P, 2, F])
        q2 = tmp("q2", [P, 2, F])
        q4 = tmp("q4", [P, 2, F])
        qs = tmp("qs", [P, 8])
        q2T = tmp("q2T", [P, 2, CH])
        x2 = tmp("x2", [P, 4, 2, F])
        yT = tmp("yT", [P, 2, CH])
        rhT = tmp("rhT", [P, CH])
        ps_x, ps_q2, ps_y, ps_q, ps_m, ps_r = (pb("f_ps_" + n, [P, 512], ctx) for n in ("x", "q2", "y", "q", "m", "r"))
        names = ("w_in", "small", "zero", "x0", "x1", "c0", "c1", "x20", "x21", "x22", "x23", "eps", "rstd", "eps2", "rstd2", "xn",
                 "xt", "xtc", "base", "q", "qc", "qss", "qsr", "q2n", "qt", "qtc", "mix", "x2", "yn", "yt", "ytc", "rh",
                 "rhc", "lg", "lgc", "kept")
        s = {n: sem("f_" + n, ctx) for n in names}
        block = ctx.enter_context(nc.Block())
        later = []
        for m, be in enumerate(("eb1", "eb2")):
            for e in range(NEXP):
                for a in range(2):
                    later.append((eb[:, m, e, a:a + 1], v[be].rearrange("e (a p b) -> e a p b", p=P, b=1)[e, a]))
        later += [(eb3[:], v["eb3"].rearrange("(a e) f -> a e f", a=1).broadcast_to((P, NEXP, F)))]
        small = [(rw1[:], v["rw1"].rearrange("(a p) f -> p a f", p=P)),
                 (rb1[:], v["rb1"].rearrange("(p b) -> p b", b=1)), (rw2[:], v["rw2"]),
                 (rb2[:], v["rb2"].rearrange("(a f) -> a f", a=1).broadcast_to((P, NEXP)))]

        for m, we in enumerate(("ew1", "ew2", "ew3")):
            for e in range(NEXP):
                later.append((ew[:, m, e], v[we][e].rearrange("(a p) f -> p a f", p=P)))
        for j in range(TT // 12):
            later.append((slots[j * 12 * P:(j + 1) * 12 * P, :].rearrange("(b p) f -> p b f", p=P),
                           zero[:].unsqueeze(1).broadcast_to((P, 12, F))))

        @block.sync
        def _(sp):
            def step(n, i, k):
                if isinstance(n, int) and 0 <= n < 5:
                    sp.wait_ge(s["zero"], 1)
                    for to, of in later[n::5]:
                        sp.dma_start(to, of).then_inc(s["w_in"], 16)
                if there(n + 2):
                    q, at = (k + 2) % 2, (n + 2) * CH
                    sp.wait_ge(s["base"], n + 3)
                    sp.dma_start(xb[:, q], x[bass.ds(at, CH), :].rearrange("(b p) f -> p b f", p=P)).then_inc(s[f"x{q}"], 16)
                    sp.dma_start(cb[:, q], conv[bass.ds(at, CH), :].rearrange("(b p) f -> p b f", p=P)).then_inc(s[f"c{q}"], 16)
                if there(n - 1):
                    sp.wait_ge(s["x2"], n)
                    sp.dma_start(x2_out[bass.ds((n - 1) * CH, CH), :].rearrange("(b p) f -> p b f", p=P), x2[:, (k - 1) % 4]
                                 ).then_inc(s[f"x2{(k - 1) % 4}"], 16)

            sp.sem_inc(s["base"], 2)
            run_chunks(sp, step)
            sp.wait_ge(s["w_in"], 16 * len(later))
            for u in range(4):
                sp.wait_ge(s[f"x2{u}"], 16 * (NCH // 4 + (u == 0)))

        @block.gpsimd
        def _(pool):
            nc.gpsimd.memset(zero[:], 0.0).then_inc(s["zero"], 1)

            def step(n, i, k):
                m, q, u = n + 2, (k + 2) % 2, (k + 2) % 4
                if there(m):
                    pool.wait_ge(s["eps"], m + 1)
                    nc.gpsimd.tensor_tensor(rstd[:, 0], eps[:, 0], cst[:, 0:1].broadcast_to((P, 2)), ALU.pow).then_inc(s["rstd"], 1)
                if there(n + 1):
                    pool.wait_ge(s["qss"], n + 2)
                    nc.gpsimd.tensor_tensor(qs[:, 4:6], qs[:, 2:4], cst[:, 1:2].broadcast_to((P, 2)), ALU.pow).then_inc(s["qsr"], 1)
                if there(m):
                    pool.wait_ge(s["xn"], m + 1)
                    if not isinstance(m, int):
                        pool.wait_ge(s[f"x2{u}"], 16 * (i + (k + 2) // 4))
                    elif m >= 4:
                        pool.wait_ge(s[f"x2{u}"], 16 * (m // 4))
                    nc.gpsimd.tensor_tensor(x2[:, u], xb[:, q], xn[:], ALU.add)
                    pool.drain()
                    pool.wait_ge(s[f"c{q}"], 16 * (2 * i + (k + 2) // 2) + 16)
                    nc.gpsimd.tensor_tensor(x2[:, u], x2[:, u], cb[:, q], ALU.add)
                    pool.drain()
                    nc.gpsimd.tensor_tensor(x2[:, u], x2[:, u], bvw[:].unsqueeze(1).broadcast_to((P, 2, F)), ALU.add
                                            ).then_inc(s["base"], 1)
                if there(n):
                    pool.wait_ge(s["eps2"], n + 1)
                    nc.gpsimd.tensor_tensor(rstd[:, 1], eps[:, 1], cst[:, 0:1].broadcast_to((P, 2)), ALU.pow).then_inc(s["rstd2"], 1)

            run_chunks(pool, step)

        @block.vector
        def _(vec):
            def moments(src, w, done):
                for b in range(2):
                    nc.vector.bn_stats(stats[:, b, :], src[:, b, :])
                vec.drain()
                for b in range(2):
                    nc.vector.bn_aggr(mv[:, w, b, :], stats[:, b, :])
                vec.drain()
                nc.vector.tensor_single_scalar(eps[:, w], mv[:, w, :, 1], LN_EPS, ALU.add).then_inc(s[done], 1)

            def centred(src, to, w, done):
                for b in range(2):
                    op = nc.vector.tensor_scalar(to[:, b, :], src[:, b, :], mv[:, w, b, 0:1], rstd[:, w, b:b + 1],
                                                 ALU.subtract, ALU.mult)
                op.then_inc(s[done], 1)

            def step(n, i, k):
                if there(n - 1):
                    vec.wait_ge(s["rstd2"], n)
                    if there(n - 3):
                        vec.wait_ge(s["kept"], n - 2)
                        vec.wait_ge(s["yt"], n - 2)
                    centred(x2[:, (k - 1) % 4], yn[:, (k - 1) % 2], 1, "yn")
                if there(n + 1):
                    vec.wait_ge(s["q"], n + 2)
                    nc.vector.tensor_tensor(qc[:], ps_q[:].rearrange("p (b f) -> p b f", b=2),
                                            bq[:].unsqueeze(1).broadcast_to((P, 2, F)), ALU.add).then_inc(s["qc"], 1)
                if there(n - 2):
                    vec.wait_ge(s["lg"], n - 1)
                    nc.vector.tensor_tensor(logits[:, bass.ds(2 * n - 4, 2), :],
                                            ps_r[:, CH:CH + 2 * NEXP].rearrange("p (b e) -> p b e", b=2),
                                            rb2[:].unsqueeze(1).broadcast_to((P, 2, NEXP)), ALU.add).then_inc(s["lgc"], 1)
                if there(n + 2):
                    m, q = n + 2, (k + 2) % 2
                    vec.wait_ge(s[f"x{q}"], 16 * (2 * i + (k + 2) // 2) + 16)
                    moments(xb[:, q], 0, "eps")
                if there(n + 2):
                    vec.wait_ge(s["rstd"], m + 1)
                    vec.wait_ge(s["xt"], m + 1)
                    vec.wait_ge(s["base"], m + 2)
                    centred(xb[:, q], xn, 0, "xn")
                if there(n + 1):
                    vec.wait_ge(s["qss"], n + 2)
                    nc.vector.tensor_single_scalar(qs[:, 0:2], qs[:, 0:2], EPS_DIV, ALU.add)
                    vec.drain()
                    nc.vector.reciprocal(qs[:, 6:8], qs[:, 0:2])
                    vec.drain()
                    vec.wait_ge(s["qsr"], n + 2)
                    nc.vector.tensor_tensor(qs[:, 4:6], qs[:, 4:6], qs[:, 6:8], ALU.mult)
                    vec.drain()
                    nc.vector.tensor_single_scalar(qs[:, 4:6], qs[:, 4:6], EPS_NORM, ALU.max)
                    vec.drain()
                    nc.vector.reciprocal(qs[:, 4:6], qs[:, 4:6])
                    vec.drain()
                    nc.vector.tensor_tensor(qs[:, 4:6], qs[:, 4:6], qs[:, 6:8], ALU.mult)
                    vec.drain()
                    for b in range(2):
                        op = nc.vector.tensor_scalar(q2[:, b, :], q2[:, b, :], qs[:, 4 + b:5 + b], None, ALU.mult)
                    op.then_inc(s["q2n"], 1)
                if there(n):
                    u = k % 4
                    vec.wait_ge(s["mix"], n + 1)
                    vec.wait_ge(s["base"], n + 3)
                    nc.vector.tensor_tensor(x2[:, u], ps_m[:].rearrange("p (b f) -> p b f", b=2), x2[:, u], ALU.add
                                            ).then_inc(s["x2"], 1)
                    vec.wait_ge(s["x2"], n + 1)
                    moments(x2[:, u], 1, "eps2")

            vec.wait_ge(s["small"], 16 * len(small))
            run_chunks(vec, step)

        @block.scalar
        def _(act):
            def turned(ps, to, wait, at, done):
                act.wait_ge(s[wait], at)
                nc.scalar.activation(to, ps[:].rearrange("p (a m) -> p a m", a=2), ACT.Copy).then_inc(s[done], 1)

            def step(n, i, k):
                if there(n):
                    turned(ps_q2, q2T[:], "qt", n + 1, "qtc")
                if there(n + 1):
                    act.wait_ge(s["qc"], n + 2)
                    if there(n):
                        act.wait_ge(s["qt"], n + 1)
                    for b in range(2):
                        nc.scalar.activation(q2[:, b, :], qc[:, b, :], ACT.Square, accum_out=qs[:, b:b + 1])
                    act.drain()
                    for b in range(2):
                        op = nc.scalar.activation(q4[:, b, :], q2[:, b, :], ACT.Square, accum_out=qs[:, 2 + b:3 + b])
                    op.then_inc(s["qss"], 1)
                if there(n + 2):
                    if there(n):
                        act.wait_ge(s["mix"], n + 1)
                    turned(ps_x, xnT[:, k % 2], "xt", n + 4, "xtc")
                if there(n - 1):
                    turned(ps_y, yT[:], "yt", n, "ytc")
                    nc.scalar.activation(yn_all[:, bass.ds(2 * n - 2, 2), :], yn[:, (k - 1) % 2], ACT.Copy).then_inc(s["kept"], 1)
                    act.wait_ge(s["rh"], n)
                    nc.scalar.activation(rhT[:], ps_r[:, 0:CH], ACT.Relu, bias=rb1[:]).then_inc(s["rhc"], 1)

            for to, of in small:
                act.dma_start(to, of).then_inc(s["small"], 16)
            act.wait_ge(s["small"], 16 * len(small))
            run_chunks(act, step)

        @block.tensor
        def _(pe):
            def turn(of, ps, done):
                for a in range(2):
                    for b in range(2):
                        op = nc.tensor.transpose(ps[:, a * CH + b * P:a * CH + b * P + P], of[:, b, a * P:a * P + P], ident[:])
                op.then_inc(s[done], 1)

            def step(n, i, k):
                if there(n):
                    pe.wait_ge(s["q2n"], n + 1)
                    pe.wait_ge(s["qtc"], n + 1)
                    turn(q2, ps_q2, "qt")
                if there(n - 2):
                    pe.wait_ge(s["rhc"], n - 1)
                    for b in range(2):
                        op = nc.tensor.matmul(ps_r[:, CH + b * NEXP:CH + b * NEXP + NEXP], rhT[:, b * P:b * P + P], rw2[:],
                                              start=True, stop=True)
                    op.then_inc(s["lg"], 1)
                if there(n + 1):
                    pe.wait_ge(s["xtc"], n + 3)
                    if there(n):
                        pe.wait_ge(s["qc"], n + 1)
                    for b in range(2):
                        for a in range(2):
                            op = nc.tensor.matmul(ps_q[:, b * F:b * F + F], xnT[:, (k + 1) % 2, a, b * P:b * P + P],
                                                  wq[:, a, :], start=(a == 0), stop=(a == 1))
                    op.then_inc(s["q"], 1)
                if there(n):
                    pe.wait_ge(s["qtc"], n + 2)
                    if there(n - 1):
                        pe.wait_ge(s["x2"], n)
                    for b in range(2):
                        for a in range(2):
                            nc.tensor.matmul(ps_m[:, b * F:b * F + F], xnT[:, k % 2, a, b * P:b * P + P], vw[:, a, :],
                                             start=(a == 0), stop=False)
                        for a in range(2):
                            op = nc.tensor.matmul(ps_m[:, b * F:b * F + F], q2T[:, a, b * P:b * P + P], kvw[:, a, :],
                                                  start=False, stop=(a == 1))
                    op.then_inc(s["mix"], 1)
                if there(n + 2):
                    pe.wait_ge(s["xn"], n + 3)
                    pe.wait_ge(s["xtc"], n + 3)
                    turn(xn, ps_x, "xt")
                if there(n - 1):
                    pe.wait_ge(s["yn"], n)
                    pe.wait_ge(s["ytc"], n)
                    turn(yn[:, (k - 1) % 2], ps_y, "yt")
                if there(n - 1):
                    pe.wait_ge(s["ytc"], n + 1)
                    if there(n - 2):
                        pe.wait_ge(s["lgc"], n - 1)
                    for a in range(2):
                        op = nc.tensor.matmul(ps_r[:, 0:CH], rw1[:, a, :], yT[:, a, :], start=(a == 0), stop=(a == 1))
                    op.then_inc(s["rh"], 1)

            pe.sem_inc(s["qtc"], 1)
            pe.sem_inc(s["xtc"], 1)
            pe.sem_inc(s["ytc"], 1)
            pe.sem_inc(s["xt"], 1)
            pe.wait_ge(s["small"], 16 * len(small))
            run_chunks(pe, step)


def dispatch(nc, sb, pb, sem, v):
    row_iota, logits, yn_all, slots = (v[k] for k in ("row_iota", "logits", "yn_all", "slots"))
    weight, place, owner = v["weight"], v["place"], v["owner"]
    with ExitStack() as ctx:
        def tmp(name, shape, dt=F32):
            return sb("d_" + name, shape, dt, ctx)

        top = tmp("top", [P, NB, 8])
        prob = tmp("prob", [P, NB, 8])
        at8 = tmp("at8", [P, NB, 8], U32)
        atf = tmp("atf", [P, NB, 8])
        a1 = tmp("a1", [P, NB])
        a2 = tmp("a2", [P, NB])
        sel = tmp("sel", [P, 2, NB, NEXP])
        both = tmp("both", [P, NB, NEXP])
        below = tmp("below", [P, P])
        ones = tmp("ones", [P, P])
        pcol = tmp("pcol", [P, 1], I32)
        pcolf = tmp("pcolf", [P, 1])
        pos = tmp("pos", [P, NB, NEXP])
        upto = tmp("upto", [P, NEXP, NB])
        tiles = tmp("tiles", [P, NEXP], I32)
        tilesf = tmp("tilesf", [P, NEXP])
        ends = tmp("ends", [P, NEXP])
        onb = tmp("onb", [P, NB])
        pick = tmp("pick", [P, NB, NEXP])
        placef = tmp("placef", [P, NB, 2])
        it = tmp("it", [P, TT + 4], I32)
        itf = tmp("itf", [P, TT + 4])
        past = tmp("past", [P, TT + 4, NEXP - 1])
        ownf = tmp("ownf", [P, TT + 4])
        ps_before = pb("d_before", [P, 512], ctx)
        ps_block = pb("d_block", [P, 512], ctx)
        s_iota, s_less, s_ex, s_gap, s_e, s_both, s_ps, s_place, s_put = (
            sem("d_" + n, ctx) for n in ("iota", "less", "ex", "gap", "e", "both", "ps", "place", "put"))
        block = ctx.enter_context(nc.Block())

        @block.gpsimd
        def _(pool):
            nc.gpsimd.iota(pcol[:], pattern=[[0, 1]], base=0, channel_multiplier=1).then_inc(s_iota, 1)
            nc.gpsimd.iota(it[:], pattern=[[1, TT + 4]], base=0, channel_multiplier=0).then_inc(s_iota, 1)
            pool.wait_ge(s_place, 1)
            for b in range(NB):
                for j in range(2):
                    nc.gpsimd.indirect_dma_start(
                        out=slots, out_offset=bass.IndirectOffsetOnAxis(ap=place[:, b, j:j + 1], axis=0),
                        in_=yn_all[:, b, :], in_offset=None).then_inc(s_put, 16)
            pool.wait_ge(s_put, 16 * 2 * NB)

        @block.scalar
        def _(act):
            act.wait_ge(s_less, 1)
            nc.scalar.activation(prob[:, :, 0:NEXP], logits[:], ACT.Exp).then_inc(s_ex, 1)
            act.wait_ge(s_gap, 1)
            nc.scalar.activation(a2[:], a1[:], ACT.Exp).then_inc(s_e, 1)

        @block.tensor
        def _(pe):
            pe.wait_ge(s_both, 1)
            nc.tensor.matmul(ps_before[:, 0:NB * NEXP], below[:], both[:].rearrange("p b e -> p (b e)"), start=True, stop=True)
            nc.tensor.matmul(ps_block[:, 0:NB * NEXP], ones[:], both[:].rearrange("p b e -> p (b e)"), start=True, stop=True
                             ).then_inc(s_ps, 1)

        @block.vector
        def _(vec):
            nc.vector.memset(prob[:, :, NEXP:8], -1.0)
            nc.vector.memset(ones[:], 1.0)
            nc.vector.memset(onb[:], 1.0)
            nc.vector.tensor_reduce(a1[:], logits[:], AX.X, ALU.max)
            vec.drain()
            nc.vector.tensor_tensor(logits[:], logits[:], a1[:].unsqueeze(2).broadcast_to((P, NB, NEXP)), ALU.subtract
                                    ).then_inc(s_less, 1)
            vec.wait_ge(s_iota, 2)
            nc.vector.tensor_copy(pcolf[:], pcol[:])
            nc.vector.tensor_copy(itf[:], it[:])
            vec.drain()
            nc.vector.tensor_scalar(below[:], row_iota[:], pcolf[:], None, ALU.is_gt)
            vec.wait_ge(s_ex, 1)
            nc.vector.tensor_reduce(a1[:], prob[:, :, 0:NEXP], AX.X, ALU.add)
            vec.drain()
            nc.vector.reciprocal(a1[:], a1[:])
            vec.drain()
            nc.vector.tensor_tensor(prob[:, :, 0:NEXP], prob[:, :, 0:NEXP], a1[:].unsqueeze(2).broadcast_to((P, NB, NEXP)),
                                    ALU.mult)
            vec.drain()
            for b in range(NB):
                nc.vector.max(top[:, b, :], prob[:, b, :])
            vec.drain()
            for b in range(NB):
                nc.vector.max_index(at8[:, b, :], top[:, b, :], prob[:, b, :])
            nc.vector.tensor_tensor(a1[:], top[:, :, 1], top[:, :, 0], ALU.subtract).then_inc(s_gap, 1)
            vec.drain()
            nc.vector.tensor_copy(atf[:], at8[:])
            vec.drain()
            for j in range(2):
                nc.vector.tensor_tensor(sel[:, j], row_iota[:, 0:NEXP].unsqueeze(1).broadcast_to((P, NB, NEXP)),
                                        atf[:, :, j:j + 1].broadcast_to((P, NB, NEXP)), ALU.is_equal)
            vec.drain()
            nc.vector.tensor_tensor(both[:], sel[:, 0], sel[:, 1], ALU.add).then_inc(s_both, 1)
            vec.wait_ge(s_e, 1)
            nc.vector.tensor_single_scalar(a1[:], a2[:], 1.0, ALU.add)
            vec.drain()
            nc.vector.reciprocal(weight[:, :, 0], a1[:])
            vec.drain()
            nc.vector.tensor_tensor(weight[:, :, 1], weight[:, :, 0], a2[:], ALU.mult)
            vec.wait_ge(s_ps, 1)
            blocks_of = ps_block[:, 0:NB * NEXP].rearrange("p (b e) -> p b e", e=NEXP)
            for e in range(NEXP):
                nc.vector.tensor_tensor_scan(upto[:, e, :], onb[:], blocks_of[:, :, e], 0.0, ALU.mult, ALU.add)
            vec.drain()
            nc.vector.tensor_single_scalar(tilesf[:], upto[:, :, NB - 1], float(P - 1), ALU.add)
            vec.drain()
            nc.vector.tensor_copy(tiles[:], tilesf[:])
            vec.drain()
            nc.vector.tensor_single_scalar(tiles[:], tiles[:], 7, ALU.logical_shift_right)
            vec.drain()
            nc.vector.tensor_copy(tilesf[:], tiles[:])
            vec.drain()
            nc.vector.tensor_tensor_scan(ends[:], onb[:, 0:NEXP], tilesf[:], 0.0, ALU.mult, ALU.add)
            vec.drain()
            nc.vector.tensor_tensor(tilesf[:], ends[:], tilesf[:], ALU.subtract)
            nc.vector.tensor_tensor(past[:], itf[:].unsqueeze(2).broadcast_to((P, TT + 4, NEXP - 1)),
                                    ends[:, 0:NEXP - 1].unsqueeze(1).broadcast_to((P, TT + 4, NEXP - 1)), ALU.is_ge)
            vec.drain()
            nc.vector.tensor_reduce(ownf[:], past[:], AX.X, ALU.add)
            nc.vector.tensor_single_scalar(tilesf[:], tilesf[:], float(P), ALU.mult)
            nc.vector.tensor_tensor(pos[:], upto[:].rearrange("p e b -> p b e"), blocks_of, ALU.subtract)
            vec.drain()
            nc.vector.tensor_copy(owner[:], ownf[0:1, :])
            nc.vector.tensor_tensor(pos[:], pos[:], ps_before[:, 0:NB * NEXP].rearrange("p (b e) -> p b e", e=NEXP), ALU.add)
            vec.drain()
            nc.vector.tensor_tensor(pos[:], pos[:], tilesf[:].unsqueeze(1).broadcast_to((P, NB, NEXP)), ALU.add)
            vec.drain()
            for j in range(2):
                nc.vector.tensor_tensor(pick[:], sel[:, j], pos[:], ALU.mult)
                vec.drain()
                nc.vector.tensor_reduce(placef[:, :, j], pick[:], AX.X, ALU.add)
                vec.drain()
            nc.vector.tensor_copy(place[:], placef[:]).then_inc(s_place, 1)


def experts(nc, sb, pb, sem, v):
    ident, slots, made, owner = v["ident"], v["slots"], v["made"], v["owner"]
    ew, eb, eb3 = v["ew"], v["eb"], v["eb3b"]
    with ExitStack() as ctx:
        def tmp(name, shape, dt=F32):
            return sb("x_" + name, shape, dt, ctx)

        y = tmp("y", [P, 4, F])
        w = tmp("w", [P, 2, 2, 2, F])
        yT = tmp("yT", [P, 2, 2, P])
        h1 = tmp("h1", [P, 2, P])
        h2 = tmp("h2", [P, 2, P])
        res = tmp("res", [P, 4, F])
        ps_y = [pb(f"x_y{q}", [P, 512], ctx) for q in range(2)]
        ps_1 = [pb(f"x_1{q}", [P, 512], ctx) for q in range(2)]
        ps_2 = [pb(f"x_2{q}", [P, 512], ctx) for q in range(2)]
        ps_3 = [pb(f"x_3{q}", [P, 512], ctx) for q in range(2)]
        names = ("y0", "y1", "y2", "y3", "yt", "ytc", "h1", "h1c", "h2", "h2c", "o", "oc", "out0", "out1", "out2", "out3", "w", "on")
        s = {n: sem("x_" + n, ctx) for n in names}
        block = ctx.enter_context(nc.Block())

        @block.sync
        def _(sp):
            def load(t, k):
                sp.wait_ge(s["yt"], t + 1)
                sp.dma_start(y[:, k, :], slots[bass.ds(t * P, P), :]).then_inc(s[f"y{k}"], 16)

            def store(t, k):
                sp.wait_ge(s["oc"], t + 3)
                sp.dma_start(made[bass.ds(t * P, P), :], res[:, k, :]).then_inc(s[f"out{k}"], 16)

            for k in range(4):
                load(k, k)
            with sp.Fori(1, TT // 4) as i:
                for k in range(4):
                    store(4 * i + k - 4, k)
                    load(4 * i + k, k)
            for k in range(4):
                store(TT - 4 + k, k)
            for k in range(4):
                sp.wait_ge(s[f"out{k}"], 16 * (TT // 4))

        @block.gpsimd
        def _(pool):
            pool.sem_inc(s["on"], 1)

        @block.scalar
        def _(act):
            regs = [act.alloc_register(f"x_act{k}") for k in range(4)]
            act.sem_inc(s["ytc"], 2)
            act.sem_inc(s["h1c"], 2)
            with act.Fori(0, TT // 4) as i:
                act.reg_load(regs, owner[0:1, bass.ds(4 * i, 4)])
                for k in range(4):
                    t, q = 4 * i + k, k % 2
                    e = act.snap(regs[k], min_val=0, max_val=NEXP - 1)
                    act.wait_ge(s["yt"], t + 5)
                    act.wait_ge(s["h1"], t + 1)
                    nc.scalar.activation(yT[:, q], ps_y[q][:, 0:F].rearrange("p (a m) -> p a m", a=2), ACT.Copy
                                         ).then_inc(s["ytc"], 1)
                    act.wait_ge(s["h1"], t + 3)
                    act.wait_ge(s["h2"], t + 2)
                    act.wait_ge(s["on"], 1)
                    for a in range(2):
                        op = nc.scalar.activation(h1[:, a, :], ps_1[q][:, a * P:a * P + P], ACT.Relu,
                                                  bias=eb[:, 0, bass.ds(e, 1), a:a + 1].rearrange("p e a -> p (e a)"))
                    op.then_inc(s["h1c"], 1)

        @block.vector
        def _(vec):
            regs = [vec.alloc_register(f"x_vec{k}") for k in range(6)]

            def weights(k, e):
                nc.vector.tensor_copy(w[:, k % 2].rearrange("p m a f -> p m (a f)"),
                                      ew[:, 0:2, bass.ds(e, 1)].rearrange("p m e a f -> p m (e a f)")).then_inc(s["w"], 1)

            def four(i, first):
                vec.reg_load(regs, owner[0:1, bass.ds(4 * i, 6)])
                own = [vec.snap(regs[k], min_val=0, max_val=NEXP - 1) for k in range(6)]
                if first:
                    vec.wait_ge(s["on"], 1)
                    weights(0, own[0])
                    weights(1, own[1])
                for k in range(4):
                    t, q = 4 * i + k, k % 2
                    e = own[k]
                    vec.wait_ge(s["h2"], t + 3)
                    vec.wait_ge(s["o"], t + 1)
                    vec.wait_ge(s["on"], 1)
                    for a in range(2):
                        op = nc.vector.tensor_scalar(h2[:, a, :], ps_2[q][:, a * P:a * P + P],
                                                     eb[:, 1, bass.ds(e, 1), a:a + 1].rearrange("p e a -> p (e a)"), 0.0,
                                                     ALU.add, ALU.max)
                    op.then_inc(s["h2c"], 1)
                    weights(k + 2, own[k + 2])
                    vec.wait_ge(s["o"], t + 2)
                    if not first:
                        vec.wait_ge(s[f"out{k}"], 16 * i)
                    vec.wait_ge(s["on"], 1)
                    nc.vector.tensor_tensor(res[:, k, :], ps_3[q][:, 0:F], eb3[:, bass.ds(e, 1), :].rearrange("p e f -> p (e f)"),
                                            ALU.add).then_inc(s["oc"], 1)

            vec.sem_inc(s["h2c"], 2)
            vec.sem_inc(s["oc"], 2)
            four(0, True)
            with vec.Fori(1, TT // 4) as i:
                four(i, False)

        @block.tensor
        def _(pe):
            regs = [pe.alloc_register(f"x_pe{k}") for k in range(4)]

            def turn(t, k, i):
                pe.wait_ge(s[f"y{k % 4}"], 16 * (i + k // 4) + 16)
                pe.wait_ge(s["ytc"], t + 1)
                for a in range(2):
                    op = nc.tensor.transpose(ps_y[k % 2][:, a * P:a * P + P], y[:, k % 4, a * P:a * P + P], ident[:])
                op.then_inc(s["yt"], 1)

            def products(k, m, ps, of, done):
                for a in range(2):
                    for h in range(2):
                        op = nc.tensor.matmul(ps[k % 2][:, a * P:a * P + P], w[:, k % 2, m, h, a * P:a * P + P],
                                              of[:, h, :], start=(h == 0), stop=(h == 1))
                op.then_inc(s[done], 1)

            def first(t, k):
                pe.wait_ge(s["w"], t + 1)
                pe.wait_ge(s["ytc"], t + 3)
                pe.wait_ge(s["h1c"], t + 1)
                products(k, 0, ps_1, yT[:, k % 2], "h1")

            def second(t, k):
                pe.wait_ge(s["h1c"], t + 3)
                pe.wait_ge(s["h2c"], t + 1)
                products(k, 1, ps_2, h1, "h2")

            def third(t, k, e):
                pe.wait_ge(s["h2c"], t + 3)
                pe.wait_ge(s["oc"], t + 1)
                pe.wait_ge(s["on"], 1)
                for h in range(2):
                    op = nc.tensor.matmul(ps_3[k % 2][:, 0:F], h2[:, h, :],
                                          ew[:, 2, bass.ds(e, 1), h, :].rearrange("p e f -> p (e f)"), start=(h == 0), stop=(h == 1))
                op.then_inc(s["o"], 1)

            def four(i, begin=False, end=False):
                pe.reg_load(regs, owner[0:1, bass.ds(4 * i, 4)])
                e = [pe.snap(regs[k], min_val=0, max_val=NEXP - 1) for k in range(4)]
                if begin:
                    turn(0, 0, 0)
                    turn(1, 1, 0)
                    first(0, 0)
                for k in range(4):
                    t = 4 * i + k
                    second(t, k)
                    if not end or k < 2:
                        turn(t + 2, k + 2, i)
                    if not end or k < 3:
                        first(t + 1, k + 1)
                    third(t, k, e[k])

            pe.sem_inc(s["yt"], 4)
            pe.sem_inc(s["h1"], 2)
            pe.sem_inc(s["h2"], 2)
            pe.sem_inc(s["o"], 1)
            four(0, begin=True)
            with pe.Fori(1, TT // 4 - 1) as i:
                four(i)
            four(TT // 4 - 1, end=True)


def combine(nc, sb, pb, sem, v):
    made, x2_out, weight, place, out = v["made"], v["x2_out"], v["weight"], v["place"], v["out"]
    BL = 5
    with ExitStack() as ctx:
        r = [sb(f"c_r{q}", [P, BL, 2, F], F32, ctx) for q in range(2)]
        idx = sb("c_idx", [P, 2, BL, 2], I32, ctx)
        x2 = sb("c_x2", [P, 2, BL, F], F32, ctx)
        w = sb("c_w", [P, 2, BL, 2], F32, ctx)
        s = {n: sem("c_" + n, ctx) for n in ("r0", "r1", "x0", "x1", "idx", "sum", "out0", "out1")}
        block = ctx.enter_context(nc.Block())

        @block.sync
        def _(sp):
            def group(n, q, i):
                if not isinstance(i, int):
                    sp.wait_ge(s[f"out{q}"], 16 * i)
                sp.dma_start(x2[:, q], x2_out[bass.ds(n * BL * P, BL * P), :].rearrange("(b p) f -> p b f", p=P)
                             ).then_inc(s[f"x{q}"], 16)

            def store(n, q):
                sp.wait_ge(s["sum"], n + 3)
                sp.dma_start(out[bass.ds(n * BL * P, BL * P), :].rearrange("(b p) f -> p b f", p=P), x2[:, q]
                             ).then_inc(s[f"out{q}"], 16)

            group(0, 0, 0)
            group(1, 1, 0)
            with sp.Fori(1, NB // BL // 2) as i:
                for q in range(2):
                    store(2 * i + q - 2, q)
                    group(2 * i + q, q, i)
            for q in range(2):
                store(NB // BL - 2 + q, q)
            for q in range(2):
                sp.wait_ge(s[f"out{q}"], 16 * (NB // BL // 2))

        @block.gpsimd
        def _(pool):
            with pool.Fori(0, NB // BL // 2) as i:
                for q in range(2):
                    n = 2 * i + q
                    pool.wait_ge(s["sum"], n + 1)
                    nc.gpsimd.tensor_copy(idx[:, q], place[:, bass.ds(n * BL, BL), :]).then_inc(s["idx"], 1)
                    pool.wait_ge(s["idx"], n + 1)
                    for b in range(BL):
                        for j in range(2):
                            pool.nop(nofuse=True)
                            nc.gpsimd.indirect_dma_start(
                                out=r[q][:, b, j, :], out_offset=None, in_=made,
                                in_offset=bass.IndirectOffsetOnAxis(ap=idx[:, q, b, j:j + 1], axis=0)).then_inc(s[f"r{q}"], 16)

        @block.vector
        def _(vec):
            vec.sem_inc(s["sum"], 2)
            with vec.Fori(0, NB // BL // 2) as i:
                for q in range(2):
                    n = 2 * i + q
                    vec.wait_ge(s[f"x{q}"], 16 * i + 16)
                    vec.wait_ge(s[f"r{q}"], 160 * i + 160)
                    nc.vector.tensor_copy(w[:, q], weight[:, bass.ds(n * BL, BL), :])
                    vec.drain()
                    for j in range(2):
                        for b in range(BL):
                            op = nc.vector.scalar_tensor_tensor(x2[:, q, b, :], r[q][:, b, j, :], w[:, q, b, j:j + 1],
                                                                x2[:, q, b, :], ALU.mult, ALU.add)
                        if j == 0:
                            vec.drain()
                    op.then_inc(s["sum"], 1)


INS = ["x", "src_t", "dst_t", "dst_g", "first_row", "last_row", "edge_b", "W1", "as1", "ad1", "We1", "ae1", "b1", "W2", "as2",
       "ad2", "We2", "ae2", "b2", "Wqkv", "bqkv", "Wout", "bout", "rw1", "rb1", "rw2", "rb2", "ew1", "eb1", "ew2", "eb2",
       "ew3", "eb3"]


def kernel(x, src, dst, edge_attr_16, **w):
    import concourse.bacc as bacc
    from concourse.bass_utils import run_bass_kernel_spmd

    src_p = np.pad(np.asarray(src), (0, EP - E))
    dst_p = np.pad(np.asarray(dst), (0, EP - E), constant_values=N)
    edge_p = np.pad(np.asarray(edge_attr_16), ((0, EP - E), (0, 0)))
    arrays = {
        "x": np.pad(np.asarray(x), ((0, NP - N), (0, 0))),
        "src_t": src_p.reshape(T, P).T,
        "dst_t": dst_p.reshape(T, P).T,
        "dst_g": dst_p.reshape(NG, GT, P),
        "first_row": dst_p[None, ::P],
        "last_row": dst_p[None, P - 1::P],
        "edge_b": edge_p.reshape(T // H, H, P, D_EDGE).transpose(1, 3, 0, 2).reshape(P, T // H, P),
    }
    for l in "12":
        for to, of in (("W", "W"), ("as", "att_src"), ("ad", "att_dst"), ("We", "W_e"), ("ae", "att_e"), ("b", "b")):
            arrays[to + l] = w["L0_gnn_" + of + l]
    for to, of in (("Wqkv", "W_qkv"), ("bqkv", "b_qkv"), ("Wout", "W_out"), ("bout", "b_out")):
        arrays[to] = w["L0_mix_" + of]
    for to, of in (("r", "router"), ("e", "expert")):
        for part in ("w1", "b1", "w2", "b2") + (("w3", "b3") if to == "e" else ()):
            arrays[to + part] = w[f"L0_ffn_{of}_{part}"]
    nc = bacc.Bacc("TRN2", target_bir_lowering=False, num_devices=1)
    maps, args = {}, []
    for name in INS:
        a = np.ascontiguousarray(arrays[name])
        maps["in_" + name] = a
        args.append(nc.dram_tensor("in_" + name, a.shape, mybir.dt.from_np(a.dtype), kind="ExternalInput").ap())
    args.append(nc.dram_tensor("out_x", (NP, F), F32, kind="ExternalOutput").ap())
    build(nc, *args)
    r = run_bass_kernel_spmd(nc, [maps], core_ids=[0])
    return r.results[0]["out_x"][:N]
```
